# Optimizing a Trainium2 kernel written in Bass

```python
import numpy as np
import jax
import jax.numpy as jnp

def _softmax(x, axis=-1):
    return jax.nn.softmax(x, axis=axis)

def _gelu(x):
    return jax.nn.gelu(x, approximate=True)

def _silu(x):
    return jax.nn.silu(x)

def _sigmoid(x):
    return jax.nn.sigmoid(x)

def _layernorm(x, axis=-1, eps=1e-05):
    m = jnp.mean(x, axis=axis, keepdims=True)
    v = jnp.var(x, axis=axis, keepdims=True)
    return (x - m) / jnp.sqrt(v + eps)

def _scatter_add(tgt, idx, src, axis=0):
    return tgt.at[idx].add(src)

def _segment_sum(src, seg, n):
    return jax.ops.segment_sum(src, seg, n)
kernel_name = 'mk_gnn_resnorm_d4_gnn_r8_4827f5'

def setup_inputs(seed: int=0):
    np.random.seed(seed)
    _w = jnp.asarray

    def _rec_inputs():
        import jax
        import jax.numpy as jnp
        _gk = jax.random.key(seed)
        x = -0.0001126 + 1 * jax.random.normal(jax.random.fold_in(_gk, 1), (1250, 768), jnp.float32)
        src = jax.random.randint(jax.random.fold_in(_gk, 2), (20000,), 0, 1250, jnp.int32)
        dst = jax.random.randint(jax.random.fold_in(_gk, 3), (20000,), 0, 1250, jnp.int32)
        _o = jnp.argsort(dst, stable=True)
        src = src[_o]
        dst = dst[_o]
        edge_type_34 = jax.random.randint(jax.random.fold_in(_gk, 14), (20000,), 0, 34, jnp.int32)
        edge_weight1 = -0.00472126 + 0.997171 * jax.random.normal(jax.random.fold_in(_gk, 15), (20000, 1), jnp.float32)
        return (x, src, dst, edge_type_34, edge_weight1)
    x, src, dst, edge_type_34, edge_weight1 = _rec_inputs()

    def _L0_gnn_setup():
        import jax, jax.numpy as jnp
        import numpy as np
        N, E, D, H, C = (1250, 12500, 768, 4, 192)
        NEG_SLOPE = 0.2

        def gat_conv(x, src, dst, W, a_src, a_dst, b):
            h = (x @ W).reshape(N, H, C)
            as_n = (h * a_src).sum(-1)
            ad_n = (h * a_dst).sum(-1)
            e = jax.nn.leaky_relu(as_n[src] + ad_n[dst], NEG_SLOPE)
            m = jax.ops.segment_max(e, dst, num_segments=N)
            p = jnp.exp(e - m[dst])
            s = jax.ops.segment_sum(p, dst, num_segments=N)
            alpha = p / (s[dst] + 1e-16)
            out = jax.ops.segment_sum(alpha[:, :, None] * h[src], dst, num_segments=N)
            return out.reshape(N, H * C) + b
        key = jax.random.key(seed)
        ks = jax.random.split(key, 16)
        w = lambda k, shape: jax.random.normal(k, shape, dtype=jnp.float32) * 0.02
        inp = {}
        inp['x'] = jax.random.normal(ks[0], (N, D), dtype=jnp.float32)
        inp['edge_index'] = jax.random.randint(ks[1], (2, E), 0, N, dtype=jnp.int32)
        inp['batch'] = jnp.zeros((N,), dtype=jnp.int32)
        inp['edge_attr'] = jax.random.normal(ks[2], (E, 1), dtype=jnp.float32)
        inp['W_ah'] = w(ks[3], (D, D))
        inp['b_ah'] = jnp.zeros((D,), jnp.float32)
        for i in range(3):
            inp[f'W{i}'] = w(ks[4 + 3 * i], (D, H * C))
            inp[f'a_src{i}'] = w(ks[5 + 3 * i], (H, C))
            inp[f'a_dst{i}'] = w(ks[6 + 3 * i], (H, C))
            inp[f'b{i}'] = jnp.zeros((H * C,), jnp.float32)
        inp['W_out'] = w(ks[13], (3 * D, D))
        inp['b_out'] = jnp.zeros((D,), jnp.float32)
        return inp
    _L0_gnn_all = _L0_gnn_setup()
    _L0_gnn_in = {k: v for k, v in _L0_gnn_all.items() if k in ('W_ah', 'b_ah', 'W0', 'a_src0', 'a_dst0', 'b0', 'W1', 'a_src1', 'a_dst1', 'b1', 'W2', 'a_src2', 'a_dst2', 'b2', 'W_out', 'b_out')}
    del _L0_gnn_all

    def _L1_gnn_setup():
        import jax, jax.numpy as jnp
        import numpy as np
        N_NODES = 1250
        key = jax.random.key(seed)
        k1, k2, k3 = jax.random.split(key, 3)
        x = jax.random.normal(k1, (N_NODES, 768), dtype=jnp.float32)
        edge_index = jax.random.randint(k2, (2, 12500), 0, N_NODES, dtype=jnp.int32)
        W = jax.random.normal(k3, (768, 768), dtype=jnp.float32) * (1.0 / np.sqrt(768))
        b = jnp.zeros((768,), dtype=jnp.float32)
        return {'x': x, 'edge_index': edge_index, 'W': W, 'b': b}
    _L1_gnn_all = _L1_gnn_setup()
    _L1_gnn_in = {k: v for k, v in _L1_gnn_all.items() if k in ('W', 'b')}
    del _L1_gnn_all

    def _L2_gnn_setup():
        import jax, jax.numpy as jnp
        import numpy as np
        N = 2500
        DEG = 16
        E = N * DEG
        H = 12
        DIN = 64
        DOUT = 64
        NEG_SLOPE = 0.2
        key = jax.random.key(seed)
        k_h, k_src, k_w, k_al, k_ar, k_wr = jax.random.split(key, 6)
        std = 1.414 * np.sqrt(2.0 / (DIN + DOUT))
        h = jax.random.normal(k_h, (N, H * DIN), dtype=jnp.float32)
        src = jax.random.randint(k_src, (E,), 0, N, dtype=jnp.int64)
        dst = jnp.repeat(jnp.arange(N, dtype=jnp.int64), DEG)
        W = jax.random.normal(k_w, (DOUT, DIN), dtype=jnp.float32) * std
        attn_l = jax.random.normal(k_al, (1, H, DOUT), dtype=jnp.float32) * std
        attn_r = jax.random.normal(k_ar, (1, H, DOUT), dtype=jnp.float32) * std
        W_res = jax.random.normal(k_wr, (DOUT, DIN), dtype=jnp.float32) * std
        return {'h': h, 'src': src, 'dst': dst, 'W': W, 'attn_l': attn_l, 'attn_r': attn_r, 'W_res': W_res}
    _L2_gnn_all = _L2_gnn_setup()
    _L2_gnn_in = {k: v for k, v in _L2_gnn_all.items() if k in ('W', 'attn_l', 'attn_r', 'W_res')}
    del _L2_gnn_all

    def _L3_gnn_setup():
        import jax, jax.numpy as jnp
        import numpy as np
        N_NODES = 1250
        N_EDGES = 12500
        N_REL = 34
        DIM = 768

        def _graph_encoder(x, edge_index, edge_type, W_rel, W_root, b_rgcn, W_gcn, b_gcn):
            n = x.shape[0]
            src, dst = (edge_index[0], edge_index[1])
            ones = jnp.ones((src.shape[0],), dtype=x.dtype)
            seg = edge_type * n + dst
            agg = jax.ops.segment_sum(x[src], seg, num_segments=N_REL * n)
            cnt = jax.ops.segment_sum(ones, seg, num_segments=N_REL * n)
            mean = agg.reshape(N_REL, n, -1) / jnp.maximum(cnt, 1.0).reshape(N_REL, n, 1)
            h1 = jnp.einsum('rni,rio->no', mean, W_rel) + x @ W_root + b_rgcn
            xw = h1 @ W_gcn
            deg = jax.ops.segment_sum(ones, dst, num_segments=n) + 1.0
            dinv = jax.lax.rsqrt(deg)
            norm = dinv[src] * dinv[dst]
            out = jax.ops.segment_sum(xw[src] * norm[:, None], dst, num_segments=n)
            out = out + xw * (dinv * dinv)[:, None]
            return out + b_gcn
        key = jax.random.key(seed)
        ks = jax.random.split(key, 6)
        scale = 1.0 / np.sqrt(DIM)
        x = jax.random.normal(ks[0], (N_NODES, DIM), dtype=jnp.float32)
        edge_index = jax.random.randint(ks[1], (2, N_EDGES), 0, N_NODES, dtype=jnp.int32)
        edge_type = jax.random.randint(ks[2], (N_EDGES,), 0, N_REL, dtype=jnp.int32)
        W_rel = jax.random.normal(ks[3], (N_REL, DIM, DIM), dtype=jnp.float32) * scale
        W_root = jax.random.normal(ks[4], (DIM, DIM), dtype=jnp.float32) * scale
        b_rgcn = jnp.zeros((DIM,), dtype=jnp.float32)
        W_gcn = jax.random.normal(ks[5], (DIM, DIM), dtype=jnp.float32) * scale
        b_gcn = jnp.zeros((DIM,), dtype=jnp.float32)
        return {'x': x, 'edge_index': edge_index, 'edge_type': edge_type, 'W_rel': W_rel, 'W_root': W_root, 'b_rgcn': b_rgcn, 'W_gcn': W_gcn, 'b_gcn': b_gcn}
    _L3_gnn_all = _L3_gnn_setup()
    _L3_gnn_in = {k: v for k, v in _L3_gnn_all.items() if k in ('W_rel', 'W_root', 'b_rgcn', 'W_gcn', 'b_gcn')}
    del _L3_gnn_all
    return {'x': x, 'src': src, 'dst': dst, 'edge_type_34': edge_type_34, 'edge_weight1': edge_weight1, 'L0_gnn_W_ah': _L0_gnn_in['W_ah'], 'L0_gnn_b_ah': _L0_gnn_in['b_ah'], 'L0_gnn_W0': _L0_gnn_in['W0'], 'L0_gnn_a_src0': _L0_gnn_in['a_src0'], 'L0_gnn_a_dst0': _L0_gnn_in['a_dst0'], 'L0_gnn_b0': _L0_gnn_in['b0'], 'L0_gnn_W1': _L0_gnn_in['W1'], 'L0_gnn_a_src1': _L0_gnn_in['a_src1'], 'L0_gnn_a_dst1': _L0_gnn_in['a_dst1'], 'L0_gnn_b1': _L0_gnn_in['b1'], 'L0_gnn_W2': _L0_gnn_in['W2'], 'L0_gnn_a_src2': _L0_gnn_in['a_src2'], 'L0_gnn_a_dst2': _L0_gnn_in['a_dst2'], 'L0_gnn_b2': _L0_gnn_in['b2'], 'L0_gnn_W_out': _L0_gnn_in['W_out'], 'L0_gnn_b_out': _L0_gnn_in['b_out'], 'L1_gnn_W': _L1_gnn_in['W'], 'L1_gnn_b': _L1_gnn_in['b'], 'L2_gnn_W': _L2_gnn_in['W'], 'L2_gnn_attn_l': _L2_gnn_in['attn_l'], 'L2_gnn_attn_r': _L2_gnn_in['attn_r'], 'L2_gnn_W_res': _L2_gnn_in['W_res'], 'L3_gnn_W_rel': _L3_gnn_in['W_rel'], 'L3_gnn_W_root': _L3_gnn_in['W_root'], 'L3_gnn_b_rgcn': _L3_gnn_in['b_rgcn'], 'L3_gnn_W_gcn': _L3_gnn_in['W_gcn'], 'L3_gnn_b_gcn': _L3_gnn_in['b_gcn']}

def reference(x, src, dst, edge_type_34, edge_weight1, L0_gnn_W_ah, L0_gnn_b_ah, L0_gnn_W0, L0_gnn_a_src0, L0_gnn_a_dst0, L0_gnn_b0, L0_gnn_W1, L0_gnn_a_src1, L0_gnn_a_dst1, L0_gnn_b1, L0_gnn_W2, L0_gnn_a_src2, L0_gnn_a_dst2, L0_gnn_b2, L0_gnn_W_out, L0_gnn_b_out, L1_gnn_W, L1_gnn_b, L2_gnn_W, L2_gnn_attn_l, L2_gnn_attn_r, L2_gnn_W_res, L3_gnn_W_rel, L3_gnn_W_root, L3_gnn_b_rgcn, L3_gnn_W_gcn, L3_gnn_b_gcn):
    import jax
    import jax.numpy as jnp

    def _L0_gnn_ref(x, edge_index, batch, edge_attr, W_ah, b_ah, W0, a_src0, a_dst0, b0, W1, a_src1, a_dst1, b1, W2, a_src2, a_dst2, b2, W_out, b_out):
        import jax, jax.numpy as jnp
        import numpy as np
        N, E, D, H, C = (1250, 12500, 768, 4, 192)
        NEG_SLOPE = 0.2

        def gat_conv(x, src, dst, W, a_src, a_dst, b):
            h = (x @ W).reshape(N, H, C)
            as_n = (h * a_src).sum(-1)
            ad_n = (h * a_dst).sum(-1)
            e = jax.nn.leaky_relu(as_n[src] + ad_n[dst], NEG_SLOPE)
            m = jax.ops.segment_max(e, dst, num_segments=N)
            p = jnp.exp(e - m[dst])
            s = jax.ops.segment_sum(p, dst, num_segments=N)
            alpha = p / (s[dst] + 1e-16)
            out = jax.ops.segment_sum(alpha[:, :, None] * h[src], dst, num_segments=N)
            return out.reshape(N, H * C) + b
        loops = jnp.arange(N, dtype=edge_index.dtype)
        src = jnp.concatenate([edge_index[0], loops])
        dst = jnp.concatenate([edge_index[1], loops])
        x1 = jax.nn.relu(x @ W_ah + b_ah)
        xs = [jax.nn.relu(gat_conv(x1, src, dst, W, a_s, a_d, b)) for W, a_s, a_d, b in ((W0, a_src0, a_dst0, b0), (W1, a_src1, a_dst1, b1), (W2, a_src2, a_dst2, b2))]
        node_emb = jnp.concatenate(xs, axis=1)
        return jax.nn.relu(node_emb @ W_out + b_out)

    def _L1_gnn_ref(x, edge_index, W, b):
        import jax, jax.numpy as jnp
        import numpy as np
        N_NODES = 1250
        n = x.shape[0]
        loops = jnp.arange(n, dtype=edge_index.dtype)
        row = jnp.concatenate([edge_index[0], loops])
        col = jnp.concatenate([edge_index[1], loops])
        ones = jnp.ones(row.shape[0], dtype=x.dtype)
        deg = jax.ops.segment_sum(ones, col, num_segments=n)
        dinv = jnp.where(deg > 0, jax.lax.rsqrt(deg), 0.0)
        norm = dinv[row] * dinv[col]
        h = x @ W
        msg = h[row] * norm[:, None]
        out = jax.ops.segment_sum(msg, col, num_segments=n) + b
        return out

    def _L2_gnn_ref(h, src, dst, W, attn_l, attn_r, W_res):
        import jax, jax.numpy as jnp
        import numpy as np
        N = 2500
        DEG = 16
        E = N * DEG
        H = 12
        DIN = 64
        DOUT = 64
        NEG_SLOPE = 0.2
        n = h.shape[0]
        hv = h.reshape(n, H, DIN)
        ft = jnp.einsum('nhd,od->nho', hv, W)
        a1 = jnp.sum(ft * attn_l, axis=-1)
        a2 = jnp.sum(ft * attn_r, axis=-1)
        e = jax.nn.leaky_relu(a1[src] + a2[dst], negative_slope=NEG_SLOPE)
        m = jax.ops.segment_max(e, dst, num_segments=n)
        m = jnp.where(jnp.isfinite(m), m, 0.0)
        w = jnp.exp(e - m[dst])
        denom = jax.ops.segment_sum(w, dst, num_segments=n)
        alpha = w / jnp.maximum(denom[dst], 1e-16)
        msg = alpha[:, :, None] * ft[src]
        agg = jax.ops.segment_sum(msg, dst, num_segments=n)
        res = jnp.einsum('nhd,od->nho', hv, W_res)
        out = jax.nn.relu((agg + res).reshape(n, H * DOUT))
        return out

    def _L3_gnn_ref(x, edge_index, edge_type, W_rel, W_root, b_rgcn, W_gcn, b_gcn):
        import jax, jax.numpy as jnp
        import numpy as np
        N_NODES = 1250
        N_EDGES = 12500
        N_REL = 34
        DIM = 768

        def _graph_encoder(x, edge_index, edge_type, W_rel, W_root, b_rgcn, W_gcn, b_gcn):
            n = x.shape[0]
            src, dst = (edge_index[0], edge_index[1])
            ones = jnp.ones((src.shape[0],), dtype=x.dtype)
            seg = edge_type * n + dst
            agg = jax.ops.segment_sum(x[src], seg, num_segments=N_REL * n)
            cnt = jax.ops.segment_sum(ones, seg, num_segments=N_REL * n)
            mean = agg.reshape(N_REL, n, -1) / jnp.maximum(cnt, 1.0).reshape(N_REL, n, 1)
            h1 = jnp.einsum('rni,rio->no', mean, W_rel) + x @ W_root + b_rgcn
            xw = h1 @ W_gcn
            deg = jax.ops.segment_sum(ones, dst, num_segments=n) + 1.0
            dinv = jax.lax.rsqrt(deg)
            norm = dinv[src] * dinv[dst]
            out = jax.ops.segment_sum(xw[src] * norm[:, None], dst, num_segments=n)
            out = out + xw * (dinv * dinv)[:, None]
            return out + b_gcn
        return _graph_encoder(x, edge_index, edge_type, W_rel, W_root, b_rgcn, W_gcn, b_gcn)
    edge_index = jnp.stack([src, dst])
    batch0 = jnp.zeros((1250,), jnp.int32)
    x = _layernorm(x + _L0_gnn_ref(x, edge_index, batch0, edge_weight1, L0_gnn_W_ah, L0_gnn_b_ah, L0_gnn_W0, L0_gnn_a_src0, L0_gnn_a_dst0, L0_gnn_b0, L0_gnn_W1, L0_gnn_a_src1, L0_gnn_a_dst1, L0_gnn_b1, L0_gnn_W2, L0_gnn_a_src2, L0_gnn_a_dst2, L0_gnn_b2, L0_gnn_W_out, L0_gnn_b_out), axis=-1)
    x = _layernorm(x + _L1_gnn_ref(x, edge_index, L1_gnn_W, L1_gnn_b), axis=-1)
    x = _layernorm(x + _L2_gnn_ref(x, src, dst, L2_gnn_W, L2_gnn_attn_l, L2_gnn_attn_r, L2_gnn_W_res), axis=-1)
    x = _layernorm(x + _L3_gnn_ref(x, edge_index, edge_type_34, L3_gnn_W_rel, L3_gnn_W_root, L3_gnn_b_rgcn, L3_gnn_W_gcn, L3_gnn_b_gcn), axis=-1)
    return x

_drawn_inputs = setup_inputs


def setup_inputs(seed=0):
    import zlib

    import numpy as np

    out = dict(_drawn_inputs(seed))
    spreads = {'L0_gnn_b_ah': (0.0, 0.1),
     'L0_gnn_b0': (0.0, 0.1),
     'L0_gnn_b1': (0.0, 0.1),
     'L0_gnn_b2': (0.0, 0.1),
     'L0_gnn_b_out': (0.0, 0.1),
     'L1_gnn_b': (0.0, 0.1),
     'L3_gnn_b_rgcn': (0.0, 0.1),
     'L3_gnn_b_gcn': (0.0, 0.1)}
    factors = {'L0_gnn_a_src0': 64.0,
     'L0_gnn_a_dst0': 64.0,
     'L0_gnn_a_src1': 64.0,
     'L0_gnn_a_dst1': 64.0,
     'L0_gnn_a_src2': 64.0,
     'L0_gnn_a_dst2': 64.0}
    for name, (base, spread) in spreads.items():
        noise = np.random.default_rng([zlib.crc32(name.encode()), seed]).standard_normal(out[name].shape)
        drawn = base * np.exp(spread * noise) if base else spread * noise
        out[name] = jnp.asarray(drawn.astype(out[name].dtype))
    for name, factor in factors.items():
        out[name] = (out[name] * factor).astype(out[name].dtype)
    return out
```

```python
from contextlib import ExitStack, contextmanager

import concourse.bass as bass
from concourse import mybir

F32 = mybir.dt.float32
BF16 = mybir.dt.bfloat16
I32 = mybir.dt.int32
U16 = mybir.dt.uint16
ALU = mybir.AluOpType
ACT = mybir.ActivationFunctionType
AX = mybir.AxisListType.X

P = 128
N = 1250
NT = (N + P - 1) // P
NP = NT * P
D = 768
KC = D // P
HALF = D // 2
E = 20000
EP, ET = 125, 160
R = 34
RT = (E + R * (P - 1)) // P + 1
BT = -(-((E + NT * (P - 1)) // P) // 4) * 4
CW = NP + R
REC = 5
NONE = -1.0e30
SLOPE = 0.2
EPS_LN = 1e-5
TINY = 1e-16
WAYS = 8




class Steps:

    def __init__(self, eng, sem, carrier=None):
        self.eng, self.sem, self.base, self.k, self.carrier = eng, sem, 0, 0, carrier

    def __call__(self, ins):
        ins.then_inc(self.sem, 1)
        self.k += 1
        self.eng.wait_ge(self.sem, self.base + self.k)

    def count(self, ins):
        ins.then_inc(self.sem, 1)
        self.k += 1

    def wait(self):
        self.eng.wait_ge(self.sem, self.base + self.k)

    def carry(self):
        self.eng.sem_inc(self.carrier, 1)

    @contextmanager
    def loop(self, times, per):
        start = self.base + self.k
        with self.eng.Fori(0, times) as i:
            self.base, self.k = start + i * per, 0
            yield i
            assert self.k == per, (self.k, per)
        self.base, self.k = start + times * per, 0


def build(nc, a, out):
    ctx = ExitStack()
    with ctx:
        def sb(name, shape, dt=F32):
            return ctx.enter_context(nc.sbuf_tensor(name, shape, dt))

        def sem(name):

            return ctx.enter_context(nc.semaphore(name))

        def dram(name, shape, dt=F32):
            return nc.dram_tensor(name, shape, dt, kind="Internal").ap()

        x0_d = dram("x0_d", (NP, D))
        xa_d = dram("xa_d", (NP, D))
        h_d = [dram(f"feat{l}_d", (NP, D + 4)) for l in range(3)]
        gat_d = [dram(f"gat{l}_d", (NP, D)) for l in range(3)]
        x1_d = dram("x1_d", (NP, D))
        x2_d = dram("x2_d", (NP, D))
        res_d = dram("res_d", (NP, D))
        agg2_d = dram("agg2_d", (NP, D))
        x3_d = dram("x3_d", (NP, D))
        h1_d = dram("h1_d", (NP, D))
        x4_d = dram("x4_d", (NP, D))
        msg_d = dram("msg_d", (RT * P, D))
        relrec_d = dram("relrec_d", (P * RT, 1), I32)
        dstrec_d = dram("dstrec_d", (P * BT, REC))
        inv_d = dram("inv_d", (NP * R, 1))

        cnt = sb("cnt", [P, NT * NP], U16)
        mask1 = sb("mask1", [P, NT * NP], BF16)
        ct = sb("ct", [P, NT * CW], U16)
        hbuf = sb("hbuf", [P, NT * (D + 12)])
        work = sb("work", [P, 21248])
        ident = sb("ident", [P, P])
        ones = sb("ones", [P, P])
        tri = sb("tri", [P, P])
        iota = sb("iota", [P, NP], U16)
        relsrc = sb("relsrc", [P, RT + 2], I32)
        drec = sb("drec", [P, BT * REC])
        tile_rel = sb("tile_rel", [1, RT], I32)
        tile_dst = sb("tile_dst", [1, BT], I32)
        end_rel = sb("end_rel", [1, R + 2], I32)
        dinv = sb("dinv", [P, NT])
        small = sb("small", [P, 64])
        ps = ctx.enter_context(nc.psum_tensor("ps", [P, 8, 512], F32))
        psf = ps[:, :, :].rearrange("p b n -> p (b n)")

        cnt3 = cnt[:, :].rearrange("p (j n) -> p j n", j=NT)
        mask1v = mask1[:, :].rearrange("p (j n) -> p j n", j=NT)
        ct3 = ct[:, :].rearrange("p (j n) -> p j n", j=NT)
        mask2v = ct[:, :].bitcast(BF16).rearrange("p (j n) -> p j n", j=NT)
        drec3 = drec[:, :].rearrange("p (k c) -> p k c", c=REC)

        class Carve:

            def __init__(self, region, size):
                self.region, self.size, self.at = region, size, 0

            def __call__(self, n, dt=F32, parts=P):
                w = n if dt in (F32, I32) else (n + 1) // 2
                v = self.region[0:parts, self.at:self.at + w]
                self.at += w
                assert self.at <= self.size, self.at
                return v if dt is F32 else v.bitcast(dt)

        def halves(v):
            return v.rearrange("p (a n) -> p a n", a=2)

        met = sem("met")
        meetings = {}

        def meet(eng):
            meetings[eng] = meetings.get(eng, 0) + 1
            eng.drain().then_inc(met, 1)
            eng.wait_ge(met, 5 * meetings[eng])

        dve_step, act_step, pool_step = sem("dve_step"), sem("act_step"), sem("pool_step")
        dve_carrier, pool_carrier = sem("dve_carrier"), sem("pool_carrier")

        dense_sems = {n: sem("dense_" + n) for n in ("w_in0", "w_in1", "turned", "taken", "product", "emptied")}
        dense_sems["rows_in"] = [sem(f"dense_rows_in{u}") for u in range(2)]
        dense_counts = {n: 0 for n in [*dense_sems, "stages"]}

        class Dense:

            def __init__(self, name, rows, weights, w_at, rows_at, xt_at, bias=None, bias_at=None, beside=None):
                self.beside = beside
                self.rows, self.w, self.K = rows, weights, len(rows)
                self.w_at, self.rows_at, self.xt_at = w_at, rows_at, xt_at
                self.bias, self.bias_at = bias, bias_at
                self.pick = f"w_in{dense_counts['stages'] % 2}"
                dense_counts["stages"] += 1
                self.w_in, self.rows_in = dense_sems[self.pick], dense_sems["rows_in"]
                self.turned = dense_sems["turned"]
                self.taken = dense_sems["taken"]
                self.product = dense_sems["product"]
                self.emptied = dense_sems["emptied"]
                K, nw = self.K, 16 * (self.K + (bias is not None))
                self.b = dict(dense_counts)
                for key, more in ((self.pick, nw), ("rows_in", 16 * K * (NT // 2)), ("turned", K * (NT + 2)), ("taken", K * NT),
                                  ("product", NT + 2), ("emptied", NT + 2)):
                    dense_counts[key] += more
                self.all_turned = dense_counts["turned"]
                self.all_products = dense_counts["product"]

            def load(self, sp):
                for r in range(self.K):
                    sp.dma_start(self.w_at[:, r * KC:(r + 1) * KC, :],
                                 self.w[r].rearrange("(c p) n -> p c n", p=P)).then_inc(self.w_in, 16)
                if self.bias is not None:
                    sp.dma_start(self.bias_at, self.bias.rearrange("(a n) -> a n", a=1)).then_inc(self.w_in, 16)

            def stream(self, sp):
                with sp.Fori(0, NT // 2) as i:
                    for u in range(2):
                        j = 2 * i + u
                        sp.wait_ge(self.turned, self.b["turned"] + self.K * (j + 1))
                        for r in range(self.K):
                            sp.dma_start(self.rows_at[:, u, r, :], self.rows[r][bass.ds(j * P, P), :])\
                              .then_inc(self.rows_in[u], 16)
                        if self.beside is not None:
                            sp.wait_ge(self.emptied, self.b["emptied"] + j + 1)
                            sp.dma_start(self.beside[1][:, u, :], self.beside[0][bass.ds(j * P, P), :]).then_inc(self.beside[2][u], 16)

            def multiply(self, pe):
                K = self.K
                pe.wait_ge(self.turned, self.b["turned"] + 0)
                pe.wait_ge(self.product, self.b["product"])
                pe.sem_inc(self.turned, 2 * K)
                pe.sem_inc(self.product, 2)
                pe.wait_ge(self.w_in, self.b[self.pick] + 16 * (K + (self.bias is not None)))
                with pe.Fori(0, NT // 2) as i:
                    def turn(u, r):
                        q = K * u + r
                        if r == 0:
                            pe.wait_ge(self.rows_in[u], self.b["rows_in"] + 16 * K * (i + 1))
                        if K > 1 and q >= 2:
                            pe.wait_ge(self.taken, self.b["taken"] + 2 * K * i + q - 1)
                        for c in range(KC):
                            last = pe.transpose(ps[:, 2 * (q % 2) + c // 3, (c % 3) * P:(c % 3 + 1) * P],
                                                self.rows_at[:, u, r, c * P:(c + 1) * P], ident[:, :])
                        last.then_inc(self.turned, 1)

                    def times(u):
                        j = 2 * i + u
                        pe.wait_ge(self.taken, self.b["taken"] + K * (j + 1))
                        pe.wait_ge(self.emptied, self.b["emptied"] + j + 1)
                        for h in range(2):
                            o = ps[:, 4 + 2 * u + h, 0:HALF]
                            for c in range(K * KC):
                                last = pe.matmul(o, self.xt_at[:, u, c, :], self.w_at[:, c, h * HALF:(h + 1) * HALF],
                                                 start=(c == 0), stop=(c == K * KC - 1 and self.bias is None))
                            if self.bias is not None:
                                last = pe.matmul(o, ones[0:1, :], self.bias_at[:, h * HALF:(h + 1) * HALF],
                                                 start=False, stop=True)
                        last.then_inc(self.product, 1)

                    if K == 1:
                        turn(0, 0)
                        turn(1, 0)
                        times(0)
                        times(1)
                    else:
                        for u in range(2):
                            for r in range(K):
                                turn(u, r)
                            times(u)

            def take(self, act, i, u, col=None):
                K, j = self.K, 2 * i + u
                act.wait_ge(self.product, self.b["product"] + j + 1)
                for r in range(K):
                    q = K * u + r
                    act.wait_ge(self.turned, self.b["turned"] + 2 * K + 2 * K * i + q + 1)
                    if col is None:
                        ins = act.activation(self.xt_at[:, u, r * KC:(r + 1) * KC, :].rearrange("p (a b) n -> p a (b n)", a=2),
                                             ps[:, 2 * (q % 2):2 * (q % 2) + 2, 0:HALF], ACT.Copy)
                    else:
                        for c in range(KC):
                            ins = act.activation(self.xt_at[:, u, r * KC + c, :],
                                                 ps[:, 2 * (q % 2) + c // 3, (c % 3) * P:(c % 3 + 1) * P],
                                                 ACT.Relu, bias=col[:, r * KC + c:r * KC + c + 1])
                    ins.then_inc(self.taken, 1)

            def psum(self, u):
                return ps[:, 4 + 2 * u:6 + 2 * u, 0:HALF]

        norm_var, norm_root = sem("norm_var"), sem("norm_root")

        class Norm:

            used = 0

            def __init__(self):
                self.var, self.root = norm_var, norm_root
                self.b = NT * Norm.used
                Norm.used += 1

            def vector(self, v, step, z, j):
                st = small[:, 0:12].rearrange("p (a n) -> p a n", a=2)
                mv = small[:, 12:14]
                step.count(v.bn_stats(st[:, 0, :], z[:, 0:HALF]))
                step(v.bn_stats(st[:, 1, :], z[:, HALF:D]))
                step.carry()
                step(v.bn_aggr(mv, st))
                v.tensor_scalar(small[:, 14:15], mv[:, 1:2], EPS_LN, None, ALU.add).then_inc(self.var, 1)
                v.wait_ge(self.root, self.b + j + 1)
                step(v.reciprocal(small[:, 16:17], small[:, 15:16]))
                step(v.tensor_scalar(z, z, mv[:, 0:1], small[:, 16:17], ALU.subtract, ALU.mult))

            def scalar(self, act, j):
                act.wait_ge(self.var, self.b + j + 1)
                act.activation(small[:, 15:16], small[:, 14:15], ACT.Sqrt).then_inc(self.root, 1)
            VSTEPS = 5

        c1 = Carve(work, 21248)
        w_slots = [c1(KC * D).rearrange("p (c n) -> p c n", c=KC) for _ in range(2)]
        rows1 = c1(2 * D).rearrange("p (u r n) -> p u r n", u=2, r=1)
        xt1 = c1(2 * D).rearrange("p (u c n) -> p u c n", u=2, c=KC)
        brow1 = c1(D, parts=1)
        outs1 = c1(2 * (D + 4)).rearrange("p (u n) -> p u n", u=2)
        edges = c1(3 * ET, I32, EP).rearrange("p (a t) -> p a t", a=3)
        rec = c1(ET * REC, F32, EP).rearrange("p (t c) -> p t c", c=REC)
        addr = c1(2 * ET, I32, EP).rearrange("p (a t) -> p a t", a=2)
        ibuf = c1(2 * ET, I32, EP).rearrange("p (a t) -> p a t", a=2)
        fbuf = c1(2 * ET, F32, EP).rearrange("p (a t) -> p a t", a=2)
        islot = c1(3 * WAYS, I32, EP).rearrange("p (a w) -> p a w", a=3)
        rslot = c1(REC * WAYS, F32, EP).rearrange("p (w c) -> p w c", c=REC)
        onehot = cnt[0:EP, :].bitcast(F32)[:, 0:R * ET]
        scan = mask1[0:EP, :].bitcast(F32)[:, 0:R * ET]
        padrel = ct[:, 0:2 * RT].bitcast(I32)
        paddst = hbuf[:, 0:BT * REC].rearrange("p (k c) -> p k c", c=REC)
        zrows = hbuf[0:NP - N, 2000:2000 + D]
        s_x = sem("x_padded")
        s_edges = sem("edges_in")
        s_const = sem("constants")
        s_tables = sem("tables_cleared")
        s_pads = sem("pad_records")
        s_rowsum = sem("row_sums")
        s_offs = sem("offsets")
        s_offtaken = sem("offsets_taken")
        s_addr = sem("addresses")
        s_scat = [sem(f"scattered{w}") for w in range(WAYS)]
        s_x1 = [sem(f"x1_out{u}") for u in range(2)]
        s_h = [sem(f"h_out{u}") for u in range(2)]
        s_recs = sem("records_in")

        W_AH = Dense("ah", [x0_d], [a["L0_gnn_W_ah"]], w_slots[0], rows1, xt1, a["L0_gnn_b_ah"], brow1)
        W_H = [Dense(f"h{l}", [xa_d], [a[f"L0_gnn_W{l}"]], w_slots[(l + 1) % 2], rows1, xt1) for l in range(3)]
        PREFIX = [(0, R, RT), (1, NT, BT)]

        def sp_phase1(sp):
            sp.dma_start(edges[:, 0, :], a["src"].rearrange("(p t) -> p t", p=EP)).then_inc(s_edges, 16)
            sp.dma_start(edges[:, 1, :], a["dst"].rearrange("(p t) -> p t", p=EP)).then_inc(s_edges, 16)
            sp.dma_start(edges[:, 2, :], a["edge_type_34"].rearrange("(p t) -> p t", p=EP)).then_inc(s_edges, 16)
            sp.dma_start(x0_d[0:N, :], a["x"]).then_inc(s_x, 16)
            W_AH.load(sp)
            W_H[0].load(sp)
            sp.wait_ge(s_const, 1)
            sp.dma_start(x0_d[N:NP, :], zrows).then_inc(s_x, 16)
            sp.wait_ge(s_x, 32)
            W_AH.stream(sp)
            for u in range(2):
                sp.wait_ge(s_x1[u], 16 * NT // 2)
            for l in range(3):
                if l:
                    sp.wait_ge(W_AH.product, (W_AH if l == 1 else W_H[0]).all_products)
                    W_H[l].load(sp)
                sp.wait_ge(W_AH.turned, (W_AH if l == 0 else W_H[l - 1]).all_turned)
                W_H[l].stream(sp)

        def act_phase1(act, step):
            act.sem_inc(W_AH.emptied, 2)
            with step.loop(NT // 2, 2) as i:
                W_AH.take(act, i, 0)
                W_AH.take(act, i, 1)
                for u in range(2):
                    j = 2 * i + u
                    act.wait_ge(W_AH.product, W_AH.b["product"] + j + 3)
                    act.wait_ge(s_x1[u], 16 * i)
                    step(act.activation(halves(outs1[:, u, 0:D]), W_AH.psum(u), ACT.Relu))
                    act.sem_inc(W_AH.emptied, 1)
                    act.dma_start(xa_d[bass.ds(j * P, P), :], outs1[:, u, 0:D]).then_inc(s_x1[u], 16)
            for u in range(2):
                act.wait_ge(s_x1[u], 16 * NT // 2)
            hv = [outs1[:, u, :].rearrange("p (h c) -> p h c", h=4) for u in range(2)]
            act.wait_ge(s_const, 2)
            for u in range(2):
                step(act.activation(hv[u][:, :, 192], ones[:, 0:4], ACT.Copy))
            for l in range(3):
                act.sem_inc(W_H[l].emptied, 2)
                with step.loop(NT // 2, 4) as i:
                    W_H[l].take(act, i, 0)
                    W_H[l].take(act, i, 1)
                    for u in range(2):
                        j = 2 * i + u
                        act.wait_ge(W_H[l].product, W_H[l].b["product"] + j + 3)
                        act.wait_ge(s_h[u], 16 * i + 16 * l * (NT // 2))
                        for b in range(2):
                            step.count(act.activation(hv[u][:, 2 * b:2 * b + 2, 0:192],
                                                      ps[:, 4 + 2 * u + b, 0:HALF].rearrange("p (h c) -> p h c", h=2), ACT.Copy))
                        step.wait()
                        act.sem_inc(W_H[l].emptied, 1)
                        act.dma_start(h_d[l][bass.ds(j * P, P), :], outs1[:, u, :]).then_inc(s_h[u], 16)
            for u in range(2):
                act.wait_ge(s_h[u], 3 * 16 * NT // 2)

        def pe_phase1(pe):
            pe.wait_ge(s_const, 3)
            for g, nb, _ in PREFIX:
                pe.wait_ge(s_rowsum, g + 1)
                pe.matmul(ps[0:EP, 0, 0:nb], tri[0:EP, 0:EP], small[0:EP, 0:nb], start=True, stop=True)
                pe.matmul(ps[:, 1, 0:nb], ones[0:EP, :], small[0:EP, 0:nb], start=True, stop=True).then_inc(s_offs, 1)
                pe.wait_ge(s_offtaken, g + 1)
            for s in [W_AH] + W_H:
                s.multiply(pe)

        def dve_phase1(v, step):
            v.wait_ge(s_edges, 48)
            v.wait_ge(s_const, 3)
            src, dst, typ = (edges[:, k, :] for k in range(3))
            step(v.tensor_scalar(ibuf[:, 0, :], dst, 7, None, ALU.arith_shift_right))
            step(v.tensor_scalar(ibuf[:, 1, :], dst, P - 1, None, ALU.bitwise_and))
            step(v.tensor_copy(rec[:, :, 0], src))
            step(v.tensor_copy(rec[:, :, 1], ibuf[:, 1, :]))
            step(v.tensor_copy(rec[:, :, 2], typ))
            step(v.tensor_copy(fbuf[:, 0, :], dst))
            step(v.tensor_copy(fbuf[:, 1, :], ibuf[:, 0, :]))
            step(v.scalar_tensor_tensor(rec[:, :, 4], fbuf[:, 0, :], float(R), rec[:, :, 2], ALU.mult, ALU.add))
            for g, nb, nt in PREFIX:
                key = rec[:, :, 2] if g == 0 else fbuf[:, 1, :]
                for b in range(nb):
                    step.count(v.tensor_scalar(onehot[:, b * ET:(b + 1) * ET], key, float(b), None, ALU.is_equal))
                step.wait()
                oh, sc = onehot[:, 0:nb * ET], scan[:, 0:nb * ET]
                sc3 = sc.rearrange("p (b t) -> p b t", b=nb)
                step(v.tensor_tensor_scan(sc, oh, oh, 0.0, ALU.add, ALU.max))
                prev = small[0:EP, 40:41]
                last = sc3[:, :, ET - 1]
                tot, rowoff = small[:, 0:nb], fbuf[:, 0, 0:nb]
                step(v.tensor_copy(tot[0:EP, 0:1], last[:, 0:1]))
                v.tensor_tensor(tot[0:EP, 1:nb], last[:, 1:nb], last[:, 0:nb - 1], ALU.subtract).then_inc(s_rowsum, 1)
                v.wait_ge(s_offs, g + 1)
                ti = padt[:, 0:nb]
                step(v.tensor_scalar(ti, ps[:, 1, 0:nb], float(P - 1), None, ALU.add))
                step(v.tensor_scalar(ti, ti, 7, None, ALU.arith_shift_right))
                tf, ef = small[:, 0:nb], endf[:, 0:nb]
                step(v.tensor_copy(tf, ti))
                step(v.tensor_tensor_scan(ef, tf, tf, 0.0, ALU.add, ALU.max))
                step(v.tensor_tensor(tf, ef, tf, ALU.subtract))
                step(v.scalar_tensor_tensor(rowoff, tf[0:EP], float(P), ps[0:EP, 0, 0:nb], ALU.mult, ALU.add))
                step(v.tensor_scalar(rowoff, rowoff, -1.0, None, ALU.add))
                step(v.tensor_tensor(rowoff[:, 1:nb], rowoff[:, 1:nb], last[:, 0:nb - 1], ALU.subtract))
                v.sem_inc(s_offtaken, 1)
                for b in range(nb):
                    o = onehot[:, b * ET:(b + 1) * ET]
                    step.count(v.scalar_tensor_tensor(o, sc3[:, b, :], rowoff[:, b:b + 1], o, ALU.add, ALU.mult))
                step.wait()
                pos = rec[:, :, 3] if g == 0 else fbuf[:, 0, :]
                step(v.tensor_reduce(pos, oh.rearrange("p (b t) -> p t b", b=nb), AX, ALU.add))
                step(v.tensor_copy(ibuf[:, 0, :], pos))
                step(v.tensor_scalar(ibuf[:, 1, :], ibuf[:, 0, :], P - 1, None, ALU.bitwise_and))
                step(v.tensor_scalar(ibuf[:, 0, :], ibuf[:, 0, :], 7, None, ALU.arith_shift_right))
                step(v.scalar_tensor_tensor(addr[:, g, :], ibuf[:, 1, :], float(nt), ibuf[:, 0, :], ALU.mult, ALU.add))
                acc, owner = small[0:1, 0:1], tilef[:, 0:nt]
                step(v.memset(owner, 0.0))
                for b in range(nb):
                    step(v.scalar_tensor_tensor(owner, iota[0:1, 0:nt], endf[0:1, b:b + 1], owner, ALU.is_ge, ALU.add))
                step(v.tensor_scalar((tile_rel if g == 0 else tile_dst)[:, :], owner, float(nb - 1), None, ALU.min))
                if g == 0:
                    step(v.memset(end_rel[:, :], 0))
                    step(v.tensor_copy(end_rel[:, 2:R + 2], endf[0:1, 0:R]))
            v.sem_inc(s_addr, 1)

        padt = sb("padt", [P, R], I32)
        endf = sb("endf", [P, R])
        tilef = sb("tilef", [1, RT])

        def pool_phase1(g, step):
            step(g.memset(hbuf[0:32, 2000:2000 + D], 0.0))
            g.sem_inc(s_const, 1)
            step(g.memset(ones[:, :], 1.0))
            g.sem_inc(s_const, 1)
            step(g.memset(ident[:, :], 0.0))
            step(g.affine_select(out=ident[:, :], in_=ident[:, :], compare_op=ALU.not_equal, fill=1.0,
                                 base=0, pattern=[[-1, P]], channel_multiplier=1))
            step(g.affine_select(out=tri[:, :], in_=ones[:, :], compare_op=ALU.is_gt, fill=0.0,
                                 base=0, pattern=[[1, P]], channel_multiplier=-1))
            step(g.iota(iota[:, :], [[1, NP]], base=0, channel_multiplier=0))
            g.sem_inc(s_const, 1)
            step(g.memset(padrel, 0))
            step(g.memset(paddst, 0.0))
            step(g.memset(paddst[:, :, 0:2], -1.0))
            g.dma_start(relrec_d.rearrange("(p k) c -> p (k c)", p=P), padrel).then_inc(s_pads, 16)
            g.dma_start(dstrec_d.rearrange("(p k) c -> p (k c)", p=P), paddst.rearrange("p k c -> p (k c)")).then_inc(s_pads, 16)
            g.wait_ge(s_pads, 32)
            step(g.memset(ct[:, :], 0))
            g.wait_ge(s_addr, 1)
            with step.loop(ET // WAYS, 4 * WAYS) as i:
                for w in range(WAYS):
                    t = WAYS * i + w
                    g.wait_ge(s_scat[w], 32 * i)
                    step.count(g.tensor_copy(islot[:, 0, w:w + 1], addr[:, 0, bass.ds(t, 1)]))
                    step.count(g.tensor_copy(islot[:, 1, w:w + 1], addr[:, 1, bass.ds(t, 1)]))
                    step.count(g.tensor_copy(islot[:, 2, w:w + 1], edges[:, 0, bass.ds(t, 1)]))
                    step.count(g.tensor_copy(rslot[:, w, :], rec[:, bass.ds(t, 1), :].rearrange("p t c -> p (t c)")))
                    step.wait()
                    step.carry()
                    g.indirect_dma_start(out=relrec_d, out_offset=bass.IndirectOffsetOnAxis(islot[:, 0, w:w + 1], 0),
                                         in_=islot[:, 2, w:w + 1], in_offset=None).then_inc(s_scat[w], 16)
                    g.indirect_dma_start(out=dstrec_d, out_offset=bass.IndirectOffsetOnAxis(islot[:, 1, w:w + 1], 0),
                                         in_=rslot[:, w, :], in_offset=None).then_inc(s_scat[w], 16)
            for w in range(WAYS):
                g.wait_ge(s_scat[w], 32 * (ET // WAYS))
            step(g.memset(relsrc[:, RT:RT + 2], 0))
            g.dma_start(relsrc[:, 0:RT], relrec_d.rearrange("(p k) c -> p (k c)", p=P)).then_inc(s_recs, 16)
            g.dma_start(drec[:, :], dstrec_d.rearrange("(p k) c -> p (k c)", p=P)).then_inc(s_recs, 16)
            g.wait_ge(s_recs, 32)

        c2 = Carve(work, 21248)
        oh_t = c2(2 * P, BF16).rearrange("p (u n) -> p u n", u=2)
        oh_s = c2(2 * CW, BF16).rearrange("p (u n) -> p u n", u=2)
        s_oh = sem("onehots")
        s_ctp = sem("count_products")
        s_cta = sem("counts_added")

        def dve_phase2(v, step):
            v.sem_inc(s_cta, 2)

            def compare(k, u):
                v.wait_ge(s_ctp, k + 1)
                dr = drec3[:, bass.ds(k, 1), :].rearrange("p k c -> p (k c)")
                v.tensor_scalar(oh_t[:, u, :], iota[:, 0:P], dr[:, 1:2], None, ALU.is_equal)
                v.tensor_scalar(oh_s[:, u, 0:NP], iota[:, :], dr[:, 0:1], None, ALU.is_equal)
                v.tensor_scalar(oh_s[:, u, NP:CW], iota[:, 0:R], dr[:, 2:3], None, ALU.is_equal).then_inc(s_oh, 1)

            with step.loop(BT // 2, 2) as i:
                compare(2 * i, 0)
                compare(2 * i + 1, 1)
                for u in range(2):
                    k = 2 * i + u
                    b = v.value_load(tile_dst[0:1, bass.ds(k, 1)], min_val=0, max_val=NT - 1)
                    v.wait_ge(s_ctp, k + 3)
                    c = ct[:, bass.ds(b * CW, CW)]
                    step(v.tensor_tensor(c, psf[:, u * 2048:u * 2048 + CW], c, ALU.add))
                    v.sem_inc(s_cta, 1)

        def pe_phase2(pe):
            pe.sem_inc(s_ctp, 2)
            with pe.Fori(0, BT // 2) as i:
                for u in range(2):
                    k = 2 * i + u
                    pe.wait_ge(s_oh, k + 1)
                    pe.wait_ge(s_cta, k + 1)
                    for n0 in range(0, CW, 512):
                        n1 = min(n0 + 512, CW)
                        last = pe.matmul(psf[:, u * 2048 + n0:u * 2048 + n1], oh_t[:, u, :], oh_s[:, u, n0:n1],
                                         start=True, stop=True)
                    last.then_inc(s_ctp, 1)

        c3 = Carve(work, 21248)
        crow = c3(2 * NP).rearrange("p (u n) -> p u n", u=2)
        deg = c3(NT)
        inv = c3(NT * R).rearrange("p (j r) -> p j r", j=NT)
        s_crow = sem("count_rows")
        s_cturn = sem("counts_turned")
        s_inv = sem("inverse_counts")
        s_invd = sem("inverse_counts_stored")
        s_deg = sem("degrees")
        s_root = sem("degree_roots")

        def dve_phase3(v, step):
            step(v.tensor_scalar(inv, ct3[:, :, NP:CW], 1.0, None, ALU.max))
            step(v.reciprocal(inv, inv))
            v.sem_inc(s_inv, 1)
            with step.loop(NT // 2, 12) as i:
                for u in range(2):
                    j = 2 * i + u
                    v.wait_ge(s_cturn, j + 1)
                    row, c = crow[:, u, :], ct[:, bass.ds(j * CW, NP)]
                    step(v.tensor_copy(row, c))
                    dg = crow[:, u, bass.ds(j * P, P)]
                    step(v.tensor_tensor(dg, dg, ident[:, :], ALU.add))
                    v.sem_inc(s_crow, 1)
                    step(v.tensor_scalar(mask1[:, bass.ds(j * NP, NP)], row, 0.0, NONE, ALU.is_equal, ALU.mult))
                    step(v.tensor_scalar(ct[:, bass.ds(j * CW, NP)].bitcast(BF16), c, 0.0, NONE, ALU.is_equal, ALU.mult))
                    step(v.tensor_reduce(deg[:, bass.ds(j, 1)], row, AX, ALU.add))
                    v.wait_ge(s_cturn, j + 3)
                    step(v.tensor_copy(cnt3[:, :, bass.ds(j * P, P)], psf[:, u * 2048:u * 2048 + NP].rearrange("p (s n) -> p s n", n=P)))
            v.sem_inc(s_deg, 1)
            v.wait_ge(s_root, 1)
            step(v.reciprocal(dinv[:, :], dinv[:, :]))

        def pe_phase3(pe):
            pe.sem_inc(s_cturn, 2)
            with pe.Fori(0, NT // 2) as i:
                for u in range(2):
                    j = 2 * i + u
                    pe.wait_ge(s_crow, j + 1)
                    for s in range(NT):
                        last = pe.transpose(psf[:, u * 2048 + s * P:u * 2048 + (s + 1) * P], crow[:, u, s * P:(s + 1) * P], ident[:, :])
                    last.then_inc(s_cturn, 1)

        class Attention:
            def __init__(self, name, HN, mask, layers):
                self.HN, self.C, self.mask, self.layers = HN, D // HN, mask, layers
                self.banks = 5 if HN == 4 else 2
                self.tpb = NT // self.banks
                cv = Carve(work, 21248)
                self.cv = cv
                self.arow = cv(2 * D).rearrange("p (a n) -> p a n", a=2)
                self.prod = cv(2 * D).rearrange("p (a n) -> p a n", a=2)
                heads = [cv((HN + 1) * NT).rearrange("p (h j) -> p h j", h=HN + 1) for _ in range(7)]
                self.after = [heads[k][:, HN, :] for k in (3, 4)]
                self.L, self.Rr, self.M, self.R1, self.R2, self.L2, self.y = heads
                self.full = heads
                self.mh = cv(NT)
                self.diag = [cv(NP) for _ in range(2)]
                self.R1b = [cv(NP) for _ in range(2)]
                self.R2b = [cv(NP) for _ in range(2)]
                self.t2 = [cv(NP) for _ in range(2)]
                self.t = [cv(NP) for _ in range(2)]
                self.p = [cv(NP) for _ in range(2)]
                self.junk = self.p[0]
                self.o = cv(NT * self.C)
                self.den = cv(NT)
                (self.s_in_, self.s_diagA, self.s_bcA, self.s_maxed, self.s_hr, self.s_diagC, self.s_bcC, self.s_rb, self.s_t2r,
                 self.s_tr, self.s_er, self.s_pr, self.s_agg, self.s_out, self.s_stored, self.s_aggfree) = (
                    sem(f"{name}_{s}") for s in ("inputs_in", "max_spread", "max_rows", "maxed", "heads_ready", "spread", "rows",
                                                 "rows_taken", "second_ready", "exponent_ready", "exp_ready", "weights_ready",
                                                 "summed", "head_ready", "head_stored", "sums_free"))
                self.H = hbuf[:, 0:NT * (D + HN)].rearrange("p (j h c) -> p j h c", j=NT, h=HN)

            def sp(self, sp, n):
                al, ar, o_dram, load_from = self.layers[n]
                sp.dma_start(self.arow[:, 0, :], al.partition_broadcast(P)).then_inc(self.s_in_, 16)
                sp.dma_start(self.arow[:, 1, :], ar.partition_broadcast(P)).then_inc(self.s_in_, 16)
                if load_from is not None:
                    sp.dma_start(hbuf[:, 0:NT * (D + self.HN)].rearrange("p (j n) -> p j n", j=NT),
                                 load_from.rearrange("(j p) n -> p j n", p=P)).then_inc(self.s_in_, 16)
                od = o_dram.rearrange("(j p) n -> p j n", p=P)
                with sp.Fori(0, self.HN) as h:
                    sp.wait_ge(self.s_out, self.HN * n + h + 1)
                    sp.dma_start(od[:, :, bass.ds(h * self.C, self.C)], self.o.rearrange("p (j c) -> p j c", j=NT))\
                      .then_inc(self.s_stored, 16)
                sp.wait_ge(self.s_stored, 16 * self.HN * (n + 1))

            def spread(self, v, out, vec):
                return v.tensor_tensor(out.rearrange("p (j n) -> p j n", j=NT),
                                       ident[:, :].unsqueeze(1).to_broadcast([P, NT, P]),
                                       vec.unsqueeze(2).to_broadcast([P, NT, P]), ALU.mult)

            def dve(self, v, step, n):
                HN, C = self.HN, self.C
                H0 = HN * n
                if n == 0:
                    v.sem_inc(self.s_tr, 2)
                    v.sem_inc(self.s_pr, 2)
                v.wait_ge(self.s_in_, 16 * (3 if self.layers[n][3] is not None else 2) * (n + 1))
                with step.loop(NT, 4) as j:
                    hj = hbuf[:, bass.ds(j * (D + HN), D + HN)].rearrange("p (h c) -> p h c", h=HN)[:, :, 0:C]
                    for k, dest in ((0, self.L), (1, self.Rr)):
                        pr = self.prod[:, k, :].rearrange("p (h c) -> p h c", h=HN)
                        step(v.tensor_tensor(pr, hj, self.arow[:, k, :].rearrange("p (h c) -> p h c", h=HN), ALU.mult))
                        step(v.tensor_reduce(dest[:, 0:HN, bass.ds(j, 1)].rearrange("p h j -> p (h j)"), pr, AX, ALU.add))
                with step.loop(HN, NT + 1) as h:
                    self.spread(v, self.diag[0], self.L[:, bass.ds(h, 1), :].rearrange("p h j -> p (h j)")).then_inc(self.s_diagA, 1)
                    v.wait_ge(self.s_bcA, H0 + h + 1)
                    step.carry()
                    for j in range(NT):
                        step(v.tensor_tensor_reduce(self.junk, self.mask[:, j, 0:NP], psf[:, 0:NP], 1.0, NONE, ALU.add,
                                                    ALU.max, self.mh[:, j:j + 1]))
                        step.carry()
                    v.sem_inc(self.s_maxed, 1)
                    step(v.tensor_copy(self.M[:, bass.ds(h, 1), :].rearrange("p h j -> p (h j)"), self.mh))
                L, Rr, M, R1, R2, L2, y = (t[:, 0:HN, :] for t in self.full)
                step(v.tensor_scalar(y, M, 0.1 * NONE, -NONE, ALU.is_lt, ALU.mult))
                step(v.tensor_tensor(M, M, y, ALU.add))
                step(v.tensor_tensor(y, M, Rr, ALU.add))
                step(v.scalar_tensor_tensor(M, y, SLOPE, y, ALU.mult, ALU.max))
                step.count(v.tensor_tensor(R1, Rr, M, ALU.subtract))
                step.count(v.scalar_tensor_tensor(R2, Rr, SLOPE, M, ALU.mult, ALU.subtract))
                for t in self.after:
                    step.count(v.memset(t, 0.0))
                step(v.tensor_scalar(L2, L, SLOPE, None, ALU.mult))
                v.sem_inc(self.s_hr, 1)

                def spreads(h, k):
                    src = (self.R1, self.R2)[k][:, bass.ds(h, 1), :].rearrange("p h j -> p (h j)")
                    self.spread(v, self.diag[k], src).then_inc(self.s_diagC, 1)

                v.sem_inc(self.s_aggfree, 1)
                spreads(0, 0)
                spreads(0, 1)
                with step.loop(HN // 2, 2 * 3) as i:
                    def T(g):
                        hh, s = divmod(g, NT)
                        h = 2 * i + hh
                        if s == 0:
                            v.wait_ge(self.s_rb, 2 * (H0 + n + h + 1))
                        v.wait_ge(self.s_pr, NT * H0 + 2 * NT * i + g + 1)
                        v.wait_ge(self.s_t2r, NT * H0 + 2 * NT * i + g + 1)
                        l = self.L[:, bass.ds(h, 1), s:s + 1].rearrange("p h s -> p (h s)")
                        v.scalar_tensor_tensor(self.t[g % 2], self.R1b[hh], l, self.t2[g % 2], ALU.add, ALU.max)\
                         .then_inc(self.s_tr, 1)

                    def PP(g):
                        v.wait_ge(self.s_er, NT * H0 + 2 * NT * i + g + 1)
                        v.wait_ge(self.s_agg, NT * H0 + 2 * NT * i + g + 1)
                        v.scalar_tensor_tensor(self.p[g % 2], self.t[g % 2], 1.0, cnt3[:, g % NT, :], ALU.min, ALU.mult)\
                         .then_inc(self.s_pr, 1)

                    def evict(hh):
                        h = 2 * i + hh
                        v.wait_ge(self.s_agg, 2 + NT * (H0 + h + 1))
                        v.wait_ge(self.s_stored, 16 * (H0 + h))
                        acc = ps[:, 3:3 + self.banks, 0:self.tpb * (C + 1)].rearrange("p b (t c) -> p b t c", c=C + 1)
                        den = self.den.rearrange("p (b t) -> p b t", b=self.banks)
                        step(v.tensor_scalar(den, acc[:, :, :, C], TINY, None, ALU.add if HN == 4 else ALU.max))
                        step(v.reciprocal(self.den, self.den))
                        step(v.tensor_tensor(self.o.rearrange("p (b t c) -> p b t c", b=self.banks, c=C), acc[:, :, :, 0:C],
                                             den.unsqueeze(3).to_broadcast([P, self.banks, self.tpb, C]), ALU.mult))
                        v.sem_inc(self.s_out, 1)
                        v.sem_inc(self.s_aggfree, 1)

                    for g in range(2 * NT):
                        T(g)
                        if g:
                            PP(g - 1)
                        if g == NT:
                            evict(0)
                        if g % NT == 3:
                            h1 = 2 * i + 1 if g < NT else 2 * i + 2
                            spreads(h1, 0)
                            spreads(h1, 1)
                    PP(2 * NT - 1)
                    evict(1)

            def pe(self, pe, n):
                HN, C = self.HN, self.C
                H0 = HN * n
                if n == 0:
                    pe.sem_inc(self.s_agg, 2)

                def repeat_rows(k):
                    for n0 in range(0, NP, 512):
                        n1 = min(NP, n0 + 512)
                        last = pe.matmul(psf[:, n0:n1], ones[:, :], self.diag[k][:, n0:n1], start=True, stop=True)
                    return last

                with pe.Fori(0, HN) as h:
                    pe.wait_ge(self.s_diagA, H0 + h + 1)
                    repeat_rows(0).then_inc(self.s_bcA, 1)
                pe.wait_ge(self.s_maxed, H0 + HN)
                for k in range(2):
                    pe.wait_ge(self.s_diagC, 2 * (H0 + n) + k + 1)
                    if k:
                        pe.wait_ge(self.s_rb, 2 * (H0 + n) + 1)
                    repeat_rows(k).then_inc(self.s_bcC, 1)
                with pe.Fori(0, HN // 2) as i:
                    for g in range(2 * NT):
                        hh, s = divmod(g, NT)
                        h = 2 * i + hh
                        pe.wait_ge(self.s_pr, 2 + NT * H0 + 2 * NT * i + g + 1)
                        if s == 0:
                            pe.wait_ge(self.s_aggfree, H0 + n + h + 1)
                        hs = hbuf[:, bass.ds(h * (C + 1) + s * (D + HN), C + 1)]
                        for dt in range(NT):
                            b, t = divmod(dt, self.tpb)
                            last = pe.matmul(ps[:, 3 + b, t * (C + 1):(t + 1) * (C + 1)], self.p[g % 2][:, dt * P:(dt + 1) * P],
                                             hs, start=(s == 0 and t == 0), stop=(s == NT - 1), skip_group_check=True)
                        last.then_inc(self.s_agg, 1)
                        if s in (5, 7):
                            k = (s - 5) // 2
                            pe.wait_ge(self.s_diagC, 2 * (H0 + n + h + 1) + k + 1)
                            pe.wait_ge(self.s_rb, 2 * (H0 + n + h + 1) + k)
                            repeat_rows(k).then_inc(self.s_bcC, 1)

            def act(self, act, step, n):
                H0 = self.HN * n

                def rows_out(hh, k, head):
                    act.wait_ge(self.s_bcC, 2 * (H0 + n + head) + k + 1)
                    act.activation((self.R1b, self.R2b)[k][hh], psf[:, 0:NP], ACT.Copy).then_inc(self.s_rb, 1)

                act.wait_ge(self.s_hr, n + 1)
                rows_out(0, 0, 0)
                rows_out(0, 1, 0)
                with act.Fori(0, self.HN // 2) as i:
                    def T2(g):
                        hh, s = divmod(g, NT)
                        h = 2 * i + hh
                        if s == 0:
                            act.wait_ge(self.s_rb, 2 * (H0 + n + h + 1))
                        act.wait_ge(self.s_tr, NT * H0 + 2 * NT * i + g + 1)
                        b = self.L2[:, bass.ds(h, 1), s:s + 1].rearrange("p h s -> p (h s)")
                        act.activation(self.t2[g % 2], self.R2b[hh], ACT.Identity, bias=b).then_inc(self.s_t2r, 1)

                    def EX(g):
                        act.wait_ge(self.s_tr, 2 + NT * H0 + 2 * NT * i + g + 1)
                        act.activation(self.t[g % 2], self.t[g % 2], ACT.Exp).then_inc(self.s_er, 1)

                    for g in range(2 * NT):
                        T2(g)
                        if g:
                            EX(g - 1)
                        hh, s = divmod(g, NT)
                        if s in (7, 9):
                            k = (s - 7) // 2
                            rows_out(1 - hh, k, 2 * i + hh + 1)
                    EX(2 * NT - 1)

        att0 = Attention("gat", 4, mask1v, [(a[f"L0_gnn_a_src{l}"].rearrange("h c -> (h c)"), a[f"L0_gnn_a_dst{l}"].rearrange("h c -> (h c)"),
                                             gat_d[l], h_d[l]) for l in range(3)])

        def store_tiles(g, step, ready, slots, dst, stored, before=0):
            with g.Fori(0, NT // 2) as i:
                for u in range(2):
                    j = 2 * i + u
                    g.wait_ge(ready, before + j + 1)
                    step.carry()
                    g.dma_start(dst[bass.ds(j * P, P), :], slots[:, u, :]).then_inc(stored[u], 16)
            for u in range(2):
                g.wait_ge(stored[u], 8 * before + 16 * (NT // 2))

        def two(name):
            return [sem(f"{name}{u}") for u in range(2)]

        c4 = Carve(work, 21248)
        h4 = Carve(hbuf, NT * (D + 12))
        colb = h4(3 * KC)
        z4 = h4(2 * D).rearrange("p (u n) -> p u n", u=2)
        x4s = c4(2 * D).rearrange("p (u n) -> p u n", u=2)
        s_x4s, s_z4st = two("wout_x_in"), two("x1_stored")
        s_z4, s_colb = sem("x1_ready"), sem("gat_bias_in")
        w4 = c4(3 * KC * D).rearrange("p (c n) -> p c n", c=3 * KC)
        r4 = c4(6 * D).rearrange("p (u r n) -> p u r n", u=2, r=3)
        xt4 = h4(6 * D).rearrange("p (u c n) -> p u c n", u=2, c=3 * KC)
        W_OUT = Dense("wout", gat_d, [a["L0_gnn_W_out"][l * D:(l + 1) * D, :] for l in range(3)], w4, r4, xt4,
                      a["L0_gnn_b_out"], h4(D, parts=1), beside=(x0_d, x4s, s_x4s))
        norm1 = Norm()

        def sp_wout(sp):
            for l in range(3):
                sp.dma_start(colb[:, l * KC:(l + 1) * KC], a[f"L0_gnn_b{l}"].rearrange("(c p) -> p c", p=P),
                             allow_slow_non_contiguous=True).then_inc(s_colb, 16)
            W_OUT.load(sp)
            W_OUT.stream(sp)

        def act_wout(act):
            act.wait_ge(s_colb, 48)
            with act.Fori(0, NT // 2) as i:
                for u in range(2):
                    W_OUT.take(act, i, u, colb)
                for u in range(2):
                    norm1.scalar(act, 2 * i + u)

        def dve_wout(v, step):
            v.sem_inc(W_OUT.emptied, 2)
            with step.loop(NT // 2, 2 * (1 + Norm.VSTEPS)) as i:
                for u in range(2):
                    j = 2 * i + u
                    z = z4[:, u, :]
                    v.wait_ge(W_OUT.product, W_OUT.b["product"] + j + 3)
                    v.wait_ge(s_x4s[u], 16 * (i + 1))
                    v.wait_ge(s_z4st[u], 16 * i)
                    step(v.scalar_tensor_tensor(halves(z), W_OUT.psum(u), 0.0, halves(x4s[:, u, :]), ALU.max, ALU.add))
                    v.sem_inc(W_OUT.emptied, 1)
                    norm1.vector(v, step, z, j)
                    v.sem_inc(s_z4, 1)

        conv_sems = {n: sem("conv_" + n) for n in ("b_in", "g", "cols", "agg", "emptied", "ready")}
        conv_sems.update(x_in=two("conv_x_in"), stored=two("conv_stored"))

        class Convolution:
            def __init__(self, turn, rows, weight, bias, x_dram, out_dram):
                self.bias, self.out_dram, self.n = bias, out_dram, turn
                cv = Carve(work, 21248)
                self.dense = Dense("conv", [rows], [weight], cv(KC * D).rearrange("p (c n) -> p c n", c=KC),
                                   cv(2 * D).rearrange("p (u r n) -> p u r n", u=2, r=1),
                                   cv(2 * D).rearrange("p (u c n) -> p u c n", u=2, c=KC))
                self.col = [cv(NP).rearrange("p (s n) -> p s n", s=NT) for _ in range(2)]
                self.brow = cv(D)
                self.xs = cv(2 * D).rearrange("p (u n) -> p u n", u=2)
                self.z = cv(2 * D).rearrange("p (u n) -> p u n", u=2)
                self.x_dram = x_dram
                self.x_in, self.stored = conv_sems["x_in"], conv_sems["stored"]
                self.s_b_in, self.s_g, self.s_cols, self.s_ready = (conv_sems[n] for n in ("b_in", "g", "cols", "ready"))
                self.s_agg, self.s_emptied = conv_sems["agg"], conv_sems["emptied"]
                self.at = turn * NT
                self.at2 = turn * (NT + 2)
                self.norm = Norm()
                self.gv = hbuf[:, 0:NT * D].rearrange("p (j n) -> p j n", j=NT)

            def sp(self, sp):
                self.dense.load(sp)
                self.dense.stream(sp)
                sp.dma_start(self.brow, self.bias.partition_broadcast(P)).then_inc(self.s_b_in, 16)
                with sp.Fori(0, NT // 2) as i:
                    for u in range(2):
                        j = 2 * i + u
                        sp.wait_ge(self.s_emptied, self.at2 + j + 1)
                        sp.dma_start(self.xs[:, u, :], self.x_dram[bass.ds(j * P, P), :]).then_inc(self.x_in[u], 16)

            def act(self, act, step):
                d = self.dense
                with step.loop(NT // 2, 2) as i:
                    d.take(act, i, 0)
                    d.take(act, i, 1)
                    for u in range(2):
                        j = 2 * i + u
                        act.wait_ge(d.product, d.b["product"] + j + 3)
                        step(act.activation(halves(hbuf[:, bass.ds(j * D, D)]), d.psum(u), ACT.Copy, scale=dinv[:, bass.ds(j, 1)]))
                        act.sem_inc(d.emptied, 1)
                act.sem_inc(self.s_g, 1)
                with act.Fori(0, NT // 2) as i:
                    for u in range(2):
                        j = 2 * i + u
                        act.wait_ge(self.s_agg, self.at2 + j + 1)
                        act.activation(self.col[u], cnt3[:, :, bass.ds(j * P, P)], ACT.Copy).then_inc(self.s_cols, 1)
                    for u in range(2):
                        self.norm.scalar(act, 2 * i + u)

            def pe(self, pe):
                self.dense.multiply(pe)
                pe.sem_inc(self.s_agg, 2)
                pe.wait_ge(self.s_g, self.n + 1)
                with pe.Fori(0, NT // 2) as i:
                    for u in range(2):
                        j = 2 * i + u
                        pe.wait_ge(self.s_cols, self.at + j + 1)
                        pe.wait_ge(self.s_emptied, self.at2 + j + 1)
                        for h in range(2):
                            for s in range(NT):
                                last = pe.matmul(ps[:, 2 * u + h, 0:HALF], self.col[u][:, s, :],
                                                 self.gv[:, s, h * HALF:(h + 1) * HALF], start=(s == 0), stop=(s == NT - 1))
                        last.then_inc(self.s_agg, 1)

            def dve(self, v, step):
                v.sem_inc(self.dense.emptied, 2)
                v.sem_inc(self.s_emptied, 2)
                v.wait_ge(self.s_b_in, 16 * (self.n + 1))
                with step.loop(NT // 2, 2 * (2 + Norm.VSTEPS)) as i:
                    for u in range(2):
                        j = 2 * i + u
                        z = self.z[:, u, :]
                        v.wait_ge(self.s_agg, self.at2 + j + 3)
                        v.wait_ge(self.stored[u], 8 * self.at + 16 * i)
                        step(v.scalar_tensor_tensor(halves(z), ps[:, 2 * u:2 * u + 2, 0:HALF], dinv[:, bass.ds(j, 1)],
                                                    halves(self.brow), ALU.mult, ALU.add))
                        v.wait_ge(self.x_in[u], 8 * self.at + 16 * (i + 1))
                        step(v.tensor_tensor(z, z, self.xs[:, u, :], ALU.add))
                        v.sem_inc(self.s_emptied, 1)
                        self.norm.vector(v, step, z, j)
                        v.sem_inc(self.s_ready, 1)

            def pool(self, g, step):
                store_tiles(g, step, self.s_ready, self.z, self.out_dram, self.stored, self.at)

        conv1 = Convolution(0, x1_d, a["L1_gnn_W"], a["L1_gnn_b"], x1_d, x2_d)

        c5 = Carve(work, 21248)
        wbd = c5(2 * P)
        rows5 = c5(2 * D).rearrange("p (u n) -> p u n", u=2)
        xt5 = c5(2 * D).rearrange("p (u c n) -> p u c n", u=2, c=KC)
        res5 = c5(2 * D).rearrange("p (u n) -> p u n", u=2)
        s_w5, s_w5z, s_ones5 = sem("wbd_in"), sem("wbd_zero"), sem("ones5")
        s_rows5, s_res5 = two("rows5_in"), two("res_stored")
        s_turn5, s_take5, s_prod5, s_free5 = sem("turned5"), sem("taken5"), sem("product5"), sem("free5")
        ft = hbuf[:, 0:NT * (D + 12)].rearrange("p (j n) -> p j n", j=NT)

        def pool_heads(g, step):
            step(g.memset(wbd, 0.0))
            g.sem_inc(s_w5z, 1)
            step(g.memset(hbuf[:, 0:NT * (D + 12)], 1.0))
            g.sem_inc(s_ones5, 1)

        def sp_heads(sp):
            sp.wait_ge(s_w5z, 1)
            for q in range(2):
                for k, w in ((0, a["L2_gnn_W"]), (1, a["L2_gnn_W_res"])):
                    sp.dma_start(wbd[64 * q:64 * q + 64, k * P + 64 * q:k * P + 64 * q + 64], w).then_inc(s_w5, 16)
            with sp.Fori(0, NT // 2) as i:
                for u in range(2):
                    j = 2 * i + u
                    sp.wait_ge(s_turn5, j + 1)
                    sp.dma_start(rows5[:, u, :], x2_d[bass.ds(j * P, P), :]).then_inc(s_rows5[u], 16)

        def pe_heads(pe):
            pe.sem_inc(s_turn5, 2)
            pe.sem_inc(s_prod5, 2)
            pe.sem_inc(s_free5, 2)
            pe.wait_ge(s_w5, 64)
            with pe.Fori(0, NT // 2) as i:
                for u in range(2):
                    pe.wait_ge(s_rows5[u], 16 * (i + 1))
                    for c in range(KC):
                        last = pe.transpose(ps[:, 2 * u + c // 3, (c % 3) * P:(c % 3 + 1) * P], rows5[:, u, c * P:(c + 1) * P], ident[:, :])
                    last.then_inc(s_turn5, 1)
                for u in range(2):
                    pe.wait_ge(s_take5, 2 * i + u + 1)
                    for hf in range(2):
                        pe.wait_ge(s_free5, 2 * (2 * i + u) + hf + 1)
                        for c in range(3):
                            last = pe.matmul(ps[:, 4 + 2 * hf + c // 2, (c % 2) * 2 * P:(c % 2 + 1) * 2 * P],
                                             xt5[:, u, 3 * hf + c, :], wbd, start=True, stop=True)
                        last.then_inc(s_prod5, 1)

        def act_heads(act, step):
            act.wait_ge(s_ones5, 1)
            with step.loop(NT // 2, 4) as i:
                for u in range(2):
                    j = 2 * i + u
                    act.wait_ge(s_turn5, j + 3)
                    act.wait_ge(s_prod5, 2 * j + 1)
                    act.activation(xt5[:, u].rearrange("p (a b) n -> p a (b n)", a=2), ps[:, 2 * u:2 * u + 2, 0:HALF], ACT.Copy)\
                       .then_inc(s_take5, 1)
                for u in range(2):
                    j = 2 * i + u
                    act.wait_ge(s_res5[u], 16 * i)
                    for hf in range(2):
                        act.wait_ge(s_prod5, 2 * j + hf + 3)
                        for b, n in ((0, 2), (1, 1)):
                            blocks = ps[:, 4 + 2 * hf + b, 0:n * 2 * P].rearrange("p (c k m) -> p c k m", k=2, m=P)
                            head = 6 * hf + 4 * b
                            act.activation(hbuf[:, bass.ds(j * (D + 12) + head * 65, 65 * 2 * n)].rearrange("p (c h m) -> p c h m", h=2, m=65)[:, :, :, 0:64],
                                           blocks[:, :, 0, :].rearrange("p c (h m) -> p c h m", h=2), ACT.Copy)
                            ins = act.activation(res5[:, u, head * 64:head * 64 + n * P].rearrange("p (c m) -> p c m", m=P),
                                                 blocks[:, :, 1, :], ACT.Copy)
                        step(ins)
                        act.sem_inc(s_free5, 1)
                    act.dma_start(res_d[bass.ds(j * P, P), :], res5[:, u, :]).then_inc(s_res5[u], 16)
            for u in range(2):
                act.wait_ge(s_res5[u], 16 * (NT // 2))

        att2 = Attention("attb", 12, mask2v, [(a["L2_gnn_attn_l"].rearrange("o h c -> (o h c)"),
                                               a["L2_gnn_attn_r"].rearrange("o h c -> (o h c)"), agg2_d, None)])

        def self_loops(v, step, op):
            for j in range(NT):
                blk = cnt3[:, j, j * P:(j + 1) * P]
                step.count(v.tensor_tensor(blk, blk, ident[:, :], op))
            step.wait()

        c6 = Carve(work, 21248)
        in6 = [c6(2 * D).rearrange("p (u n) -> p u n", u=2) for _ in range(3)]
        s_in6, s_st6 = two("x3_parts_in"), two("x3_stored")
        s_free6, s_ready6 = sem("x3_free"), sem("x3_ready")
        norm6 = Norm()

        def sp_join(sp):
            with sp.Fori(0, NT // 2) as i:
                for u in range(2):
                    j = 2 * i + u
                    sp.wait_ge(s_st6[u], 16 * i)
                    for t, src in zip(in6, (agg2_d, res_d, x2_d)):
                        sp.dma_start(t[:, u, :], src[bass.ds(j * P, P), :]).then_inc(s_in6[u], 16)

        def act_join(act):
            with act.Fori(0, NT) as j:
                norm6.scalar(act, j)

        def dve_join(v, step):
            with step.loop(NT // 2, 2 * (2 + Norm.VSTEPS)) as i:
                for u in range(2):
                    z = in6[0][:, u, :]
                    v.wait_ge(s_in6[u], 48 * (i + 1))
                    step(v.tensor_tensor(z, z, in6[1][:, u, :], ALU.add))
                    step(v.scalar_tensor_tensor(z, z, 0.0, in6[2][:, u, :], ALU.max, ALU.add))
                    norm6.vector(v, step, z, 2 * i + u)
                    v.sem_inc(s_ready6, 1)

        c7 = Carve(work, 21248)
        wrel = c7(2 * KC * D)
        rows7 = c7(2 * D).rearrange("p (u r n) -> p u r n", u=2, r=1)
        xt7 = c7(2 * D).rearrange("p (u c n) -> p u c n", u=2, c=KC)
        brow7 = c7(D, parts=1)
        msg7 = c7(2 * D).rearrange("p (u n) -> p u n", u=2)
        idx7 = c7(2, I32)
        W_ROOT = Dense("root", [x3_d], [a["L3_gnn_W_root"]], wrel[:, 0:KC * D].rearrange("p (c n) -> p c n", c=KC),
                       rows7, xt7, a["L3_gnn_b_rgcn"], brow7)
        conv3 = Convolution(1, h1_d, a["L3_gnn_W_gcn"], a["L3_gnn_b_gcn"], x3_d, x4_d)
        s_wrel, s_gath, s_msgst = two("wrel_in"), two("rows_gathered"), two("messages_stored")
        s_turn7, s_take7, s_prod7, s_emp7, s_msg7 = (sem(n) for n in ("turned7", "taken7", "product7", "emptied7", "message_ready"))
        s_rootout = sem("root_out")

        def sp_rel(sp):
            W_ROOT.load(sp)
            W_ROOT.stream(sp)
            sp.wait_ge(W_ROOT.product, W_ROOT.all_products)
            with sp.Fori(0, R // 2) as i:
                for u in range(2):
                    r = 2 * i + u
                    last = sp.value_load(end_rel[0:1, bass.ds(r, 1)], min_val=0, max_val=RT)
                    sp.wait_ge(s_prod7, last + 2)
                    sp.dma_start(wrel[:, u * KC * D:(u + 1) * KC * D].rearrange("p (c n) -> p c n", c=KC),
                                 a["L3_gnn_W_rel"].rearrange("r (c p) n -> r p c n", p=P)[bass.ds(r, 1)].rearrange("r p c n -> (r p) c n"))\
                      .then_inc(s_wrel[u], 16)

        def pool_rel(g, step):
            def gather(k, u, n):
                g.wait_ge(s_turn7, k + 1)
                g.wait_ge(s_gath[u], n)
                step(g.tensor_copy(idx7[:, u:u + 1], relsrc[:, bass.ds(k, 1)]))
                step.carry()
                g.indirect_dma_start(out=rows7[:, u, 0, :], out_offset=None, in_=x3_d,
                                     in_offset=bass.IndirectOffsetOnAxis(idx7[:, u:u + 1], 0)).then_inc(s_gath[u], 16)

            g.wait_ge(W_ROOT.turned, W_ROOT.all_turned)
            for u in range(2):
                gather(u, u, 0)
            with step.loop(RT // 2, 2) as i:
                for u in range(2):
                    gather(2 * i + 2 + u, u, 16 * (i + 1))
                for u in range(2):
                    k = 2 * i + u
                    g.wait_ge(s_msg7, k + 1)
                    step.carry()
                    g.dma_start(msg_d[bass.ds(k * P, P), :], msg7[:, u, :]).then_inc(s_msgst[u], 16)
            for u in range(2):
                g.wait_ge(s_msgst[u], 16 * (RT // 2))
                g.wait_ge(s_gath[u], 16 * (RT // 2 + 1))

        def pe_rel(pe):
            W_ROOT.multiply(pe)
            pe.wait_ge(s_rootout, 1)
            pe.sem_inc(s_turn7, 2)
            pe.sem_inc(s_prod7, 2)
            with pe.Fori(0, RT // 2) as i:
                for u in range(2):
                    pe.wait_ge(s_gath[u], 16 * (i + 1))
                    for c in range(KC):
                        last = pe.transpose(ps[:, 2 * u + c // 3, (c % 3) * P:(c % 3 + 1) * P], rows7[:, u, 0, c * P:(c + 1) * P], ident[:, :])
                    last.then_inc(s_turn7, 1)
                for u in range(2):
                    k = 2 * i + u
                    r = pe.value_load(tile_rel[0:1, bass.ds(k, 1)], min_val=0, max_val=R - 1)
                    pe.wait_ge(s_wrel[0], (r + 2) // 2 * 16)
                    pe.wait_ge(s_wrel[1], (r + 1) // 2 * 16)
                    base = (r % 2) * (KC * D)
                    pe.wait_ge(s_take7, k + 1)
                    pe.wait_ge(s_emp7, k + 1)
                    for h in range(2):
                        for c in range(KC):
                            last = pe.matmul(ps[:, 4 + 2 * u + h, 0:HALF], xt7[:, u, c, :],
                                             wrel[:, bass.ds(base + (c * D + h * HALF), HALF)], start=(c == 0), stop=(c == KC - 1))
                    last.then_inc(s_prod7, 1)

        def act_rel(act, step):
            with step.loop(NT // 2, 2) as i:
                W_ROOT.take(act, i, 0)
                W_ROOT.take(act, i, 1)
                for u in range(2):
                    j = 2 * i + u
                    act.wait_ge(W_ROOT.product, W_ROOT.b["product"] + j + 3)
                    step(act.activation(halves(hbuf[:, bass.ds(j * D, D)]), W_ROOT.psum(u), ACT.Copy))
                    act.sem_inc(W_ROOT.emptied, 1)
            act.sem_inc(s_rootout, 1)
            with act.Fori(0, RT // 2) as i:
                for u in range(2):
                    k = 2 * i + u
                    act.wait_ge(s_turn7, k + 3)
                    act.wait_ge(s_prod7, k + 1)
                    act.activation(xt7[:, u].rearrange("p (a b) n -> p a (b n)", a=2), ps[:, 2 * u:2 * u + 2, 0:HALF], ACT.Copy)\
                       .then_inc(s_take7, 1)

        def dve_rel(v, step):
            v.sem_inc(W_ROOT.emptied, 2)
            v.sem_inc(s_emp7, 2)
            with v.Fori(0, RT // 2) as i:
                for u in range(2):
                    k = 2 * i + u
                    v.wait_ge(s_prod7, k + 3)
                    v.wait_ge(s_msgst[u], 16 * i)
                    v.tensor_copy(halves(msg7[:, u, :]), ps[:, 4 + 2 * u:6 + 2 * u, 0:HALF]).then_inc(s_msg7, 1)
                    v.wait_ge(s_msg7, k + 1)
                    v.sem_inc(s_emp7, 1)

        c8 = Carve(work, 21248)
        WAYS8 = 4
        mg8 = c8(WAYS8 * D).rearrange("p (u n) -> p u n", u=WAYS8)
        iv8 = c8(WAYS8)
        sel8 = c8(WAYS8 * P).rearrange("p (u n) -> p u n", u=WAYS8)
        idx8 = c8(2 * WAYS8, I32).rearrange("p (a u) -> p a u", a=2)
        idxs = c8(2 * BT, I32).rearrange("p (a k) -> p a k", a=2)
        s_g8 = [sem(f"messages_in{u}") for u in range(WAYS8)]
        s_idx8, s_sel8, s_sum8, s_add8, s_h1 = (sem(n) for n in ("indices8", "selected8", "summed8", "added8", "h1_stored"))

        def pool_sum(g, step):
            g.wait_ge(s_idx8, 1)
            with step.loop(BT // WAYS8, 2 * WAYS8) as i:
                for u in range(WAYS8):
                    k = WAYS8 * i + u
                    g.wait_ge(s_sum8, k + 1)
                    g.wait_ge(s_g8[u], 32 * i)
                    for q in range(2):
                        step.count(g.tensor_copy(idx8[:, q, u:u + 1], idxs[:, q, bass.ds(k, 1)]))
                    step.wait()
                    step.carry()
                    g.indirect_dma_start(out=mg8[:, u, :], out_offset=None, in_=msg_d,
                                         in_offset=bass.IndirectOffsetOnAxis(idx8[:, 0, u:u + 1], 0)).then_inc(s_g8[u], 16)
                    g.indirect_dma_start(out=iv8[:, u:u + 1], out_offset=None, in_=inv_d,
                                         in_offset=bass.IndirectOffsetOnAxis(idx8[:, 1, u:u + 1], 0)).then_inc(s_g8[u], 16)

        def pe_sum(pe):
            pe.sem_inc(s_sum8, WAYS8)
            with pe.Fori(0, BT // WAYS8) as i:
                for u in range(WAYS8):
                    k = WAYS8 * i + u
                    pe.wait_ge(s_sel8, k + 1)
                    pe.wait_ge(s_add8, k + 1)
                    for h in range(2):
                        last = pe.matmul(ps[:, 2 * (u % 4) + h, 0:HALF], sel8[:, u, :], mg8[:, u, h * HALF:(h + 1) * HALF], start=True, stop=True)
                    last.then_inc(s_sum8, 1)

        def dve_sum(v, step):
            step(v.tensor_copy(idxs[:, 0, :], drec3[:, :, 3]))
            step(v.tensor_copy(idxs[:, 1, :], drec3[:, :, 4]))
            v.sem_inc(s_idx8, 1)
            v.sem_inc(s_add8, WAYS8)
            with step.loop(BT // WAYS8, WAYS8) as i:
                def select(u):
                    k = WAYS8 * i + u
                    v.wait_ge(s_g8[u], 32 * (i + 1))
                    dr = drec3[:, bass.ds(k, 1), 1:2].rearrange("p k c -> p (k c)")
                    v.tensor_scalar(sel8[:, u, :], iota[:, 0:P], dr, iv8[:, u:u + 1], ALU.is_equal, ALU.mult).then_inc(s_sel8, 1)

                select(0)
                for u in range(WAYS8):
                    if u + 1 < WAYS8:
                        select(u + 1)
                    k = WAYS8 * i + u
                    b = v.value_load(tile_dst[0:1, bass.ds(k, 1)], min_val=0, max_val=NT - 1)
                    v.wait_ge(s_sum8, WAYS8 + k + 1)
                    t = halves(hbuf[:, bass.ds(b * D, D)])
                    step(v.tensor_tensor(t, ps[:, 2 * (u % 4):2 * (u % 4) + 2, 0:HALF], t, ALU.add))
                    v.sem_inc(s_add8, 1)

        def sp_h1(sp):
            sp.dma_start(h1_d.rearrange("(j p) n -> p j n", p=P), hbuf[:, 0:NT * D].rearrange("p (j n) -> p j n", j=NT)).then_inc(s_h1, 16)
            sp.wait_ge(s_h1, 16)

        s_out = sem("out_stored")

        block = ctx.enter_context(nc.Block())

        @block.sync
        def _(sp):
            sp_phase1(sp)
            meet(sp)
            meet(sp)
            sp.wait_ge(s_inv, 1)
            sp.dma_start(inv_d.rearrange("(j p r) c -> p j (r c)", p=P, r=R), inv).then_inc(s_invd, 16)
            sp.wait_ge(s_invd, 16)
            meet(sp)
            for l in range(3):
                att0.sp(sp, l)
                meet(sp)
            sp_wout(sp)
            meet(sp)
            conv1.sp(sp)
            meet(sp)
            sp_heads(sp)
            meet(sp)
            att2.sp(sp, 0)
            meet(sp)
            sp_join(sp)
            meet(sp)
            sp_rel(sp)
            meet(sp)
            meet(sp)
            sp_h1(sp)
            meet(sp)
            conv3.sp(sp)
            meet(sp)
            sp.dma_start(out, x4_d[0:N, :]).then_inc(s_out, 16)
            sp.wait_ge(s_out, 16)

        @block.tensor
        def _(pe):
            pe_phase1(pe)
            meet(pe)
            pe_phase2(pe)
            meet(pe)
            pe_phase3(pe)
            meet(pe)
            for l in range(3):
                att0.pe(pe, l)
                meet(pe)
            W_OUT.multiply(pe)
            meet(pe)
            conv1.pe(pe)
            meet(pe)
            pe_heads(pe)
            meet(pe)
            att2.pe(pe, 0)
            meet(pe)
            meet(pe)
            pe_rel(pe)
            meet(pe)
            pe_sum(pe)
            meet(pe)
            meet(pe)
            conv3.pe(pe)
            meet(pe)

        @block.scalar
        def _(act):
            step = Steps(act, act_step)
            act_phase1(act, step)
            meet(act)
            meet(act)
            act.wait_ge(s_deg, 1)
            act.activation(dinv[:, :], deg, ACT.Sqrt).then_inc(s_root, 1)
            meet(act)
            for l in range(3):
                att0.act(act, step, l)
                meet(act)
            act_wout(act)
            meet(act)
            conv1.act(act, step)
            meet(act)
            act_heads(act, step)
            meet(act)
            att2.act(act, step, 0)
            meet(act)
            act_join(act)
            meet(act)
            act_rel(act, step)
            meet(act)
            meet(act)
            meet(act)
            conv3.act(act, step)
            meet(act)

        @block.vector
        def _(v):
            step = Steps(v, dve_step, dve_carrier)
            dve_phase1(v, step)
            meet(v)
            dve_phase2(v, step)
            meet(v)
            dve_phase3(v, step)
            meet(v)
            for l in range(3):
                att0.dve(v, step, l)
                meet(v)
            dve_wout(v, step)
            meet(v)
            conv1.dve(v, step)
            meet(v)
            self_loops(v, step, ALU.subtract)
            meet(v)
            att2.dve(v, step, 0)
            meet(v)
            self_loops(v, step, ALU.add)
            dve_join(v, step)
            meet(v)
            dve_rel(v, step)
            meet(v)
            dve_sum(v, step)
            meet(v)
            meet(v)
            conv3.dve(v, step)
            meet(v)

        @block.gpsimd
        def _(g):
            step = Steps(g, pool_step, pool_carrier)
            pool_phase1(g, step)
            for _ in range(6):
                meet(g)
            store_tiles(g, step, s_z4, z4, x1_d, s_z4st)
            meet(g)
            conv1.pool(g, step)
            meet(g)
            pool_heads(g, step)
            meet(g)
            meet(g)
            store_tiles(g, step, s_ready6, in6[0], x3_d, s_st6)
            meet(g)
            pool_rel(g, step)
            meet(g)
            pool_sum(g, step)
            meet(g)
            meet(g)
            conv3.pool(g, step)
            meet(g)


_OUTS = [((N, D), "float32")]


def kernel(**inputs):
    import numpy as _np
    import concourse.bacc as _bacc
    from concourse import mybir as _mybir
    from concourse.bass_utils import run_bass_kernel_spmd as _run

    nc = _bacc.Bacc("TRN2", target_bir_lowering=False, num_devices=1)
    arrays, args = {}, {}
    for name, value in inputs.items():
        if name == "edge_weight1":
            continue
        v = _np.ascontiguousarray(value)
        if name in ("L2_gnn_W", "L2_gnn_W_res"):
            v = _np.ascontiguousarray(v.T)
        arrays[f"in_{name}"] = v
        args[name] = nc.dram_tensor(f"in_{name}", v.shape, _mybir.dt.from_np(v.dtype), kind="ExternalInput").ap()
    o = nc.dram_tensor("out_0", (N, D), _mybir.dt.float32, kind="ExternalOutput").ap()
    build(nc, args, o)
    r = _run(nc, [arrays], core_ids=[0])
    return r.results[0]["out_0"]
```

```python
from contextlib import ExitStack, contextmanager

import concourse.bass as bass
from concourse import mybir

F32 = mybir.dt.float32
F32R = mybir.dt.float32r
BF16 = mybir.dt.bfloat16
I32 = mybir.dt.int32
U16 = mybir.dt.uint16
ALU = mybir.AluOpType
ACT = mybir.ActivationFunctionType
AX = mybir.AxisListType.X

P = 128
N = 1250
NT = (N + P - 1) // P
NP = NT * P
D = 768
KC = D // P
HALF = D // 2
E = 20000
EP, ET = 125, 160
R = 34
RT = (E + R * (P - 1)) // P + 1
GT = 4
BG = (E + NT * (GT * P - 1)) // (GT * P)
BT = BG * GT
CW = NP + R
REC = 4
NONE = -1.0e30
SLOPE = 0.2
EPS_LN = 1e-5
TINY = 1e-16
WORK = 5 * KC * D
WAYS = 8




class Steps:

    def __init__(self, eng, sem, carrier=None):
        self.eng, self.sem, self.base, self.k, self.carrier = eng, sem, 0, 0, carrier

    def __call__(self, ins):
        ins.then_inc(self.sem, 1)
        self.k += 1
        self.eng.wait_ge(self.sem, self.base + self.k)

    def count(self, ins):
        ins.then_inc(self.sem, 1)
        self.k += 1

    def wait(self):
        self.eng.wait_ge(self.sem, self.base + self.k)

    def carry(self):
        self.eng.sem_inc(self.carrier, 1)

    @contextmanager
    def loop(self, times, per):
        start = self.base + self.k
        with self.eng.Fori(0, times) as i:
            self.base, self.k = start + i * per, 0
            yield i
            assert self.k == per, (self.k, per)
        self.base, self.k = start + times * per, 0


def build(nc, a, out):
    ctx = ExitStack()
    with ctx:
        def sb(name, shape, dt=F32):
            return ctx.enter_context(nc.sbuf_tensor(name, shape, dt))

        def sem(name):

            return ctx.enter_context(nc.semaphore(name))

        def dram(name, shape, dt=F32):
            return nc.dram_tensor(name, shape, dt, kind="Internal").ap()

        x0_d = dram("x0_d", (NP, D))
        xa_d = dram("xa_d", (NP, D))
        h_d = [dram(f"feat{l}_d", (NP, D + 4)) for l in range(3)]
        gat_d = [dram(f"gat{l}_d", (NP, D)) for l in range(3)]
        x1_d = dram("x1_d", (NP, D))
        x2_d = dram("x2_d", (NP, D))
        res_d = dram("res_d", (NP, D))
        agg2_d = dram("agg2_d", (NP, D))
        x3_d = dram("x3_d", (NP, D))
        h1_d = dram("h1_d", (NP, D))
        x4_d = dram("x4_d", (NP, D))
        msg_d = dram("msg_d", (RT * P, D))
        relrec_d = dram("relrec_d", (P * RT, 2), I32)
        dstrec_d = dram("dstrec_d", (P * BT, REC))
        inv_d = dram("inv_d", (NP * R, 1))

        cnt = sb("cnt", [P, NT * NP], U16)
        ct = sb("ct", [P, NT * CW], U16)
        hbuf = sb("hbuf", [P, NT * (D + 12)])
        ident = sb("ident", [P, P])
        ones = sb("ones", [P, P])
        tri = sb("tri", [P, P])
        iota = sb("iota", [P, NP], U16)
        relrec = sb("relrec", [P, (RT + 2) * 2], I32)
        drec = sb("drec", [P, BT * REC])
        tile_rel = sb("tile_rel", [1, RT], I32)
        group_dst = sb("group_dst", [1, BG], I32)
        end_rel = sb("end_rel", [1, R + 2], I32)
        dinv = sb("dinv", [P, NT])
        small = sb("small", [P, 64])
        padt = sb("padt", [P, R], I32)
        endf = sb("endf", [P, R])
        owners = sb("owners", [1, RT])
        with nc.sbuf_tensor("mask1", [P, NT * NP], BF16) as mask1, nc.sbuf_tensor("work", [P, WORK], F32) as work:
            pass
        xsplit = sb("xsplit", [P, 4 * D], F32R)
        xplain = sb("xplain", [P, NT * NP // 2 - 4 * D])
        wsplit = sb("wsplit", [P, 4 * KC * D], F32R)
        wplain = sb("wplain", [P, KC * D])
        ps = ctx.enter_context(nc.psum_tensor("ps", [P, 8, 512], F32))
        psf = ps[:, :, :].rearrange("p b n -> p (b n)")

        cnt3 = cnt[:, :].rearrange("p (j n) -> p j n", j=NT)
        mask1v = mask1[:, :].rearrange("p (j n) -> p j n", j=NT)
        ct3 = ct[:, :].rearrange("p (j n) -> p j n", j=NT)
        mask2v = ct[:, :].bitcast(BF16).rearrange("p (j n) -> p j n", j=NT)
        drec3 = drec[:, :].rearrange("p (k c) -> p k c", c=REC)

        class Carve:

            def __init__(self, region, size):
                self.region, self.size, self.at = region, size, 0

            def __call__(self, n, dt=F32, parts=P):
                w = n if dt in (F32, I32) else (n + 1) // 2
                v = self.region[0:parts, self.at:self.at + w]
                self.at += w
                assert self.at <= self.size, self.at
                return v if dt is F32 else v.bitcast(dt)

        def halves(v):
            return v.rearrange("p (a n) -> p a n", a=2)

        met = sem("met")
        meetings = {}

        def meet(eng):
            meetings[eng] = meetings.get(eng, 0) + 1
            eng.drain().then_inc(met, 1)
            eng.wait_ge(met, 5 * meetings[eng])

        dve_step, act_step, pool_step = sem("dve_step"), sem("act_step"), sem("pool_step")
        dve_carrier, pool_carrier = sem("dve_carrier"), sem("pool_carrier")

        dense_sems = {n: sem("dense_" + n) for n in ("w_in0", "w_in1", "turned", "taken", "product", "emptied")}
        dense_sems["rows_in"] = [sem(f"dense_rows_in{u}") for u in range(2)]
        dense_counts = {n: 0 for n in [*dense_sems, "stages"]}

        class Dense:

            def __init__(self, name, rows, weights, w_at, rows_at, xt_at, bias=None, bias_at=None, beside=None):
                self.beside = beside
                self.rows, self.w, self.K = rows, weights, len(rows)
                self.w_at, self.rows_at, self.xt_at = w_at, rows_at, xt_at
                self.bias, self.bias_at = bias, bias_at
                self.pick = f"w_in{dense_counts['stages'] % 2}"
                dense_counts["stages"] += 1
                self.w_in, self.rows_in = dense_sems[self.pick], dense_sems["rows_in"]
                self.turned = dense_sems["turned"]
                self.taken = dense_sems["taken"]
                self.product = dense_sems["product"]
                self.emptied = dense_sems["emptied"]
                K, nw = self.K, 16 * (self.K + (bias is not None))
                self.b = dict(dense_counts)
                for key, more in ((self.pick, nw), ("rows_in", 16 * K * (NT // 2)), ("turned", K * (NT + 2)), ("taken", K * NT),
                                  ("product", NT + 2), ("emptied", NT + 2)):
                    dense_counts[key] += more
                self.all_turned = dense_counts["turned"]
                self.all_products = dense_counts["product"]

            def load(self, sp):
                for r in range(self.K):
                    sp.dma_start(self.w_at[:, r * KC:(r + 1) * KC, :],
                                 self.w[r].rearrange("(c p) n -> p c n", p=P)).then_inc(self.w_in, 16)
                if self.bias is not None:
                    sp.dma_start(self.bias_at, self.bias.rearrange("(a n) -> a n", a=1)).then_inc(self.w_in, 16)

            def stream(self, sp):
                with sp.Fori(0, NT // 2) as i:
                    for u in range(2):
                        j = 2 * i + u
                        sp.wait_ge(self.turned, self.b["turned"] + self.K * (j + 1))
                        for r in range(self.K):
                            sp.dma_start(self.rows_at[:, u, r, :], self.rows[r][bass.ds(j * P, P), :])\
                              .then_inc(self.rows_in[u], 16)
                        if self.beside is not None:
                            sp.wait_ge(self.emptied, self.b["emptied"] + j + 1)
                            sp.dma_start(self.beside[1][:, u, :], self.beside[0][bass.ds(j * P, P), :]).then_inc(self.beside[2][u], 16)

            def multiply(self, pe):
                K = self.K
                pe.wait_ge(self.turned, self.b["turned"] + 0)
                pe.wait_ge(self.product, self.b["product"])
                pe.sem_inc(self.turned, 2 * K)
                pe.sem_inc(self.product, 2)
                pe.wait_ge(self.w_in, self.b[self.pick] + 16 * (K + (self.bias is not None)))
                with pe.Fori(0, NT // 2) as i:
                    def turn(u, r):
                        q = K * u + r
                        if r == 0:
                            pe.wait_ge(self.rows_in[u], self.b["rows_in"] + 16 * K * (i + 1))
                        if K > 1 and q >= 2:
                            pe.wait_ge(self.taken, self.b["taken"] + 2 * K * i + q - 1)
                        for c in range(KC):
                            last = pe.transpose(ps[:, 2 * (q % 2) + c // 3, (c % 3) * P:(c % 3 + 1) * P],
                                                self.rows_at[:, u, r, c * P:(c + 1) * P], ident[:, :])
                        last.then_inc(self.turned, 1)

                    def times(u):
                        j = 2 * i + u
                        pe.wait_ge(self.taken, self.b["taken"] + K * (j + 1))
                        pe.wait_ge(self.emptied, self.b["emptied"] + j + 1)
                        for h in range(2):
                            o = ps[:, 4 + 2 * u + h, 0:HALF]
                            for c in range(K * KC):
                                last = pe.matmul(o, self.xt_at[:, u, c, :], self.w_at[:, c, h * HALF:(h + 1) * HALF],
                                                 start=(c == 0), stop=(c == K * KC - 1 and self.bias is None))
                            if self.bias is not None:
                                last = pe.matmul(o, ones[0:1, :], self.bias_at[:, h * HALF:(h + 1) * HALF],
                                                 start=False, stop=True)
                        last.then_inc(self.product, 1)

                    if K == 1:
                        turn(0, 0)
                        turn(1, 0)
                        times(0)
                        times(1)
                    else:
                        for u in range(2):
                            for r in range(K):
                                turn(u, r)
                            times(u)

            def take(self, act, i, u, col=None):
                K, j = self.K, 2 * i + u
                act.wait_ge(self.product, self.b["product"] + j + 1)
                for r in range(K):
                    q = K * u + r
                    act.wait_ge(self.turned, self.b["turned"] + 2 * K + 2 * K * i + q + 1)
                    if col is None:
                        ins = act.activation(self.xt_at[:, u, r * KC:(r + 1) * KC, :].rearrange("p (a b) n -> p a (b n)", a=2),
                                             ps[:, 2 * (q % 2):2 * (q % 2) + 2, 0:HALF], ACT.Copy)
                    else:
                        for c in range(KC):
                            ins = act.activation(self.xt_at[:, u, r * KC + c, :],
                                                 ps[:, 2 * (q % 2) + c // 3, (c % 3) * P:(c % 3 + 1) * P],
                                                 ACT.Relu, bias=col[:, r * KC + c:r * KC + c + 1])
                    ins.then_inc(self.taken, 1)

            def psum(self, u):
                return ps[:, 4 + 2 * u:6 + 2 * u, 0:HALF]

        norm_var, norm_root = sem("norm_var"), sem("norm_root")

        class Norm:

            used = 0

            def __init__(self):
                self.var, self.root = norm_var, norm_root
                self.b = NT * Norm.used
                Norm.used += 1

            def vector(self, v, step, z, j):
                st = small[:, 0:12].rearrange("p (a n) -> p a n", a=2)
                mv = small[:, 12:14]
                step.count(v.bn_stats(st[:, 0, :], z[:, 0:HALF]))
                step(v.bn_stats(st[:, 1, :], z[:, HALF:D]))
                step.carry()
                step(v.bn_aggr(mv, st))
                v.tensor_scalar(small[:, 14:15], mv[:, 1:2], EPS_LN, None, ALU.add).then_inc(self.var, 1)
                v.wait_ge(self.root, self.b + j + 1)
                step(v.reciprocal(small[:, 16:17], small[:, 15:16]))
                step(v.tensor_scalar(z, z, mv[:, 0:1], small[:, 16:17], ALU.subtract, ALU.mult))

            def scalar(self, act, j):
                act.wait_ge(self.var, self.b + j + 1)
                act.activation(small[:, 15:16], small[:, 14:15], ACT.Sqrt).then_inc(self.root, 1)
            VSTEPS = 5

        c1 = Carve(work, WORK)
        w_slots = [c1(KC * D).rearrange("p (c n) -> p c n", c=KC) for _ in range(2)]
        rows1 = c1(2 * D).rearrange("p (u r n) -> p u r n", u=2, r=1)
        xt1 = c1(2 * D).rearrange("p (u c n) -> p u c n", u=2, c=KC)
        brow1 = c1(D, parts=1)
        outs1 = c1(2 * (D + 4)).rearrange("p (u n) -> p u n", u=2)
        edges = c1(3 * ET, I32, EP).rearrange("p (a t) -> p a t", a=3)
        rec = c1(ET * REC, F32, EP).rearrange("p (t c) -> p t c", c=REC)
        addr = c1(2 * ET, I32, EP).rearrange("p (a t) -> p a t", a=2)
        relpay = c1(2 * ET, I32, EP).rearrange("p (t c) -> p t c", c=2)
        ibuf = c1(2 * ET, I32, EP).rearrange("p (a t) -> p a t", a=2)
        fbuf = c1(2 * ET, F32, EP).rearrange("p (a t) -> p a t", a=2)
        islot = c1(4 * WAYS, I32, EP).rearrange("p (w c) -> p w c", w=WAYS)
        rslot = c1(REC * WAYS, F32, EP).rearrange("p (w c) -> p w c", c=REC)
        offs = c1(2 * (R + NT)).rearrange("p (a n) -> p a n", a=2)
        marks = [cnt[0:EP, :].bitcast(F32)[:, 0:R * ET], hbuf[0:EP, 3000:3000 + NT * ET]]
        scans = [mask1[0:EP, :].bitcast(F32)[:, 0:R * ET], hbuf[0:EP, 3000 + NT * ET:3000 + 2 * NT * ET]]
        padrel = ct[:, 0:4 * RT].bitcast(I32)
        paddst = hbuf[:, 0:BT * REC].rearrange("p (k c) -> p k c", c=REC)
        zrows = hbuf[0:NP - N, 2000:2000 + D]
        s_x = sem("x_padded")
        s_edges = sem("edges_in")
        s_const = sem("constants")
        s_tables = sem("tables_cleared")
        s_pads = sem("pad_records")
        s_rowsum = sem("row_sums")
        s_offs = sem("offsets")
        s_offtaken = sem("offsets_taken")
        s_addr = sem("addresses")
        s_scat = [sem(f"scattered{w}") for w in range(WAYS)]
        s_x1 = [sem(f"x1_out{u}") for u in range(2)]
        s_h = [sem(f"h_out{u}") for u in range(2)]
        s_recs = sem("records_in")

        W_AH = Dense("ah", [x0_d], [a["L0_gnn_W_ah"]], w_slots[0], rows1, xt1, a["L0_gnn_b_ah"], brow1)
        W_H = [Dense(f"h{l}", [xa_d], [a[f"L0_gnn_W{l}"]], w_slots[(l + 1) % 2], rows1, xt1) for l in range(3)]
        PREFIX = [(0, 0, R, 7, RT, RT), (1, R, NT, 7 + (GT - 1).bit_length(), BT, BG)]

        def sp_phase1(sp):
            sp.dma_start(edges[:, 0, :], a["src"].rearrange("(p t) -> p t", p=EP)).then_inc(s_edges, 16)
            sp.dma_start(edges[:, 1, :], a["dst"].rearrange("(p t) -> p t", p=EP)).then_inc(s_edges, 16)
            sp.dma_start(edges[:, 2, :], a["edge_type_34"].rearrange("(p t) -> p t", p=EP)).then_inc(s_edges, 16)
            sp.dma_start(x0_d[0:N, :], a["x"]).then_inc(s_x, 16)
            W_AH.load(sp)
            W_H[0].load(sp)
            sp.wait_ge(s_const, 1)
            sp.dma_start(x0_d[N:NP, :], zrows).then_inc(s_x, 16)
            sp.wait_ge(s_x, 32)
            W_AH.stream(sp)
            for u in range(2):
                sp.wait_ge(s_x1[u], 16 * NT // 2)
            for l in range(3):
                if l:
                    sp.wait_ge(W_AH.product, (W_AH if l == 1 else W_H[0]).all_products)
                    W_H[l].load(sp)
                sp.wait_ge(W_AH.turned, (W_AH if l == 0 else W_H[l - 1]).all_turned)
                W_H[l].stream(sp)

        def act_phase1(act, step):
            act.sem_inc(W_AH.emptied, 2)
            with step.loop(NT // 2, 2) as i:
                W_AH.take(act, i, 0)
                W_AH.take(act, i, 1)
                for u in range(2):
                    j = 2 * i + u
                    act.wait_ge(W_AH.product, W_AH.b["product"] + j + 3)
                    act.wait_ge(s_x1[u], 16 * i)
                    step(act.activation(halves(outs1[:, u, 0:D]), W_AH.psum(u), ACT.Relu))
                    act.sem_inc(W_AH.emptied, 1)
                    act.dma_start(xa_d[bass.ds(j * P, P), :], outs1[:, u, 0:D]).then_inc(s_x1[u], 16)
            for u in range(2):
                act.wait_ge(s_x1[u], 16 * NT // 2)
            hv = [outs1[:, u, :].rearrange("p (h c) -> p h c", h=4) for u in range(2)]
            act.wait_ge(s_const, 2)
            for u in range(2):
                step(act.activation(hv[u][:, :, 192], ones[:, 0:4], ACT.Copy))
            for l in range(3):
                act.sem_inc(W_H[l].emptied, 2)
                with step.loop(NT // 2, 4) as i:
                    W_H[l].take(act, i, 0)
                    W_H[l].take(act, i, 1)
                    for u in range(2):
                        j = 2 * i + u
                        act.wait_ge(W_H[l].product, W_H[l].b["product"] + j + 3)
                        act.wait_ge(s_h[u], 16 * i + 16 * l * (NT // 2))
                        for b in range(2):
                            step.count(act.activation(hv[u][:, 2 * b:2 * b + 2, 0:192],
                                                      ps[:, 4 + 2 * u + b, 0:HALF].rearrange("p (h c) -> p h c", h=2), ACT.Copy))
                        step.wait()
                        act.sem_inc(W_H[l].emptied, 1)
                        act.dma_start(h_d[l][bass.ds(j * P, P), :], outs1[:, u, :]).then_inc(s_h[u], 16)
            for u in range(2):
                act.wait_ge(s_h[u], 3 * 16 * NT // 2)

        def pe_phase1(pe):
            pe.wait_ge(s_const, 3)
            W_AH.multiply(pe)
            pe.wait_ge(s_rowsum, 1)
            pe.matmul(ps[:, 0, HALF:HALF + R + NT], tri[0:EP, :], small[0:EP, 0:R + NT], start=True, stop=True)
            pe.matmul(ps[:, 1, HALF:HALF + R + NT], ones[0:EP, :], small[0:EP, 0:R + NT], start=True, stop=True).then_inc(s_offs, 1)
            pe.wait_ge(s_offtaken, 1)
            for s in W_H:
                s.multiply(pe)

        def dve_phase1(v, step):
            v.wait_ge(s_edges, 48)
            v.wait_ge(s_const, 3)
            src, dst, typ = (edges[:, k, :] for k in range(3))
            step(v.tensor_scalar(ibuf[:, 0, :], dst, 7, None, ALU.arith_shift_right))
            step(v.tensor_scalar(ibuf[:, 1, :], dst, P - 1, None, ALU.bitwise_and))
            step(v.tensor_copy(rec[:, :, 0], src))
            step(v.tensor_copy(rec[:, :, 1], ibuf[:, 1, :]))
            step(v.tensor_copy(rec[:, :, 2], typ))
            step(v.tensor_copy(fbuf[:, 0, :], dst))
            step(v.tensor_copy(fbuf[:, 1, :], ibuf[:, 0, :]))
            step(v.tensor_copy(relpay[:, :, 0], src))
            step(v.scalar_tensor_tensor(relpay[:, :, 1], fbuf[:, 0, :], float(R), rec[:, :, 2], ALU.mult, ALU.add))
            for g, b0, nb, _, _, _ in PREFIX:
                key = rec[:, :, 2] if g == 0 else fbuf[:, 1, :]
                for b in range(nb):
                    step.count(v.tensor_scalar(marks[g][:, b * ET:(b + 1) * ET], key, float(b), None, ALU.is_equal))
                step.wait()
                step(v.tensor_tensor_scan(scans[g], marks[g], marks[g], 0.0, ALU.add, ALU.max))
                last = scans[g].rearrange("p (b t) -> p b t", b=nb)[:, :, ET - 1]
                tot = small[0:EP, b0:b0 + nb]
                step.count(v.tensor_copy(tot[:, 0:1], last[:, 0:1]))
                step(v.tensor_tensor(tot[:, 1:nb], last[:, 1:nb], last[:, 0:nb - 1], ALU.subtract))
            v.sem_inc(s_rowsum, 1)
            v.wait_ge(s_offs, 1)
            step(v.tensor_copy(offs, ps[:, 0:2, HALF:HALF + R + NT]))
            v.sem_inc(s_offtaken, 1)
            for g, b0, nb, shift, nt, units in PREFIX:
                scan3 = scans[g].rearrange("p (b t) -> p b t", b=nb)
                last, rowoff = scan3[:, :, ET - 1], fbuf[:, 0, 0:nb]
                ti, tf, ef = padt[:, 0:nb], small[:, 0:nb], endf[:, 0:nb]
                step(v.tensor_scalar(ti, offs[:, 1, b0:b0 + nb], float((1 << shift) - 1), None, ALU.add))
                step(v.tensor_scalar(ti, ti, shift, None, ALU.arith_shift_right))
                step(v.tensor_copy(tf, ti))
                step(v.tensor_tensor_scan(ef, tf, tf, 0.0, ALU.add, ALU.max))
                step(v.tensor_tensor(tf, ef, tf, ALU.subtract))
                step(v.scalar_tensor_tensor(rowoff, tf[0:EP], float(1 << shift), offs[0:EP, 0, b0:b0 + nb], ALU.mult, ALU.add))
                step(v.tensor_scalar(rowoff, rowoff, -1.0, None, ALU.add))
                step(v.tensor_tensor(rowoff[:, 1:nb], rowoff[:, 1:nb], last[:, 0:nb - 1], ALU.subtract))
                for b in range(nb):
                    o = marks[g][:, b * ET:(b + 1) * ET]
                    step.count(v.scalar_tensor_tensor(o, scan3[:, b, :], rowoff[:, b:b + 1], o, ALU.add, ALU.mult))
                step.wait()
                pos = rec[:, :, 3] if g == 0 else fbuf[:, 0, :]
                step(v.tensor_reduce(pos, marks[g].rearrange("p (b t) -> p t b", b=nb), AX, ALU.add))
                step(v.tensor_copy(ibuf[:, 0, :], pos))
                step(v.tensor_scalar(ibuf[:, 1, :], ibuf[:, 0, :], P - 1, None, ALU.bitwise_and))
                step(v.tensor_scalar(ibuf[:, 0, :], ibuf[:, 0, :], 7, None, ALU.arith_shift_right))
                step(v.scalar_tensor_tensor(addr[:, g, :], ibuf[:, 1, :], float(nt), ibuf[:, 0, :], ALU.mult, ALU.add))
                owner = owners[:, 0:units]
                step(v.memset(owner, 0.0))
                for b in range(nb):
                    step(v.scalar_tensor_tensor(owner, iota[0:1, 0:units], endf[0:1, b:b + 1], owner, ALU.is_ge, ALU.add))
                step(v.tensor_scalar((tile_rel if g == 0 else group_dst)[:, :], owner, float(nb - 1), None, ALU.min))
                if g == 0:
                    step(v.memset(end_rel[:, :], 0))
                    step(v.tensor_copy(end_rel[:, 2:R + 2], endf[0:1, 0:R]))
            v.sem_inc(s_addr, 1)

        def pool_phase1(g, step):
            step(g.memset(hbuf[0:32, 2000:2000 + D], 0.0))
            g.sem_inc(s_const, 1)
            step(g.memset(ones[:, :], 1.0))
            g.sem_inc(s_const, 1)
            step(g.memset(ident[:, :], 0.0))
            step(g.affine_select(out=ident[:, :], in_=ident[:, :], compare_op=ALU.not_equal, fill=1.0,
                                 base=0, pattern=[[-1, P]], channel_multiplier=1))
            step(g.affine_select(out=tri[:, :], in_=ones[:, :], compare_op=ALU.is_gt, fill=0.0,
                                 base=0, pattern=[[1, P]], channel_multiplier=-1))
            step(g.iota(iota[:, :], [[1, NP]], base=0, channel_multiplier=0))
            g.sem_inc(s_const, 1)
            step(g.memset(padrel, 0))
            step(g.memset(paddst, 0.0))
            step(g.memset(paddst[:, :, 0:2], -1.0))
            g.dma_start(relrec_d.rearrange("(p k) c -> p (k c)", p=P), padrel).then_inc(s_pads, 16)
            g.dma_start(dstrec_d.rearrange("(p k) c -> p (k c)", p=P), paddst.rearrange("p k c -> p (k c)")).then_inc(s_pads, 16)
            g.wait_ge(s_pads, 32)
            step(g.memset(ct[:, :], 0))
            g.wait_ge(s_addr, 1)
            scatter(g, step, 1)
            g.dma_start(drec[:, :], dstrec_d.rearrange("(p k) c -> p (k c)", p=P)).then_inc(s_recs, 16)
            g.wait_ge(s_recs, 16)

        def scatter(g, step, which):
            before = 0 if which == 1 else 16 * (ET // WAYS)

            def column(t, w, first):
                if not first:
                    g.wait_ge(s_scat[w], before + 16 * (t // WAYS))
                if which == 0:
                    step.count(g.tensor_copy(islot[:, w, 2:4], relpay[:, bass.ds(t, 1), :].rearrange("p t c -> p (t c)")))
                else:
                    step.count(g.tensor_copy(rslot[:, w, :], rec[:, bass.ds(t, 1), :].rearrange("p t c -> p (t c)")))
                step(g.tensor_copy(islot[:, w, which:which + 1], addr[:, which, bass.ds(t, 1)]))
                step.carry()
                g.indirect_dma_start(out=(relrec_d, dstrec_d)[which],
                                     out_offset=bass.IndirectOffsetOnAxis(islot[:, w, which:which + 1], 0),
                                     in_=(islot[:, w, 2:4], rslot[:, w, :])[which], in_offset=None).then_inc(s_scat[w], 16)

            for w in range(WAYS):
                column(w, w, which == 1)
            with step.loop(ET // WAYS - 1, 2 * WAYS) as i:
                for w in range(WAYS):
                    column(WAYS * (i + 1) + w, w, False)
            for w in range(WAYS):
                g.wait_ge(s_scat[w], before + 16 * (ET // WAYS))

        def pool_phase2(g, step):
            scatter(g, step, 0)
            step(g.memset(relrec[:, 2 * RT:], 0))
            g.dma_start(relrec[:, 0:2 * RT], relrec_d.rearrange("(p k) c -> p (k c)", p=P)).then_inc(s_recs, 16)
            g.wait_ge(s_recs, 32)

        c2 = Carve(work, WORK)
        oh_t = c2(2 * GT * P, BF16).rearrange("p (u n) -> p u n", u=2 * GT)
        oh_s = c2(2 * GT * CW, BF16).rearrange("p (u n) -> p u n", u=2 * GT)
        s_oh = sem("onehots")
        s_ctp = sem("count_products")
        s_cta = sem("counts_added")

        def group_loop(fori, group):
            with fori(BG // 2) as i:
                for u in range(2):
                    group(2 * i + u, u)
            if BG % 2:
                group(BG - 1, 0)

        def dve_phase2(v, step):
            v.sem_inc(s_cta, 2)

            def compare(k, u):
                v.wait_ge(s_ctp, k + 1)
                for w in range(GT):
                    dr = drec3[:, bass.ds(GT * k + w, 1), :].rearrange("p k c -> p (k c)")
                    v.tensor_scalar(oh_t[:, GT * u + w, :], iota[:, 0:P], dr[:, 1:2], None, ALU.is_equal)
                    v.tensor_scalar(oh_s[:, GT * u + w, 0:NP], iota[:, :], dr[:, 0:1], None, ALU.is_equal)
                    v.tensor_scalar(oh_s[:, GT * u + w, NP:CW], iota[:, 0:R], dr[:, 2:3], None, ALU.is_equal).then_inc(s_oh, 1)

            def add(k, u):
                b = v.value_load(group_dst[0:1, bass.ds(k, 1)], min_val=0, max_val=NT - 1)
                v.wait_ge(s_ctp, k + 3)
                c = ct[:, bass.ds(b * CW, CW)]
                step(v.tensor_tensor(c, psf[:, u * 2048:u * 2048 + CW], c, ALU.add))
                v.sem_inc(s_cta, 1)

            compare(0, 0)
            with step.loop((BG - 1) // 2, 2) as i:
                for u in range(2):
                    compare(2 * i + u + 1, 1 - u)
                    add(2 * i + u, u)
            for k in range((BG - 1) // 2 * 2, BG):
                if k + 1 < BG:
                    compare(k + 1, (k + 1) % 2)
                add(k, k % 2)

        def pe_phase2(pe):
            def group(k, u):
                pe.wait_ge(s_cta, k + 1)
                for w in range(GT):
                    pe.wait_ge(s_oh, GT * k + w + 1)
                    for n0 in range(0, CW, 512):
                        n1 = min(n0 + 512, CW)
                        last = pe.matmul(psf[:, u * 2048 + n0:u * 2048 + n1], oh_t[:, GT * u + w, :], oh_s[:, GT * u + w, n0:n1],
                                         start=(w == 0), stop=(w == GT - 1))
                last.then_inc(s_ctp, 1)

            pe.sem_inc(s_ctp, 2)
            group_loop(lambda n: pe.Fori(0, n), group)

        c3 = Carve(work, WORK)
        crow = c3(2 * NP).rearrange("p (u n) -> p u n", u=2)
        deg = c3(NT)
        inv = c3(NT * R).rearrange("p (j r) -> p j r", j=NT)
        s_crow = sem("count_rows")
        s_cturn = sem("counts_turned")
        s_inv = sem("inverse_counts")
        s_invd = sem("inverse_counts_stored")
        s_deg = sem("degrees")
        s_root = sem("degree_roots")

        def dve_phase3(v, step):
            step(v.tensor_scalar(inv, ct3[:, :, NP:CW], 1.0, None, ALU.max))
            step(v.reciprocal(inv, inv))
            v.sem_inc(s_inv, 1)
            with step.loop(NT // 2, 12) as i:
                for u in range(2):
                    j = 2 * i + u
                    v.wait_ge(s_cturn, j + 1)
                    row, c = crow[:, u, :], ct[:, bass.ds(j * CW, NP)]
                    step(v.tensor_copy(row, c))
                    dg = crow[:, u, bass.ds(j * P, P)]
                    step(v.tensor_tensor(dg, dg, ident[:, :], ALU.add))
                    v.sem_inc(s_crow, 1)
                    step(v.tensor_scalar(mask1[:, bass.ds(j * NP, NP)], row, 0.0, NONE, ALU.is_equal, ALU.mult))
                    step(v.tensor_scalar(ct[:, bass.ds(j * CW, NP)].bitcast(BF16), c, 0.0, NONE, ALU.is_equal, ALU.mult))
                    step(v.tensor_reduce(deg[:, bass.ds(j, 1)], row, AX, ALU.add))
                    v.wait_ge(s_cturn, j + 3)
                    step(v.tensor_copy(cnt3[:, :, bass.ds(j * P, P)], psf[:, u * 2048:u * 2048 + NP].rearrange("p (s n) -> p s n", n=P)))
            v.sem_inc(s_deg, 1)
            v.wait_ge(s_root, 1)
            step(v.reciprocal(dinv[:, :], dinv[:, :]))

        def pe_phase3(pe):
            pe.sem_inc(s_cturn, 2)
            with pe.Fori(0, NT // 2) as i:
                for u in range(2):
                    j = 2 * i + u
                    pe.wait_ge(s_crow, j + 1)
                    for s in range(NT):
                        last = pe.transpose(psf[:, u * 2048 + s * P:u * 2048 + (s + 1) * P], crow[:, u, s * P:(s + 1) * P], ident[:, :])
                    last.then_inc(s_cturn, 1)

        class Attention:
            def __init__(self, name, HN, mask, layers):
                self.HN, self.C, self.mask, self.layers = HN, D // HN, mask, layers
                self.banks = 5 if HN == 4 else 2
                self.tpb = NT // self.banks
                cv = Carve(work, WORK)
                self.cv = cv
                self.arow = cv(2 * D).rearrange("p (a n) -> p a n", a=2)
                self.prod = cv(2 * D).rearrange("p (a n) -> p a n", a=2)
                heads = [cv((HN + 1) * NT).rearrange("p (h j) -> p h j", h=HN + 1) for _ in range(7)]
                self.after = [heads[k][:, HN, :] for k in (3, 4)]
                self.L, self.Rr, self.M, self.R1, self.R2, self.L2, self.y = heads
                self.full = heads
                self.mh = cv(NT)
                self.diag = [cv(NP) for _ in range(2)]
                self.R1b = [cv(NP) for _ in range(2)]
                self.R2b = [cv(NP) for _ in range(2)]
                self.t2 = [cv(NP) for _ in range(2)]
                self.t = [cv(NP) for _ in range(2)]
                self.p = [cv(NP) for _ in range(2)]
                self.junk = self.p[0]
                self.o = cv(NT * self.C)
                self.den = cv(NT)
                (self.s_in_, self.s_diagA, self.s_bcA, self.s_maxed, self.s_hr, self.s_diagC, self.s_bcC, self.s_rb, self.s_t2r,
                 self.s_tr, self.s_er, self.s_pr, self.s_agg, self.s_out, self.s_stored, self.s_aggfree) = (
                    sem(f"{name}_{s}") for s in ("inputs_in", "max_spread", "max_rows", "maxed", "heads_ready", "spread", "rows",
                                                 "rows_taken", "second_ready", "exponent_ready", "exp_ready", "weights_ready",
                                                 "summed", "head_ready", "head_stored", "sums_free"))
                self.H = hbuf[:, 0:NT * (D + HN)].rearrange("p (j h c) -> p j h c", j=NT, h=HN)

            def sp(self, sp, n):
                al, ar, o_dram, load_from = self.layers[n]
                sp.dma_start(self.arow[:, 0, :], al.partition_broadcast(P)).then_inc(self.s_in_, 16)
                sp.dma_start(self.arow[:, 1, :], ar.partition_broadcast(P)).then_inc(self.s_in_, 16)
                if load_from is not None:
                    sp.dma_start(hbuf[:, 0:NT * (D + self.HN)].rearrange("p (j n) -> p j n", j=NT),
                                 load_from.rearrange("(j p) n -> p j n", p=P)).then_inc(self.s_in_, 16)
                od = o_dram.rearrange("(j p) n -> p j n", p=P)
                with sp.Fori(0, self.HN) as h:
                    sp.wait_ge(self.s_out, self.HN * n + h + 1)
                    sp.dma_start(od[:, :, bass.ds(h * self.C, self.C)], self.o.rearrange("p (j c) -> p j c", j=NT))\
                      .then_inc(self.s_stored, 16)
                sp.wait_ge(self.s_stored, 16 * self.HN * (n + 1))

            def spread(self, v, out, vec):
                return v.tensor_tensor(out.rearrange("p (j n) -> p j n", j=NT),
                                       ident[:, :].unsqueeze(1).to_broadcast([P, NT, P]),
                                       vec.unsqueeze(2).to_broadcast([P, NT, P]), ALU.mult)

            def dve(self, v, step, n):
                HN, C = self.HN, self.C
                H0 = HN * n
                if n == 0:
                    v.sem_inc(self.s_tr, 2)
                    v.sem_inc(self.s_pr, 2)
                v.wait_ge(self.s_in_, 16 * (3 if self.layers[n][3] is not None else 2) * (n + 1))
                with step.loop(NT, 4) as j:
                    hj = hbuf[:, bass.ds(j * (D + HN), D + HN)].rearrange("p (h c) -> p h c", h=HN)[:, :, 0:C]
                    for k, dest in ((0, self.L), (1, self.Rr)):
                        pr = self.prod[:, k, :].rearrange("p (h c) -> p h c", h=HN)
                        step(v.tensor_tensor(pr, hj, self.arow[:, k, :].rearrange("p (h c) -> p h c", h=HN), ALU.mult))
                        step(v.tensor_reduce(dest[:, 0:HN, bass.ds(j, 1)].rearrange("p h j -> p (h j)"), pr, AX, ALU.add))
                with step.loop(HN, NT + 1) as h:
                    self.spread(v, self.diag[0], self.L[:, bass.ds(h, 1), :].rearrange("p h j -> p (h j)")).then_inc(self.s_diagA, 1)
                    v.wait_ge(self.s_bcA, H0 + h + 1)
                    step.carry()
                    for j in range(NT):
                        step(v.tensor_tensor_reduce(self.junk, self.mask[:, j, 0:NP], psf[:, 0:NP], 1.0, NONE, ALU.add,
                                                    ALU.max, self.mh[:, j:j + 1]))
                        step.carry()
                    v.sem_inc(self.s_maxed, 1)
                    step(v.tensor_copy(self.M[:, bass.ds(h, 1), :].rearrange("p h j -> p (h j)"), self.mh))
                L, Rr, M, R1, R2, L2, y = (t[:, 0:HN, :] for t in self.full)
                step(v.tensor_scalar(y, M, 0.1 * NONE, -NONE, ALU.is_lt, ALU.mult))
                step(v.tensor_tensor(M, M, y, ALU.add))
                step(v.tensor_tensor(y, M, Rr, ALU.add))
                step(v.scalar_tensor_tensor(M, y, SLOPE, y, ALU.mult, ALU.max))
                step.count(v.tensor_tensor(R1, Rr, M, ALU.subtract))
                step.count(v.scalar_tensor_tensor(R2, Rr, SLOPE, M, ALU.mult, ALU.subtract))
                for t in self.after:
                    step.count(v.memset(t, 0.0))
                step(v.tensor_scalar(L2, L, SLOPE, None, ALU.mult))
                v.sem_inc(self.s_hr, 1)

                def spreads(h, k):
                    src = (self.R1, self.R2)[k][:, bass.ds(h, 1), :].rearrange("p h j -> p (h j)")
                    self.spread(v, self.diag[k], src).then_inc(self.s_diagC, 1)

                v.sem_inc(self.s_aggfree, 1)
                spreads(0, 0)
                spreads(0, 1)
                with step.loop(HN // 2, 2 * 3) as i:
                    def T(g):
                        hh, s = divmod(g, NT)
                        h = 2 * i + hh
                        if s == 0:
                            v.wait_ge(self.s_rb, 2 * (H0 + n + h + 1))
                        v.wait_ge(self.s_pr, NT * H0 + 2 * NT * i + g + 1)
                        v.wait_ge(self.s_t2r, NT * H0 + 2 * NT * i + g + 1)
                        l = self.L[:, bass.ds(h, 1), s:s + 1].rearrange("p h s -> p (h s)")
                        v.scalar_tensor_tensor(self.t[g % 2], self.R1b[hh], l, self.t2[g % 2], ALU.add, ALU.max)\
                         .then_inc(self.s_tr, 1)

                    def PP(g):
                        v.wait_ge(self.s_er, NT * H0 + 2 * NT * i + g + 1)
                        v.wait_ge(self.s_agg, NT * H0 + 2 * NT * i + g + 1)
                        v.scalar_tensor_tensor(self.p[g % 2], self.t[g % 2], 1.0, cnt3[:, g % NT, :], ALU.min, ALU.mult)\
                         .then_inc(self.s_pr, 1)

                    def evict(hh):
                        h = 2 * i + hh
                        v.wait_ge(self.s_agg, 2 + NT * (H0 + h + 1))
                        v.wait_ge(self.s_stored, 16 * (H0 + h))
                        acc = ps[:, 3:3 + self.banks, 0:self.tpb * (C + 1)].rearrange("p b (t c) -> p b t c", c=C + 1)
                        den = self.den.rearrange("p (b t) -> p b t", b=self.banks)
                        step(v.tensor_scalar(den, acc[:, :, :, C], TINY, None, ALU.add if HN == 4 else ALU.max))
                        step(v.reciprocal(self.den, self.den))
                        step(v.tensor_tensor(self.o.rearrange("p (b t c) -> p b t c", b=self.banks, c=C), acc[:, :, :, 0:C],
                                             den.unsqueeze(3).to_broadcast([P, self.banks, self.tpb, C]), ALU.mult))
                        v.sem_inc(self.s_out, 1)
                        v.sem_inc(self.s_aggfree, 1)

                    for g in range(2 * NT):
                        T(g)
                        if g:
                            PP(g - 1)
                        if g % NT == 0:
                            h1 = 2 * i + 1 if g < NT else 2 * i + 2
                            spreads(h1, 0)
                            spreads(h1, 1)
                        if g == NT:
                            evict(0)
                    PP(2 * NT - 1)
                    evict(1)

            def pe(self, pe, n):
                HN, C = self.HN, self.C
                H0 = HN * n
                if n == 0:
                    pe.sem_inc(self.s_agg, 2)

                def repeat_rows(k):
                    for n0 in range(0, NP, 512):
                        n1 = min(NP, n0 + 512)
                        last = pe.matmul(psf[:, n0:n1], ones[:, :], self.diag[k][:, n0:n1], start=True, stop=True)
                    return last

                with pe.Fori(0, HN) as h:
                    pe.wait_ge(self.s_diagA, H0 + h + 1)
                    repeat_rows(0).then_inc(self.s_bcA, 1)
                pe.wait_ge(self.s_maxed, H0 + HN)
                for k in range(2):
                    pe.wait_ge(self.s_diagC, 2 * (H0 + n) + k + 1)
                    if k:
                        pe.wait_ge(self.s_rb, 2 * (H0 + n) + 1)
                    repeat_rows(k).then_inc(self.s_bcC, 1)
                with pe.Fori(0, HN // 2) as i:
                    for g in range(2 * NT):
                        hh, s = divmod(g, NT)
                        h = 2 * i + hh
                        pe.wait_ge(self.s_pr, 2 + NT * H0 + 2 * NT * i + g + 1)
                        if s == 0:
                            pe.wait_ge(self.s_aggfree, H0 + n + h + 1)
                        hs = hbuf[:, bass.ds(h * (C + 1) + s * (D + HN), C + 1)]
                        for dt in range(NT):
                            b, t = divmod(dt, self.tpb)
                            last = pe.matmul(ps[:, 3 + b, t * (C + 1):(t + 1) * (C + 1)], self.p[g % 2][:, dt * P:(dt + 1) * P],
                                             hs, start=(s == 0 and t == 0), stop=(s == NT - 1), skip_group_check=True)
                        last.then_inc(self.s_agg, 1)
                        if s in (1, 3):
                            k = (s - 1) // 2
                            pe.wait_ge(self.s_diagC, 2 * (H0 + n + h + 1) + k + 1)
                            pe.wait_ge(self.s_rb, 2 * (H0 + n + h + 1) + k)
                            repeat_rows(k).then_inc(self.s_bcC, 1)

            def act(self, act, step, n):
                H0 = self.HN * n

                def rows_out(hh, k, head):
                    act.wait_ge(self.s_bcC, 2 * (H0 + n + head) + k + 1)
                    act.activation((self.R1b, self.R2b)[k][hh], psf[:, 0:NP], ACT.Copy).then_inc(self.s_rb, 1)

                act.wait_ge(self.s_hr, n + 1)
                rows_out(0, 0, 0)
                rows_out(0, 1, 0)
                with act.Fori(0, self.HN // 2) as i:
                    def T2(g):
                        hh, s = divmod(g, NT)
                        h = 2 * i + hh
                        if s == 0:
                            act.wait_ge(self.s_rb, 2 * (H0 + n + h + 1))
                        act.wait_ge(self.s_tr, NT * H0 + 2 * NT * i + g + 1)
                        b = self.L2[:, bass.ds(h, 1), s:s + 1].rearrange("p h s -> p (h s)")
                        act.activation(self.t2[g % 2], self.R2b[hh], ACT.Identity, bias=b).then_inc(self.s_t2r, 1)

                    def EX(g):
                        act.wait_ge(self.s_tr, 2 + NT * H0 + 2 * NT * i + g + 1)
                        act.activation(self.t[g % 2], self.t[g % 2], ACT.Exp).then_inc(self.s_er, 1)

                    for g in range(2 * NT):
                        T2(g)
                        if g:
                            EX(g - 1)
                        hh, s = divmod(g, NT)
                        if s in (4, 7):
                            k = (s - 4) // 3
                            rows_out(1 - hh, k, 2 * i + hh + 1)
                    EX(2 * NT - 1)

        att0 = Attention("gat", 4, mask1v, [(a[f"L0_gnn_a_src{l}"].rearrange("h c -> (h c)"), a[f"L0_gnn_a_dst{l}"].rearrange("h c -> (h c)"),
                                             gat_d[l], h_d[l]) for l in range(3)])

        def store_tiles(g, step, ready, slots, dst, stored, before=0):
            with g.Fori(0, NT // 2) as i:
                for u in range(2):
                    j = 2 * i + u
                    g.wait_ge(ready, before + j + 1)
                    step.carry()
                    g.dma_start(dst[bass.ds(j * P, P), :], slots[:, u, :]).then_inc(stored[u], 16)
            for u in range(2):
                g.wait_ge(stored[u], 8 * before + 16 * (NT // 2))

        def two(name):
            return [sem(f"{name}{u}") for u in range(2)]

        c4 = Carve(work, WORK)
        h4 = Carve(hbuf, NT * (D + 12))
        colb = h4(3 * KC)
        z4 = h4(2 * D).rearrange("p (u n) -> p u n", u=2)
        x4s = c4(2 * D).rearrange("p (u n) -> p u n", u=2)
        s_x4s, s_z4st = two("wout_x_in"), two("x1_stored")
        s_z4, s_colb = sem("x1_ready"), sem("gat_bias_in")
        w4 = c4(3 * KC * D).rearrange("p (c n) -> p c n", c=3 * KC)
        r4 = c4(6 * D).rearrange("p (u r n) -> p u r n", u=2, r=3)
        xt4 = h4(6 * D).rearrange("p (u c n) -> p u c n", u=2, c=3 * KC)
        W_OUT = Dense("wout", gat_d, [a["L0_gnn_W_out"][l * D:(l + 1) * D, :] for l in range(3)], w4, r4, xt4,
                      a["L0_gnn_b_out"], h4(D, parts=1), beside=(x0_d, x4s, s_x4s))
        norm1 = Norm()

        def sp_wout(sp):
            for l in range(3):
                sp.dma_start(colb[:, l * KC:(l + 1) * KC], a[f"L0_gnn_b{l}"].rearrange("(c p) -> p c", p=P),
                             allow_slow_non_contiguous=True).then_inc(s_colb, 16)
            W_OUT.load(sp)
            W_OUT.stream(sp)

        def act_wout(act):
            act.wait_ge(s_colb, 48)
            with act.Fori(0, NT // 2) as i:
                for u in range(2):
                    W_OUT.take(act, i, u, colb)
                for u in range(2):
                    norm1.scalar(act, 2 * i + u)

        def dve_wout(v, step):
            v.sem_inc(W_OUT.emptied, 2)
            with step.loop(NT // 2, 2 * (1 + Norm.VSTEPS)) as i:
                for u in range(2):
                    j = 2 * i + u
                    z = z4[:, u, :]
                    v.wait_ge(W_OUT.product, W_OUT.b["product"] + j + 3)
                    v.wait_ge(s_x4s[u], 16 * (i + 1))
                    v.wait_ge(s_z4st[u], 16 * i)
                    step(v.scalar_tensor_tensor(halves(z), W_OUT.psum(u), 0.0, halves(x4s[:, u, :]), ALU.max, ALU.add))
                    v.sem_inc(W_OUT.emptied, 1)
                    norm1.vector(v, step, z, j)
                    v.sem_inc(s_z4, 1)

        conv_sems = {n: sem("conv_" + n) for n in ("b_in", "g", "cols", "agg", "emptied", "ready")}
        conv_sems.update(x_in=two("conv_x_in"), stored=two("conv_stored"))

        class Convolution:
            def __init__(self, turn, rows, weight, bias, x_dram, out_dram):
                self.bias, self.out_dram, self.n = bias, out_dram, turn
                cv = Carve(work, WORK)
                self.dense = Dense("conv", [rows], [weight], cv(KC * D).rearrange("p (c n) -> p c n", c=KC),
                                   cv(2 * D).rearrange("p (u r n) -> p u r n", u=2, r=1),
                                   cv(2 * D).rearrange("p (u c n) -> p u c n", u=2, c=KC))
                self.col = [cv(NP).rearrange("p (s n) -> p s n", s=NT) for _ in range(2)]
                self.brow = cv(D)
                self.xs = cv(2 * D).rearrange("p (u n) -> p u n", u=2)
                self.z = cv(2 * D).rearrange("p (u n) -> p u n", u=2)
                self.x_dram = x_dram
                self.x_in, self.stored = conv_sems["x_in"], conv_sems["stored"]
                self.s_b_in, self.s_g, self.s_cols, self.s_ready = (conv_sems[n] for n in ("b_in", "g", "cols", "ready"))
                self.s_agg, self.s_emptied = conv_sems["agg"], conv_sems["emptied"]
                self.at = turn * NT
                self.at2 = turn * (NT + 2)
                self.norm = Norm()
                self.gv = hbuf[:, 0:NT * D].rearrange("p (j n) -> p j n", j=NT)

            def sp(self, sp):
                self.dense.load(sp)
                self.dense.stream(sp)
                sp.dma_start(self.brow, self.bias.partition_broadcast(P)).then_inc(self.s_b_in, 16)
                with sp.Fori(0, NT // 2) as i:
                    for u in range(2):
                        j = 2 * i + u
                        sp.wait_ge(self.s_emptied, self.at2 + j + 1)
                        sp.dma_start(self.xs[:, u, :], self.x_dram[bass.ds(j * P, P), :]).then_inc(self.x_in[u], 16)

            def act(self, act, step):
                d = self.dense
                with step.loop(NT // 2, 2) as i:
                    d.take(act, i, 0)
                    d.take(act, i, 1)
                    for u in range(2):
                        j = 2 * i + u
                        act.wait_ge(d.product, d.b["product"] + j + 3)
                        step(act.activation(halves(hbuf[:, bass.ds(j * D, D)]), d.psum(u), ACT.Copy, scale=dinv[:, bass.ds(j, 1)]))
                        act.sem_inc(d.emptied, 1)
                act.sem_inc(self.s_g, 1)
                with act.Fori(0, NT // 2) as i:
                    for u in range(2):
                        j = 2 * i + u
                        act.wait_ge(self.s_agg, self.at2 + j + 1)
                        act.activation(self.col[u], cnt3[:, :, bass.ds(j * P, P)], ACT.Copy).then_inc(self.s_cols, 1)
                    for u in range(2):
                        self.norm.scalar(act, 2 * i + u)

            def pe(self, pe):
                self.dense.multiply(pe)
                pe.sem_inc(self.s_agg, 2)
                pe.wait_ge(self.s_g, self.n + 1)
                with pe.Fori(0, NT // 2) as i:
                    for u in range(2):
                        j = 2 * i + u
                        pe.wait_ge(self.s_cols, self.at + j + 1)
                        pe.wait_ge(self.s_emptied, self.at2 + j + 1)
                        for h in range(2):
                            for s in range(NT):
                                last = pe.matmul(ps[:, 2 * u + h, 0:HALF], self.col[u][:, s, :],
                                                 self.gv[:, s, h * HALF:(h + 1) * HALF], start=(s == 0), stop=(s == NT - 1))
                        last.then_inc(self.s_agg, 1)

            def dve(self, v, step):
                v.sem_inc(self.dense.emptied, 2)
                v.sem_inc(self.s_emptied, 2)
                v.wait_ge(self.s_b_in, 16 * (self.n + 1))
                with step.loop(NT // 2, 2 * (2 + Norm.VSTEPS)) as i:
                    for u in range(2):
                        j = 2 * i + u
                        z = self.z[:, u, :]
                        v.wait_ge(self.s_agg, self.at2 + j + 3)
                        v.wait_ge(self.stored[u], 8 * self.at + 16 * i)
                        step(v.scalar_tensor_tensor(halves(z), ps[:, 2 * u:2 * u + 2, 0:HALF], dinv[:, bass.ds(j, 1)],
                                                    halves(self.brow), ALU.mult, ALU.add))
                        v.wait_ge(self.x_in[u], 8 * self.at + 16 * (i + 1))
                        step(v.tensor_tensor(z, z, self.xs[:, u, :], ALU.add))
                        v.sem_inc(self.s_emptied, 1)
                        self.norm.vector(v, step, z, j)
                        v.sem_inc(self.s_ready, 1)

            def pool(self, g, step):
                store_tiles(g, step, self.s_ready, self.z, self.out_dram, self.stored, self.at)

        conv1 = Convolution(0, x1_d, a["L1_gnn_W"], a["L1_gnn_b"], x1_d, x2_d)

        c5 = Carve(work, WORK)
        wbd = c5(2 * P)
        rows5 = c5(2 * D).rearrange("p (u n) -> p u n", u=2)
        xt5 = c5(2 * D).rearrange("p (u c n) -> p u c n", u=2, c=KC)
        res5 = c5(2 * D).rearrange("p (u n) -> p u n", u=2)
        s_w5, s_w5z, s_ones5 = sem("wbd_in"), sem("wbd_zero"), sem("ones5")
        s_rows5, s_res5 = two("rows5_in"), two("res_stored")
        s_turn5, s_take5, s_prod5, s_free5 = sem("turned5"), sem("taken5"), sem("product5"), sem("free5")
        ft = hbuf[:, 0:NT * (D + 12)].rearrange("p (j n) -> p j n", j=NT)

        def pool_heads(g, step):
            step(g.memset(wbd, 0.0))
            g.sem_inc(s_w5z, 1)
            step(g.memset(hbuf[:, 0:NT * (D + 12)], 1.0))
            g.sem_inc(s_ones5, 1)

        def sp_heads(sp):
            sp.wait_ge(s_w5z, 1)
            for q in range(2):
                for k, w in ((0, a["L2_gnn_W"]), (1, a["L2_gnn_W_res"])):
                    sp.dma_start(wbd[64 * q:64 * q + 64, k * P + 64 * q:k * P + 64 * q + 64], w).then_inc(s_w5, 16)
            with sp.Fori(0, NT // 2) as i:
                for u in range(2):
                    j = 2 * i + u
                    sp.wait_ge(s_turn5, j + 1)
                    sp.dma_start(rows5[:, u, :], x2_d[bass.ds(j * P, P), :]).then_inc(s_rows5[u], 16)

        def pe_heads(pe):
            pe.sem_inc(s_turn5, 2)
            pe.sem_inc(s_prod5, 2)
            pe.sem_inc(s_free5, 2)
            pe.wait_ge(s_w5, 64)
            with pe.Fori(0, NT // 2) as i:
                for u in range(2):
                    pe.wait_ge(s_rows5[u], 16 * (i + 1))
                    for c in range(KC):
                        last = pe.transpose(ps[:, 2 * u + c // 3, (c % 3) * P:(c % 3 + 1) * P], rows5[:, u, c * P:(c + 1) * P], ident[:, :])
                    last.then_inc(s_turn5, 1)
                for u in range(2):
                    pe.wait_ge(s_take5, 2 * i + u + 1)
                    for hf in range(2):
                        pe.wait_ge(s_free5, 2 * (2 * i + u) + hf + 1)
                        for c in range(3):
                            last = pe.matmul(ps[:, 4 + 2 * hf + c // 2, (c % 2) * 2 * P:(c % 2 + 1) * 2 * P],
                                             xt5[:, u, 3 * hf + c, :], wbd, start=True, stop=True)
                        last.then_inc(s_prod5, 1)

        def act_heads(act, step):
            act.wait_ge(s_ones5, 1)
            with step.loop(NT // 2, 4) as i:
                for u in range(2):
                    j = 2 * i + u
                    act.wait_ge(s_turn5, j + 3)
                    act.wait_ge(s_prod5, 2 * j + 1)
                    act.activation(xt5[:, u].rearrange("p (a b) n -> p a (b n)", a=2), ps[:, 2 * u:2 * u + 2, 0:HALF], ACT.Copy)\
                       .then_inc(s_take5, 1)
                for u in range(2):
                    j = 2 * i + u
                    act.wait_ge(s_res5[u], 16 * i)
                    for hf in range(2):
                        act.wait_ge(s_prod5, 2 * j + hf + 3)
                        for b, n in ((0, 2), (1, 1)):
                            blocks = ps[:, 4 + 2 * hf + b, 0:n * 2 * P].rearrange("p (c k m) -> p c k m", k=2, m=P)
                            head = 6 * hf + 4 * b
                            act.activation(hbuf[:, bass.ds(j * (D + 12) + head * 65, 65 * 2 * n)].rearrange("p (c h m) -> p c h m", h=2, m=65)[:, :, :, 0:64],
                                           blocks[:, :, 0, :].rearrange("p c (h m) -> p c h m", h=2), ACT.Copy)
                            ins = act.activation(res5[:, u, head * 64:head * 64 + n * P].rearrange("p (c m) -> p c m", m=P),
                                                 blocks[:, :, 1, :], ACT.Copy)
                        step(ins)
                        act.sem_inc(s_free5, 1)
                    act.dma_start(res_d[bass.ds(j * P, P), :], res5[:, u, :]).then_inc(s_res5[u], 16)
            for u in range(2):
                act.wait_ge(s_res5[u], 16 * (NT // 2))

        att2 = Attention("attb", 12, mask2v, [(a["L2_gnn_attn_l"].rearrange("o h c -> (o h c)"),
                                               a["L2_gnn_attn_r"].rearrange("o h c -> (o h c)"), agg2_d, None)])

        def self_loops(v, step, op):
            for j in range(NT):
                blk = cnt3[:, j, j * P:(j + 1) * P]
                step.count(v.tensor_tensor(blk, blk, ident[:, :], op))
            step.wait()

        c6 = Carve(work, WORK)
        in6 = [c6(2 * D).rearrange("p (u n) -> p u n", u=2) for _ in range(3)]
        s_in6, s_st6 = two("x3_parts_in"), two("x3_stored")
        s_free6, s_ready6 = sem("x3_free"), sem("x3_ready")
        norm6 = Norm()

        def sp_join(sp):
            with sp.Fori(0, NT // 2) as i:
                for u in range(2):
                    j = 2 * i + u
                    sp.wait_ge(s_st6[u], 16 * i)
                    for t, src in zip(in6, (agg2_d, res_d, x2_d)):
                        sp.dma_start(t[:, u, :], src[bass.ds(j * P, P), :]).then_inc(s_in6[u], 16)

        def act_join(act):
            with act.Fori(0, NT) as j:
                norm6.scalar(act, j)

        def dve_join(v, step):
            with step.loop(NT // 2, 2 * (2 + Norm.VSTEPS)) as i:
                for u in range(2):
                    z = in6[0][:, u, :]
                    v.wait_ge(s_in6[u], 48 * (i + 1))
                    step(v.tensor_tensor(z, z, in6[1][:, u, :], ALU.add))
                    step(v.scalar_tensor_tensor(z, z, 0.0, in6[2][:, u, :], ALU.max, ALU.add))
                    norm6.vector(v, step, z, 2 * i + u)
                    v.sem_inc(s_ready6, 1)

        whi7, wlo7 = wsplit[:, 0:2 * KC * D], wsplit[:, 2 * KC * D:4 * KC * D]
        GW = 4
        c7 = Carve(ct[:, :].bitcast(F32), NT * CW // 2)
        rows7 = c7(GW * D).rearrange("p (u r n) -> p u r n", u=GW, r=1)
        brow7 = c7(D, parts=1)
        idx7 = c7(2 * GW, I32).rearrange("p (u c) -> p u c", c=2)
        iv7 = c7(GW)
        invs7 = c7(RT)
        xt7 = xplain[:, 0:2 * D].rearrange("p (u c n) -> p u c n", u=2, c=KC)
        msg7 = xplain[:, 2 * D:4 * D].rearrange("p (u n) -> p u n", u=2)
        xhi7, xlo7 = (xsplit[:, k * 2 * D:(k + 1) * 2 * D].rearrange("p (u n) -> p u n", u=2) for k in range(2))
        W_ROOT = Dense("root", [x3_d], [a["L3_gnn_W_root"]], wplain[:, :].rearrange("p (c n) -> p c n", c=KC),
                       rows7, xt7, a["L3_gnn_b_rgcn"], brow7)
        conv3 = Convolution(1, h1_d, a["L3_gnn_W_gcn"], a["L3_gnn_b_gcn"], x3_d, x4_d)
        s_wrel, s_msgst = sem("wrel_in"), two("messages_stored")
        s_gath = [sem(f"rows_gathered{u}") for u in range(GW)]
        s_turn7, s_take7, s_prod7, s_emp7, s_lo7 = (sem(n) for n in ("turned7", "taken7", "product7", "emptied7", "low_parts7"))
        s_split7 = sem("weights_split7")
        s_rootout = sem("root_out")

        def sp_rel(sp):
            W_ROOT.load(sp)
            W_ROOT.stream(sp)
            sp.wait_ge(W_ROOT.product, W_ROOT.all_products)
            with sp.Fori(0, R) as r:
                sp.wait_ge(s_split7, r + 1)
                sp.dma_start(wplain[:, :].rearrange("p (c n) -> p c n", c=KC),
                             a["L3_gnn_W_rel"].rearrange("r (c p) n -> r p c n", p=P)[bass.ds(r, 1)].rearrange("r p c n -> (r p) c n"))\
                  .then_inc(s_wrel, 16)

        def dve_rel(v, step):
            v.sem_inc(W_ROOT.emptied, 2)
            v.sem_inc(s_split7, 1)
            with step.loop(R // 2, 4) as i:
                for u in range(2):
                    r = 2 * i + u
                    lo, hi = (w[:, u * KC * D:(u + 1) * KC * D] for w in (wlo7, whi7))
                    last = v.value_load(end_rel[0:1, bass.ds(r, 1)], min_val=0, max_val=RT)
                    v.wait_ge(s_wrel, 16 * (r + 1))
                    v.wait_ge(s_prod7, last + 2)
                    step(v.tensor_copy(hi, wplain[:, :]))
                    step(v.tensor_tensor(lo, wplain[:, :], hi.bitcast(F32), ALU.subtract))
                    v.sem_inc(s_split7, 1)

        def pool_rel(g, step):
            def gather(k, u, n):
                if n is not None:
                    g.wait_ge(s_turn7, k - GW + 3)
                    g.wait_ge(s_gath[u], n)
                step(g.tensor_copy(idx7[:, u, :], relrec[:, bass.ds(2 * k, 2)]))
                step.carry()
                g.indirect_dma_start(out=rows7[:, u, 0, :], out_offset=None, in_=x3_d,
                                     in_offset=bass.IndirectOffsetOnAxis(idx7[:, u, 0:1], 0)).then_inc(s_gath[u], 16)
                g.indirect_dma_start(out=iv7[:, u:u + 1], out_offset=None, in_=inv_d,
                                     in_offset=bass.IndirectOffsetOnAxis(idx7[:, u, 1:2], 0)).then_inc(s_gath[u], 16)

            def low(k, u, way, gathers):
                g.wait_ge(s_gath[way], 32 * gathers)
                step(g.tensor_copy(invs7[:, bass.ds(k, 1)], iv7[:, way:way + 1]))
                g.wait_ge(s_take7, k + 1)
                g.wait_ge(s_prod7, k + 1)
                step(g.tensor_tensor(xlo7[:, u, :], xt7[:, u].rearrange("p c n -> p (c n)"), xhi7[:, u, :].bitcast(F32), ALU.subtract))
                g.sem_inc(s_lo7, 1)

            g.sem_inc(s_lo7, 2)
            g.wait_ge(W_ROOT.turned, W_ROOT.all_turned)
            for u in range(GW):
                gather(u, u, None)
            low(0, 0, 0, 1)
            with step.loop(RT // GW, 3 * GW) as i:
                for u in range(GW):
                    k = GW * i + u
                    gather(k + GW, u, 32 * (i + 1))
                    low(k + 1, (u + 1) % 2, (u + 1) % GW, i + 1 + (u + 1) // GW)
            for k in range(RT // GW * GW, RT - 1):
                low(k + 1, (k + 1) % 2, (k + 1) % GW, (k + 1) // GW + 1)
            for u in range(GW):
                g.wait_ge(s_gath[u], 32 * (RT // GW + 1))

        def pe_rel(pe):
            W_ROOT.multiply(pe)
            pe.wait_ge(s_rootout, 1)
            pe.sem_inc(s_turn7, 2)
            pe.sem_inc(s_prod7, 2)

            def turn(u, gathers):
                pe.wait_ge(s_gath[u], 32 * gathers)
                for c in range(KC):
                    last = pe.transpose(ps[:, 2 * (u % 2) + c // 3, (c % 3) * P:(c % 3 + 1) * P], rows7[:, u, 0, c * P:(c + 1) * P], ident[:, :])
                last.then_inc(s_turn7, 1)

            def messages(k, u):
                r = pe.value_load(tile_rel[0:1, bass.ds(k, 1)], min_val=0, max_val=R - 1)
                pe.wait_ge(s_split7, r + 2)
                base = (r % 2) * (KC * D)
                pe.wait_ge(s_take7, k + 1)
                pe.wait_ge(s_lo7, k + 3)
                pe.wait_ge(s_emp7, k + 1)
                for h in range(2):
                    for q, (x, w) in enumerate(((xhi7, whi7), (xhi7, wlo7), (xlo7, whi7))):
                        for c in range(KC):
                            last = pe.matmul(ps[:, 4 + 2 * u + h, 0:HALF], x[:, u, c * P:(c + 1) * P],
                                             w[:, bass.ds(base + (c * D + h * HALF), HALF)],
                                             start=(q == 0 and c == 0), stop=(q == 2 and c == KC - 1))
                last.then_inc(s_prod7, 1)

            turn(0, 1)
            with pe.Fori(0, RT // GW) as i:
                for u in range(GW):
                    turn((u + 1) % GW, i + 1 + (u + 1) // GW)
                    messages(GW * i + u, u % 2)
            for k in range(RT // GW * GW, RT):
                if k + 1 < RT:
                    turn((k + 1) % GW, (k + 1) // GW + 1)
                messages(k, k % 2)

        def act_rel(act, step):
            with step.loop(NT // 2, 2) as i:
                W_ROOT.take(act, i, 0)
                W_ROOT.take(act, i, 1)
                for u in range(2):
                    j = 2 * i + u
                    act.wait_ge(W_ROOT.product, W_ROOT.b["product"] + j + 3)
                    step(act.activation(halves(hbuf[:, bass.ds(j * D, D)]), W_ROOT.psum(u), ACT.Copy))
                    act.sem_inc(W_ROOT.emptied, 1)
            act.sem_inc(s_rootout, 1)

            def take(k, u):
                act.wait_ge(s_turn7, k + 3)
                act.wait_ge(s_lo7, k + 1)
                act.wait_ge(s_prod7, k + 1)
                step.count(act.activation(xt7[:, u].rearrange("p (a b) n -> p a (b n)", a=2), ps[:, 2 * u:2 * u + 2, 0:HALF], ACT.Copy))
                step(act.activation(halves(xhi7[:, u, :]), ps[:, 2 * u:2 * u + 2, 0:HALF], ACT.Copy))
                act.sem_inc(s_take7, 1)

            def store(k, u, i):
                act.wait_ge(s_prod7, k + 3)
                act.wait_ge(s_msgst[u], 16 * (i + 1))
                step(act.activation(halves(msg7[:, u, :]), ps[:, 4 + 2 * u:6 + 2 * u, 0:HALF], ACT.Copy,
                                    scale=invs7[:, bass.ds(k, 1)]))
                act.sem_inc(s_emp7, 1)
                act.dma_start(msg_d[bass.ds(k * P, P), :], msg7[:, u, :]).then_inc(s_msgst[u], 16)

            act.sem_inc(s_emp7, 2)
            for u in range(2):
                act.sem_inc(s_msgst[u], 16)
            take(0, 0)
            with step.loop(RT // 2 - 1, 6) as i:
                for u in range(2):
                    take(2 * i + u + 1, 1 - u)
                    store(2 * i + u, u, i)
            take(RT - 1, 1)
            store(RT - 2, 0, RT // 2 - 1)
            store(RT - 1, 1, RT // 2 - 1)
            for u in range(2):
                act.wait_ge(s_msgst[u], 16 * (RT // 2 + 1))

        c8 = Carve(work, WORK)
        mg8 = c8(2 * GT * D).rearrange("p (u n) -> p u n", u=2 * GT)
        sel8 = c8(2 * GT * P).rearrange("p (u n) -> p u n", u=2 * GT)
        idx8 = c8(2 * GT, I32)
        rows8 = c8(BT, I32)
        s_g8 = [sem(f"messages_in{u}") for u in range(2 * GT)]
        s_idx8, s_sel8, s_sum8, s_add8, s_h1 = (sem(n) for n in ("indices8", "selected8", "summed8", "added8", "h1_stored"))

        def pool_sum(g, step):
            def group(k, u, first=False):
                for w in range(GT):
                    way = GT * u + w
                    if not first:
                        g.wait_ge(s_sum8, k + 1)
                        g.wait_ge(s_g8[way], 16 * (k // 2))
                    step(g.tensor_copy(idx8[:, way:way + 1], rows8[:, bass.ds(GT * k + w, 1)]))
                    step.carry()
                    g.indirect_dma_start(out=mg8[:, way, :], out_offset=None, in_=msg_d,
                                         in_offset=bass.IndirectOffsetOnAxis(idx8[:, way:way + 1], 0)).then_inc(s_g8[way], 16)

            g.wait_ge(s_idx8, 1)
            for u in range(2):
                group(u, u, True)
            with step.loop(BG // 2 - 1, 2 * GT) as i:
                for u in range(2):
                    group(2 * (i + 1) + u, u)
            if BG % 2:
                group(BG - 1, 0)

        def pe_sum(pe):
            def group(k, u):
                pe.wait_ge(s_sel8, k + 1)
                pe.wait_ge(s_add8, k + 1)
                for w in range(GT):
                    way = GT * u + w
                    pe.wait_ge(s_g8[way], 16 * (k // 2 + 1))
                    for h in range(2):
                        last = pe.matmul(ps[:, 2 * u + h, 0:HALF], sel8[:, way, :], mg8[:, way, h * HALF:(h + 1) * HALF],
                                         start=(w == 0), stop=(w == GT - 1))
                last.then_inc(s_sum8, 1)

            pe.sem_inc(s_sum8, 2)
            group_loop(lambda n: pe.Fori(0, n), group)

        def dve_sum(v, step):
            step(v.tensor_copy(rows8, drec3[:, :, 3]))
            v.sem_inc(s_idx8, 1)
            v.sem_inc(s_add8, 2)

            def select(k, u):
                v.wait_ge(s_sum8, k + 1)
                for w in range(GT):
                    dr = drec3[:, bass.ds(GT * k + w, 1), 1:2].rearrange("p k c -> p (k c)")
                    step.count(v.tensor_scalar(sel8[:, GT * u + w, :], iota[:, 0:P], dr, None, ALU.is_equal))
                step.wait()
                v.sem_inc(s_sel8, 1)

            def add(k, u):
                b = v.value_load(group_dst[0:1, bass.ds(k, 1)], min_val=0, max_val=NT - 1)
                v.wait_ge(s_sum8, k + 3)
                t = halves(hbuf[:, bass.ds(b * D, D)])
                step(v.tensor_tensor(t, ps[:, 2 * u:2 * u + 2, 0:HALF], t, ALU.add))
                v.sem_inc(s_add8, 1)

            select(0, 0)
            with step.loop((BG - 1) // 2, 2 * (GT + 1)) as i:
                for u in range(2):
                    select(2 * i + u + 1, 1 - u)
                    add(2 * i + u, u)
            for k in range((BG - 1) // 2 * 2, BG):
                if k + 1 < BG:
                    select(k + 1, (k + 1) % 2)
                add(k, k % 2)

        def sp_h1(sp):
            sp.dma_start(h1_d.rearrange("(j p) n -> p j n", p=P), hbuf[:, 0:NT * D].rearrange("p (j n) -> p j n", j=NT)).then_inc(s_h1, 16)
            sp.wait_ge(s_h1, 16)

        s_out = sem("out_stored")

        block = ctx.enter_context(nc.Block())

        @block.sync
        def _(sp):
            sp_phase1(sp)
            meet(sp)
            meet(sp)
            sp.wait_ge(s_inv, 1)
            sp.dma_start(inv_d.rearrange("(j p r) c -> p j (r c)", p=P, r=R), inv).then_inc(s_invd, 16)
            sp.wait_ge(s_invd, 16)
            meet(sp)
            for l in range(3):
                att0.sp(sp, l)
                meet(sp)
            sp_wout(sp)
            meet(sp)
            conv1.sp(sp)
            meet(sp)
            sp_heads(sp)
            meet(sp)
            att2.sp(sp, 0)
            meet(sp)
            sp_join(sp)
            meet(sp)
            sp_rel(sp)
            meet(sp)
            meet(sp)
            sp_h1(sp)
            meet(sp)
            conv3.sp(sp)
            meet(sp)
            sp.dma_start(out, x4_d[0:N, :]).then_inc(s_out, 16)
            sp.wait_ge(s_out, 16)

        @block.tensor
        def _(pe):
            pe_phase1(pe)
            meet(pe)
            pe_phase2(pe)
            meet(pe)
            pe_phase3(pe)
            meet(pe)
            for l in range(3):
                att0.pe(pe, l)
                meet(pe)
            W_OUT.multiply(pe)
            meet(pe)
            conv1.pe(pe)
            meet(pe)
            pe_heads(pe)
            meet(pe)
            att2.pe(pe, 0)
            meet(pe)
            meet(pe)
            pe_rel(pe)
            meet(pe)
            pe_sum(pe)
            meet(pe)
            meet(pe)
            conv3.pe(pe)
            meet(pe)

        @block.scalar
        def _(act):
            step = Steps(act, act_step)
            act_phase1(act, step)
            meet(act)
            meet(act)
            act.wait_ge(s_deg, 1)
            act.activation(dinv[:, :], deg, ACT.Sqrt).then_inc(s_root, 1)
            meet(act)
            for l in range(3):
                att0.act(act, step, l)
                meet(act)
            act_wout(act)
            meet(act)
            conv1.act(act, step)
            meet(act)
            act_heads(act, step)
            meet(act)
            att2.act(act, step, 0)
            meet(act)
            act_join(act)
            meet(act)
            act_rel(act, step)
            meet(act)
            meet(act)
            meet(act)
            conv3.act(act, step)
            meet(act)

        @block.vector
        def _(v):
            step = Steps(v, dve_step, dve_carrier)
            dve_phase1(v, step)
            meet(v)
            dve_phase2(v, step)
            meet(v)
            dve_phase3(v, step)
            meet(v)
            for l in range(3):
                att0.dve(v, step, l)
                meet(v)
            dve_wout(v, step)
            meet(v)
            conv1.dve(v, step)
            meet(v)
            self_loops(v, step, ALU.subtract)
            meet(v)
            att2.dve(v, step, 0)
            meet(v)
            self_loops(v, step, ALU.add)
            dve_join(v, step)
            meet(v)
            dve_rel(v, step)
            meet(v)
            dve_sum(v, step)
            meet(v)
            meet(v)
            conv3.dve(v, step)
            meet(v)

        @block.gpsimd
        def _(g):
            step = Steps(g, pool_step, pool_carrier)
            pool_phase1(g, step)
            meet(g)
            pool_phase2(g, step)
            for _ in range(5):
                meet(g)
            store_tiles(g, step, s_z4, z4, x1_d, s_z4st)
            meet(g)
            conv1.pool(g, step)
            meet(g)
            pool_heads(g, step)
            meet(g)
            meet(g)
            store_tiles(g, step, s_ready6, in6[0], x3_d, s_st6)
            meet(g)
            pool_rel(g, step)
            meet(g)
            pool_sum(g, step)
            meet(g)
            meet(g)
            conv3.pool(g, step)
            meet(g)


_OUTS = [((N, D), "float32")]


def kernel(**inputs):
    import numpy as _np
    import concourse.bacc as _bacc
    from concourse import mybir as _mybir
    from concourse.bass_utils import run_bass_kernel_spmd as _run

    nc = _bacc.Bacc("TRN2", target_bir_lowering=False, num_devices=1)
    arrays, args = {}, {}
    for name, value in inputs.items():
        if name == "edge_weight1":
            continue
        v = _np.ascontiguousarray(value)
        if name in ("L2_gnn_W", "L2_gnn_W_res"):
            v = _np.ascontiguousarray(v.T)
        arrays[f"in_{name}"] = v
        args[name] = nc.dram_tensor(f"in_{name}", v.shape, _mybir.dt.from_np(v.dtype), kind="ExternalInput").ap()
    o = nc.dram_tensor("out_0", (N, D), _mybir.dt.float32, kind="ExternalOutput").ap()
    build(nc, args, o)
    r = _run(nc, [arrays], core_ids=[0])
    return r.results[0]["out_0"]
```

```python
from contextlib import ExitStack, contextmanager

import concourse.bass as bass
from concourse import mybir

F32 = mybir.dt.float32
F32R = mybir.dt.float32r
BF16 = mybir.dt.bfloat16
I32 = mybir.dt.int32
U16 = mybir.dt.uint16
ALU = mybir.AluOpType
ACT = mybir.ActivationFunctionType
AX = mybir.AxisListType.X

P = 128
N = 1250
NT = (N + P - 1) // P
NP = NT * P
D = 768
KC = D // P
HALF = D // 2
E = 20000
EP, ET = 125, 160
R = 34
RT = (E + R * (P - 1)) // P + 1
GT = 4
BG = (E + NT * (GT * P - 1)) // (GT * P)
BT = BG * GT
CW = NP + R
REC = 4
NONE = -1.0e30
SLOPE = 0.2
EPS_LN = 1e-5
TINY = 1e-16
WORK = 5 * KC * D
WAYS = 8


class Steps:

    def __init__(self, eng, sem, carrier=None):
        self.eng, self.sem, self.base, self.k, self.carrier = eng, sem, 0, 0, carrier

    def __call__(self, ins):
        ins.then_inc(self.sem, 1)
        self.k += 1
        self.eng.wait_ge(self.sem, self.base + self.k)

    def count(self, ins):
        ins.then_inc(self.sem, 1)
        self.k += 1

    def wait(self):
        self.eng.wait_ge(self.sem, self.base + self.k)

    def carry(self):
        self.eng.sem_inc(self.carrier, 1)

    @contextmanager
    def loop(self, times, per):
        start = self.base + self.k
        with self.eng.Fori(0, times) as i:
            self.base, self.k = start + i * per, 0
            yield i
            assert self.k == per, (self.k, per)
        self.base, self.k = start + times * per, 0


def build(nc, a, out):
    ctx = ExitStack()
    with ctx:
        def sb(name, shape, dt=F32):
            return ctx.enter_context(nc.sbuf_tensor(name, shape, dt))

        def sem(name):
            return ctx.enter_context(nc.semaphore(name))

        def dram(name, shape, dt=F32):
            return nc.dram_tensor(name, shape, dt, kind="Internal").ap()

        xa_d = dram("xa_d", (NP, D))
        h_d = [dram(f"feat{l}_d", (NP, D + 4)) for l in range(3)]
        gat_d = [dram(f"gat{l}_d", (NP, D)) for l in range(3)]
        x1_d = dram("x1_d", (NP, D))
        x2_d = dram("x2_d", (NP, D))
        res_d = dram("res_d", (NP, D))
        agg2_d = dram("agg2_d", (NP, D))
        x3_d = dram("x3_d", (NP, D))
        h1_d = dram("h1_d", (NP, D))
        msg_d = dram("msg_d", (RT * P, D))
        relrec_d = dram("relrec_d", (P * RT, 2), I32)
        dstrec_d = dram("dstrec_d", (P * BT, REC))
        inv_d = dram("inv_d", (NP * R, 1))

        cnt = sb("cnt", [P, NT * NP], U16)
        ct = sb("ct", [P, NT * CW], U16)
        ident = sb("ident", [P, P])
        ones = sb("ones", [P, P])
        tri = sb("tri", [P, P])
        iota = sb("iota", [P, NP], U16)
        relrec = sb("relrec", [P, (RT + 2) * 2], I32)
        drec = sb("drec", [P, BT * REC])
        tile_rel = sb("tile_rel", [1, RT], I32)
        group_dst = sb("group_dst", [1, BG], I32)
        end_rel = sb("end_rel", [1, R + 2], I32)
        dinv = sb("dinv", [P, NT])
        small = sb("small", [P, 64])
        lr = sb("lr", [P, 240])
        with nc.sbuf_tensor("mask1", [P, NT * NP], BF16) as mask1, nc.sbuf_tensor("work", [P, WORK], F32) as work, \
             nc.sbuf_tensor("hbuf", [P, NT * (D + 12)], F32) as hbuf:
            pass
        xsplit = sb("xsplit", [P, 4 * D], F32R)
        xplain = sb("xplain", [P, NT * NP // 2 - 4 * D])
        wsplit = sb("wsplit", [P, 4 * KC * D], F32R)
        wplain = sb("wplain", [P, KC * D])
        hsplit = sb("hsplit", [P, NT * (D + 12)], F32R)
        ps = ctx.enter_context(nc.psum_tensor("ps", [P, 8, 512], F32))
        psf = ps[:, :, :].rearrange("p b n -> p (b n)")

        cnt3 = cnt[:, :].rearrange("p (j n) -> p j n", j=NT)
        mask1v = mask1[:, :].rearrange("p (j n) -> p j n", j=NT)
        ct3 = ct[:, :].rearrange("p (j n) -> p j n", j=NT)
        mask2v = ct[:, :].bitcast(BF16).rearrange("p (j n) -> p j n", j=NT)
        drec3 = drec[:, :].rearrange("p (k c) -> p k c", c=REC)

        class Carve:

            def __init__(self, region, size):
                self.region, self.size, self.at = region, size, 0

            def __call__(self, n, dt=F32, parts=P):
                w = n if dt in (F32, I32) else (n + 1) // 2
                v = self.region[0:parts, self.at:self.at + w]
                self.at += w
                assert self.at <= self.size, self.at
                return v if dt is F32 else v.bitcast(dt)

        def tile_rows(j):
            return N - j * P if isinstance(j, int) and j == NT - 1 else P

        def halves(v):
            return v.rearrange("p (a n) -> p a n", a=2)

        met = sem("met")
        meetings = {}

        def meet(eng):
            meetings[eng] = meetings.get(eng, 0) + 1
            eng.drain().then_inc(met, 1)
            eng.wait_ge(met, 5 * meetings[eng])

        dve_step, act_step, pool_step = sem("dve_step"), sem("act_step"), sem("pool_step")
        dve_carrier, pool_carrier = sem("dve_carrier"), sem("pool_carrier")

        dense_sems = {n: sem("dense_" + n) for n in ("w_in0", "w_in1", "turned", "taken", "product", "emptied")}
        dense_sems["rows_in"] = [sem(f"dense_rows_in{u}") for u in range(2)]
        dense_counts = {n: 0 for n in [*dense_sems, "stages"]}

        class Dense:

            def __init__(self, name, rows, weights, w_at, rows_at, xt_at, bias=None, bias_at=None, beside=None, split=None):
                self.split = split
                self.beside = beside
                self.rows, self.w, self.K = rows, weights, len(rows)
                self.w_at, self.rows_at, self.xt_at = w_at, rows_at, xt_at
                self.bias, self.bias_at = bias, bias_at
                self.pick = f"w_in{dense_counts['stages'] % 2}"
                dense_counts["stages"] += 1
                self.w_in, self.rows_in = dense_sems[self.pick], dense_sems["rows_in"]
                self.turned = dense_sems["turned"]
                self.taken = dense_sems["taken"]
                self.product = dense_sems["product"]
                self.emptied = dense_sems["emptied"]
                K, nw = self.K, 16 * (self.K + (bias is not None))
                self.b = dict(dense_counts)
                for key, more in ((self.pick, nw), ("rows_in", 16 * K * (NT // 2)), ("turned", K * (NT + 2)), ("taken", K * NT),
                                  ("product", NT + 2), ("emptied", NT + 2)):
                    dense_counts[key] += more
                self.all_turned = dense_counts["turned"]
                self.all_products = dense_counts["product"]

            def weight(self, c):
                return self.w_at[c // KC][:, c % KC, :] if isinstance(self.w_at, list) else self.w_at[:, c, :]

            def load(self, sp, parts=None):
                for r in range(self.K) if parts is None else parts:
                    sp.dma_start(self.w_at[r] if isinstance(self.w_at, list) else self.w_at[:, r * KC:(r + 1) * KC, :],
                                 self.w[r].rearrange("(c p) n -> p c n", p=P)).then_inc(self.w_in, 16)
                if self.bias is not None and (parts is None or 1 in parts):
                    sp.dma_start(self.bias_at, self.bias.rearrange("(a n) -> a n", a=1)).then_inc(self.w_in, 16)

            def stream_tile(self, sp, j, u, rows=None):
                n = rows or tile_rows(j)
                sp.wait_ge(self.turned, self.b["turned"] + self.K * (j + 1))
                for r in range(self.K):
                    sp.dma_start(self.rows_at[0:n, u, r, :], self.rows[r][bass.ds(j * P, n), :]).then_inc(self.rows_in[u], 16)
                if self.beside is not None:
                    sp.wait_ge(self.emptied, self.b["emptied"] + j + 1)
                    sp.dma_start(self.beside[1][0:n, u, :], self.beside[0][bass.ds(j * P, n), :]).then_inc(self.beside[2][u], 16)

            def stream(self, sp, first=0, last=NT // 2):
                if first == 0:
                    for u in range(2):
                        self.stream_tile(sp, u, u)
                if last > 1:
                    with sp.Fori(0, NT // 2 - 2) as i:
                        for u in range(2):
                            self.stream_tile(sp, 2 * (i + 1) + u, u)
                    for u in range(2):
                        self.stream_tile(sp, NT - 2 + u, u)

            def multiply(self, pe):
                K = self.K
                pe.wait_ge(self.turned, self.b["turned"])
                pe.wait_ge(self.product, self.b["product"])
                pe.sem_inc(self.turned, 2 * K)
                pe.sem_inc(self.product, 2)
                pe.wait_ge(self.w_in, self.b[self.pick] + 16 * (K + (self.bias is not None)))

                def turn(i, u, r):
                    q = K * u + r
                    if r == 0:
                        pe.wait_ge(self.rows_in[u], self.b["rows_in"] + 16 * K * (i + 1))
                    if K > 1 and q >= 2:
                        pe.wait_ge(self.taken, self.b["taken"] + 2 * K * i + q - 1)
                    for c in range(KC):
                        last = pe.transpose(ps[:, 2 * (q % 2) + c // 3, (c % 3) * P:(c % 3 + 1) * P],
                                            self.rows_at[:, u, r, c * P:(c + 1) * P], ident[:, :])
                    last.then_inc(self.turned, 1)

                def times(i, u):
                    j = 2 * i + u
                    pe.wait_ge(self.taken, self.b["taken"] + K * (j + 1))
                    pe.wait_ge(self.emptied, self.b["emptied"] + j + 1)
                    if self.split is not None:
                        whi, wlo, xhi, xlo, (s_w, s_x), n = self.split
                        pe.wait_ge(s_w, n + 1)
                        pe.wait_ge(s_x, NT * n + j + 1)
                    for h in range(2):
                        o = ps[:, 4 + 2 * u + h, 0:HALF]
                        if self.split is not None:
                            for q, (x, w) in enumerate(((xhi, whi), (xhi, wlo), (xlo, whi))):
                                for c in range(KC):
                                    last = pe.matmul(o, x[:, u, c * P:(c + 1) * P], w[:, c * D + h * HALF:c * D + (h + 1) * HALF],
                                                     start=(q == 0 and c == 0), stop=(q == 2 and c == KC - 1))
                            continue
                        for c in range(K * KC):
                            last = pe.matmul(o, self.xt_at[:, u, c, :], self.weight(c)[:, h * HALF:(h + 1) * HALF],
                                             start=(c == 0), stop=(c == K * KC - 1 and self.bias is None))
                        if self.bias is not None:
                            last = pe.matmul(o, ones[0:1, :], self.bias_at[:, h * HALF:(h + 1) * HALF],
                                             start=False, stop=True)
                    last.then_inc(self.product, 1)

                if K == 1:
                    turn(0, 0, 0)
                    turn(0, 1, 0)
                    with pe.Fori(0, NT // 2 - 1) as i:
                        for u in range(2):
                            times(i, u)
                            turn(i + 1, u, 0)
                    for u in range(2):
                        times(NT // 2 - 1, u)
                else:
                    with pe.Fori(0, NT // 2) as i:
                        for u in range(2):
                            for r in range(K):
                                turn(i, u, r)
                            times(i, u)

            def take(self, act, i, u, col=None):
                K, j = self.K, 2 * i + u
                act.wait_ge(self.product, self.b["product"] + j + 1)
                for r in range(K):
                    q = K * u + r
                    act.wait_ge(self.turned, self.b["turned"] + 2 * K + 2 * K * i + q + 1)
                    if col is None:
                        ins = act.activation(self.xt_at[:, u, r * KC:(r + 1) * KC, :].rearrange("p (a b) n -> p a (b n)", a=2),
                                             ps[:, 2 * (q % 2):2 * (q % 2) + 2, 0:HALF], ACT.Copy)
                    else:
                        for c in range(KC):
                            ins = act.activation(self.xt_at[:, u, r * KC + c, :],
                                                 ps[:, 2 * (q % 2) + c // 3, (c % 3) * P:(c % 3 + 1) * P],
                                                 ACT.Relu, bias=col[:, r * KC + c:r * KC + c + 1])
                    if self.split is not None:
                        ins = act.activation(halves(self.split[2][:, u, :]), ps[:, 2 * (q % 2):2 * (q % 2) + 2, 0:HALF], ACT.Copy)
                    ins.then_inc(self.taken, 1)

            def split_weights(self, v, step):
                whi, wlo, _, _, (s_w, _), n = self.split
                w = self.w_at.rearrange("p c n -> p (c n)")
                v.wait_ge(self.w_in, self.b[self.pick] + 16)
                step(v.tensor_copy(whi, w))
                step(v.tensor_tensor(wlo, w, whi.bitcast(F32), ALU.subtract))
                v.sem_inc(s_w, 1)

            def low_rows(self, v, i, u):
                _, _, xhi, xlo, (_, s_x), n = self.split
                v.wait_ge(self.taken, self.b["taken"] + 2 * i + u + 1)
                v.wait_ge(self.product, self.b["product"] + 2 * i + u + 1)
                v.tensor_tensor(xlo[:, u, :], self.xt_at[:, u].rearrange("p c n -> p (c n)"), xhi[:, u, :].bitcast(F32), ALU.subtract)\
                 .then_inc(s_x, 1)

            def take_and_empty(self, act, loop, per, empty, before=None):
                for u in range(2):
                    self.take(act, 0, u)
                with loop(NT // 2 - 1, per) as i:
                    if before is not None:
                        before(i + 1)
                    for u in range(2):
                        empty(2 * i + u, u, i)
                        self.take(act, i + 1, u)
                for u in range(2):
                    empty(NT - 2 + u, u, NT // 2 - 1)

            def psum(self, u):
                return ps[:, 4 + 2 * u:6 + 2 * u, 0:HALF]

        norm_var, norm_root = sem("norm_var"), sem("norm_root")

        class Norm:

            used = 0

            def __init__(self):
                self.var, self.root = norm_var, norm_root
                self.b = NT * Norm.used
                Norm.used += 1

            def vector(self, v, step, z, j):
                st = small[:, 0:12].rearrange("p (a n) -> p a n", a=2)
                mv = small[:, 12:14]
                step.count(v.bn_stats(st[:, 0, :], z[:, 0:HALF]))
                step(v.bn_stats(st[:, 1, :], z[:, HALF:D]))
                step.carry()
                step(v.bn_aggr(mv, st))
                v.tensor_scalar(small[:, 14:15], mv[:, 1:2], EPS_LN, None, ALU.add).then_inc(self.var, 1)
                v.wait_ge(self.root, self.b + j + 1)
                step(v.reciprocal(small[:, 16:17], small[:, 15:16]))
                step(v.tensor_scalar(z, z, mv[:, 0:1], small[:, 16:17], ALU.subtract, ALU.mult))

            def scalar(self, act, j):
                act.wait_ge(self.var, self.b + j + 1)
                act.activation(small[:, 15:16], small[:, 14:15], ACT.Sqrt).then_inc(self.root, 1)
            VSTEPS = 5

        c1 = Carve(work, WORK)
        w_slots = [c1(KC * D).rearrange("p (c n) -> p c n", c=KC) for _ in range(2)]
        rows1 = c1(2 * D).rearrange("p (u r n) -> p u r n", u=2, r=1)
        xt1 = c1(2 * D).rearrange("p (u c n) -> p u c n", u=2, c=KC)
        brow1 = c1(D, parts=1)
        outs1 = c1(2 * (D + 4)).rearrange("p (u n) -> p u n", u=2)
        edges = c1(3 * ET, I32, EP).rearrange("p (a t) -> p a t", a=3)
        rec = c1(ET * REC, F32, EP).rearrange("p (t c) -> p t c", c=REC)
        addr = c1(2 * ET, I32, EP).rearrange("p (a t) -> p a t", a=2)
        relpay = c1(2 * ET, I32, EP).rearrange("p (t c) -> p t c", c=2)
        ibuf = c1(2 * ET, I32, EP).rearrange("p (a t) -> p a t", a=2)
        fbuf = c1(2 * ET, F32, EP).rearrange("p (a t) -> p a t", a=2)
        islot = c1(4 * WAYS, I32, EP).rearrange("p (w c) -> p w c", w=WAYS)
        rslot = c1(REC * WAYS, F32, EP).rearrange("p (w c) -> p w c", c=REC)
        padt, endf, owners = c1(R, I32), c1(R), c1(RT, parts=1)
        avecs = [[c1(D) for _ in range(2)] for _ in range(3)]
        prod1 = c1(D)
        offs = c1(2 * (R + NT)).rearrange("p (a n) -> p a n", a=2)
        marks = [cnt[0:EP, :].bitcast(F32)[:, 0:R * ET], hbuf[0:EP, 3000:3000 + NT * ET]]
        scans = [mask1[0:EP, :].bitcast(F32)[:, 0:R * ET], hbuf[0:EP, 3000 + NT * ET:3000 + 2 * NT * ET]]
        padrel = ct[:, 0:4 * RT].bitcast(I32)
        paddst = hbuf[:, 0:BT * REC].rearrange("p (k c) -> p k c", c=REC)
        s_edges = sem("edges_in")
        s_const = sem("constants")
        s_pads = sem("pad_records")
        s_rowsum = sem("row_sums")
        s_offs = sem("offsets")
        s_offtaken = sem("offsets_taken")
        s_addr = sem("addresses")
        s_scat = [sem(f"scattered{w}") for w in range(WAYS)]
        s_x1 = [sem(f"x1_out{u}") for u in range(2)]
        s_h = [sem(f"h_out{u}") for u in range(2)]
        s_recs = sem("records_in")

        W_AH = Dense("ah", [a["x"]], [a["L0_gnn_W_ah"]], w_slots[0], rows1, xt1, a["L0_gnn_b_ah"], brow1)
        W_H = [Dense(f"h{l}", [xa_d], [a[f"L0_gnn_W{l}"]], w_slots[(l + 1) % 2], rows1, xt1) for l in range(3)]
        PREFIX = [(0, 0, R, 7, RT, RT), (1, R, NT, 7 + (GT - 1).bit_length(), BT, BG)]

        def project(v, step, h, vecs, prod, lr_heads, j, HN):
            for vec, dest in zip(vecs, lr_heads):
                pr = prod.rearrange("p (h c) -> p h c", h=HN)
                step(v.tensor_tensor(pr, h, vec.rearrange("p (h c) -> p h c", h=HN), ALU.mult))
                step(v.tensor_reduce(dest[:, :, bass.ds(j, 1)].rearrange("p h j -> p (h j)"), pr, AX, ALU.add))

        lr0 = [[lr[:, (2 * l + k) * 4 * NT:(2 * l + k + 1) * 4 * NT].rearrange("p (h j) -> p h j", h=4) for k in range(2)] for l in range(3)]
        lr2 = [lr[:, k * 12 * NT:(k + 1) * 12 * NT].rearrange("p (h j) -> p h j", h=12) for k in range(2)]
        s_vecs, s_hready, s_hread = sem("attention_vectors_in"), sem("h_tile_ready"), sem("h_tile_read")

        def sp_phase1(sp):
            sp.dma_start(edges[:, 0, :], a["src"].rearrange("(p t) -> p t", p=EP)).then_inc(s_edges, 16)
            sp.dma_start(edges[:, 1, :], a["dst"].rearrange("(p t) -> p t", p=EP)).then_inc(s_edges, 16)
            sp.dma_start(edges[:, 2, :], a["edge_type_34"].rearrange("(p t) -> p t", p=EP)).then_inc(s_edges, 16)
            W_AH.load(sp)
            W_AH.stream(sp, 0, 1)
            W_H[0].load(sp)
            for l in range(3):
                for k, name in enumerate(("a_src", "a_dst")):
                    sp.dma_start(avecs[l][k], a[f"L0_gnn_{name}{l}"].rearrange("h c -> (h c)").partition_broadcast(P)).then_inc(s_vecs, 16)
            W_AH.stream(sp, 1)
            for u in range(2):
                sp.wait_ge(s_x1[u], 16 * (NT // 2 + 1))
            for l in range(3):
                if l:
                    sp.wait_ge(W_AH.product, (W_AH if l == 1 else W_H[0]).all_products)
                    W_H[l].load(sp)
                sp.wait_ge(W_AH.turned, (W_AH if l == 0 else W_H[l - 1]).all_turned)
                W_H[l].stream(sp)

        def act_phase1(act, step):
            act.sem_inc(W_AH.emptied, 2)
            for u in range(2):
                act.sem_inc(s_x1[u], 16)
                act.sem_inc(s_h[u], 16)

            def empty_x1(j, u, i):
                act.wait_ge(W_AH.product, W_AH.b["product"] + j + 3)
                act.wait_ge(s_x1[u], 16 * (i + 1))
                step(act.activation(halves(outs1[:, u, 0:D]), W_AH.psum(u), ACT.Relu))
                act.sem_inc(W_AH.emptied, 1)
                act.dma_start(xa_d[bass.ds(j * P, P), :], outs1[:, u, 0:D]).then_inc(s_x1[u], 16)

            W_AH.take_and_empty(act, step.loop, 2, empty_x1)
            for u in range(2):
                act.wait_ge(s_x1[u], 16 * (NT // 2 + 1))
            hv = [outs1[:, u, :].rearrange("p (h c) -> p h c", h=4) for u in range(2)]
            act.wait_ge(s_const, 1)
            for u in range(2):
                step(act.activation(hv[u][:, :, 192], ones[:, 0:4], ACT.Copy))
            for l in range(3):
                act.sem_inc(W_H[l].emptied, 2)

                def empty_h(j, u, i):
                    act.wait_ge(W_H[l].product, W_H[l].b["product"] + j + 3)
                    act.wait_ge(s_h[u], 16 * (i + 1) + 16 * l * (NT // 2))
                    act.wait_ge(s_hread, NT * l + j + 1)
                    for b in range(2):
                        step.count(act.activation(hv[u][:, 2 * b:2 * b + 2, 0:192],
                                                  ps[:, 4 + 2 * u + b, 0:HALF].rearrange("p (h c) -> p h c", h=2), ACT.Copy))
                    step.wait()
                    act.sem_inc(W_H[l].emptied, 1)
                    act.sem_inc(s_hready, 1)
                    act.dma_start(h_d[l][bass.ds(j * P, P), :], outs1[:, u, :]).then_inc(s_h[u], 16)

                W_H[l].take_and_empty(act, step.loop, 4, empty_h)
            for u in range(2):
                act.wait_ge(s_h[u], 16 * (3 * NT // 2 + 1))

        def pe_phase1(pe):
            pe.wait_ge(s_const, 2)
            pe.wait_ge(s_rowsum, 1)
            pe.matmul(ps[:, 0, HALF:HALF + R + NT], tri[0:EP, :], small[0:EP, 0:R + NT], start=True, stop=True)
            pe.matmul(ps[:, 1, HALF:HALF + R + NT], ones[0:EP, :], small[0:EP, 0:R + NT], start=True, stop=True).then_inc(s_offs, 1)
            pe.wait_ge(s_offtaken, 1)
            for s in [W_AH] + W_H:
                s.multiply(pe)

        def dve_phase1(v, step):
            v.wait_ge(s_edges, 48)
            v.wait_ge(s_const, 2)
            src, dst, typ = (edges[:, k, :] for k in range(3))
            step(v.tensor_scalar(ibuf[:, 0, :], dst, 7, None, ALU.arith_shift_right))
            step(v.tensor_scalar(ibuf[:, 1, :], dst, P - 1, None, ALU.bitwise_and))
            step(v.tensor_copy(rec[:, :, 0], src))
            step(v.tensor_copy(rec[:, :, 1], ibuf[:, 1, :]))
            step(v.tensor_copy(rec[:, :, 2], typ))
            step(v.tensor_copy(fbuf[:, 0, :], dst))
            step(v.tensor_copy(fbuf[:, 1, :], ibuf[:, 0, :]))
            step(v.tensor_copy(relpay[:, :, 0], src))
            step(v.scalar_tensor_tensor(relpay[:, :, 1], fbuf[:, 0, :], float(R), rec[:, :, 2], ALU.mult, ALU.add))
            for g, b0, nb, _, _, _ in PREFIX:
                key = rec[:, :, 2] if g == 0 else fbuf[:, 1, :]
                for b in range(nb):
                    step.count(v.tensor_scalar(marks[g][:, b * ET:(b + 1) * ET], key, float(b), None, ALU.is_equal))
                step.wait()
                step(v.tensor_tensor_scan(scans[g], marks[g], marks[g], 0.0, ALU.add, ALU.max))
                last = scans[g].rearrange("p (b t) -> p b t", b=nb)[:, :, ET - 1]
                tot = small[0:EP, b0:b0 + nb]
                step.count(v.tensor_copy(tot[:, 0:1], last[:, 0:1]))
                step(v.tensor_tensor(tot[:, 1:nb], last[:, 1:nb], last[:, 0:nb - 1], ALU.subtract))
            v.sem_inc(s_rowsum, 1)
            v.wait_ge(s_offs, 1)
            step(v.tensor_copy(offs, ps[:, 0:2, HALF:HALF + R + NT]))
            v.sem_inc(s_offtaken, 1)
            for g, b0, nb, shift, nt, units in PREFIX:
                scan3 = scans[g].rearrange("p (b t) -> p b t", b=nb)
                last, rowoff = scan3[:, :, ET - 1], fbuf[:, 0, 0:nb]
                ti, tf, ef = padt[:, 0:nb], small[:, 0:nb], endf[:, 0:nb]
                step(v.tensor_scalar(ti, offs[:, 1, b0:b0 + nb], float((1 << shift) - 1), None, ALU.add))
                step(v.tensor_scalar(ti, ti, shift, None, ALU.arith_shift_right))
                step(v.tensor_copy(tf, ti))
                step(v.tensor_tensor_scan(ef, tf, tf, 0.0, ALU.add, ALU.max))
                step(v.tensor_tensor(tf, ef, tf, ALU.subtract))
                step(v.scalar_tensor_tensor(rowoff, tf[0:EP], float(1 << shift), offs[0:EP, 0, b0:b0 + nb], ALU.mult, ALU.add))
                step(v.tensor_scalar(rowoff, rowoff, -1.0, None, ALU.add))
                step(v.tensor_tensor(rowoff[:, 1:nb], rowoff[:, 1:nb], last[:, 0:nb - 1], ALU.subtract))
                for b in range(nb):
                    o = marks[g][:, b * ET:(b + 1) * ET]
                    step.count(v.scalar_tensor_tensor(o, scan3[:, b, :], rowoff[:, b:b + 1], o, ALU.add, ALU.mult))
                step.wait()
                pos = rec[:, :, 3] if g == 0 else fbuf[:, 0, :]
                step(v.tensor_reduce(pos, marks[g].rearrange("p (b t) -> p t b", b=nb), AX, ALU.add))
                step(v.tensor_copy(ibuf[:, 0, :], pos))
                step(v.tensor_scalar(ibuf[:, 1, :], ibuf[:, 0, :], P - 1, None, ALU.bitwise_and))
                step(v.tensor_scalar(ibuf[:, 0, :], ibuf[:, 0, :], 7, None, ALU.arith_shift_right))
                step(v.scalar_tensor_tensor(addr[:, g, :], ibuf[:, 1, :], float(nt), ibuf[:, 0, :], ALU.mult, ALU.add))
                owner = owners[:, 0:units]
                step(v.memset(owner, 0.0))
                for b in range(nb):
                    step(v.scalar_tensor_tensor(owner, iota[0:1, 0:units], endf[0:1, b:b + 1], owner, ALU.is_ge, ALU.add))
                step(v.tensor_scalar((tile_rel if g == 0 else group_dst)[:, :], owner, float(nb - 1), None, ALU.min))
                if g == 0:
                    step(v.memset(end_rel[:, :], 0))
                    step(v.tensor_copy(end_rel[:, 2:R + 2], endf[0:1, 0:R]))
            v.sem_inc(s_addr, 1)
            v.wait_ge(s_vecs, 96)
            v.sem_inc(s_hread, 2)
            for l in range(3):
                with step.loop(NT // 2, 8) as i:
                    for u in range(2):
                        j = 2 * i + u
                        v.wait_ge(s_hready, NT * l + j + 1)
                        project(v, step, outs1[:, u, :].rearrange("p (h c) -> p h c", h=4)[:, :, 0:192], avecs[l], prod1, lr0[l], j, 4)
                        v.sem_inc(s_hread, 1)

        def pool_phase1(g, step):
            step(g.memset(ones[:, :], 1.0))
            g.sem_inc(s_const, 1)
            step(g.memset(ident[:, :], 0.0))
            step(g.affine_select(out=ident[:, :], in_=ident[:, :], compare_op=ALU.not_equal, fill=1.0,
                                 base=0, pattern=[[-1, P]], channel_multiplier=1))
            step(g.affine_select(out=tri[:, :], in_=ones[:, :], compare_op=ALU.is_gt, fill=0.0,
                                 base=0, pattern=[[1, P]], channel_multiplier=-1))
            step(g.iota(iota[:, :], [[1, NP]], base=0, channel_multiplier=0))
            g.sem_inc(s_const, 1)
            step(g.memset(padrel, 0))
            step(g.memset(paddst, 0.0))
            step(g.memset(paddst[:, :, 0:2], -1.0))
            g.dma_start(relrec_d.rearrange("(p k) c -> p (k c)", p=P), padrel).then_inc(s_pads, 16)
            g.dma_start(dstrec_d.rearrange("(p k) c -> p (k c)", p=P), paddst.rearrange("p k c -> p (k c)")).then_inc(s_pads, 16)
            g.wait_ge(s_pads, 32)
            step(g.memset(ct[:, :], 0))
            g.wait_ge(s_addr, 1)
            scatter(g, step, 1)
            g.dma_start(drec[:, :], dstrec_d.rearrange("(p k) c -> p (k c)", p=P)).then_inc(s_recs, 16)
            g.wait_ge(s_recs, 16)

        def scatter(g, step, which):
            before = 0 if which == 1 else 16 * (ET // WAYS)

            def column(t, w, first):
                if not first:
                    g.wait_ge(s_scat[w], before + 16 * (t // WAYS))
                if which == 0:
                    step.count(g.tensor_copy(islot[:, w, 2:4], relpay[:, bass.ds(t, 1), :].rearrange("p t c -> p (t c)")))
                else:
                    step.count(g.tensor_copy(rslot[:, w, :], rec[:, bass.ds(t, 1), :].rearrange("p t c -> p (t c)")))
                step(g.tensor_copy(islot[:, w, which:which + 1], addr[:, which, bass.ds(t, 1)]))
                step.carry()
                g.indirect_dma_start(out=(relrec_d, dstrec_d)[which],
                                     out_offset=bass.IndirectOffsetOnAxis(islot[:, w, which:which + 1], 0),
                                     in_=(islot[:, w, 2:4], rslot[:, w, :])[which], in_offset=None).then_inc(s_scat[w], 16)

            for w in range(WAYS):
                column(w, w, which == 1)
            with step.loop(ET // WAYS - 1, 2 * WAYS) as i:
                for w in range(WAYS):
                    column(WAYS * (i + 1) + w, w, False)
            for w in range(WAYS):
                g.wait_ge(s_scat[w], before + 16 * (ET // WAYS))

        def pool_phase2(g, step):
            scatter(g, step, 0)
            step(g.memset(relrec[:, 2 * RT:], 0))
            g.dma_start(relrec[:, 0:2 * RT], relrec_d.rearrange("(p k) c -> p (k c)", p=P)).then_inc(s_recs, 16)
            g.wait_ge(s_recs, 32)

        c2 = Carve(work, WORK)
        oh_t = c2(2 * GT * P, BF16).rearrange("p (u n) -> p u n", u=2 * GT)
        oh_s = c2(2 * GT * CW, BF16).rearrange("p (u n) -> p u n", u=2 * GT)
        s_oh = sem("onehots")
        s_ctp = sem("count_products")
        s_cta = sem("counts_added")

        def group_loop(fori, group):
            with fori(BG // 2) as i:
                for u in range(2):
                    group(2 * i + u, u)
            if BG % 2:
                group(BG - 1, 0)

        def dve_phase2(v, step):
            v.sem_inc(s_cta, 2)

            def compare(k, u):
                v.wait_ge(s_ctp, k + 1)
                for w in range(GT):
                    dr = drec3[:, bass.ds(GT * k + w, 1), :].rearrange("p k c -> p (k c)")
                    v.tensor_scalar(oh_t[:, GT * u + w, :], iota[:, 0:P], dr[:, 1:2], None, ALU.is_equal)
                    v.tensor_scalar(oh_s[:, GT * u + w, 0:NP], iota[:, :], dr[:, 0:1], None, ALU.is_equal)
                    v.tensor_scalar(oh_s[:, GT * u + w, NP:CW], iota[:, 0:R], dr[:, 2:3], None, ALU.is_equal).then_inc(s_oh, 1)

            def add(k, u):
                b = v.value_load(group_dst[0:1, bass.ds(k, 1)], min_val=0, max_val=NT - 1)
                v.wait_ge(s_ctp, k + 3)
                c = ct[:, bass.ds(b * CW, CW)]
                step(v.tensor_tensor(c, psf[:, u * 2048:u * 2048 + CW], c, ALU.add))
                v.sem_inc(s_cta, 1)

            compare(0, 0)
            with step.loop((BG - 1) // 2, 2) as i:
                for u in range(2):
                    compare(2 * i + u + 1, 1 - u)
                    add(2 * i + u, u)
            for k in range((BG - 1) // 2 * 2, BG):
                if k + 1 < BG:
                    compare(k + 1, (k + 1) % 2)
                add(k, k % 2)

        def pe_phase2(pe):
            def group(k, u):
                pe.wait_ge(s_cta, k + 1)
                for w in range(GT):
                    pe.wait_ge(s_oh, GT * k + w + 1)
                    for n0 in range(0, CW, 512):
                        n1 = min(n0 + 512, CW)
                        last = pe.matmul(psf[:, u * 2048 + n0:u * 2048 + n1], oh_t[:, GT * u + w, :], oh_s[:, GT * u + w, n0:n1],
                                         start=(w == 0), stop=(w == GT - 1))
                last.then_inc(s_ctp, 1)

            pe.sem_inc(s_ctp, 2)
            group_loop(lambda n: pe.Fori(0, n), group)

        c3 = Carve(work, WORK)
        crow = c3(2 * NP).rearrange("p (u n) -> p u n", u=2)
        deg = c3(NT)
        inv = c3(NT * R).rearrange("p (j r) -> p j r", j=NT)
        s_crow = sem("count_rows")
        s_row, s_rused, s_cout = sem("plain_rows"), sem("plain_rows_used"), sem("counts_copied")
        s_cturn = sem("counts_turned")
        s_inv = sem("inverse_counts")
        s_invd = sem("inverse_counts_stored")
        s_deg = sem("degrees")
        s_root = sem("degree_roots")

        def dve_phase3(v, step):
            step(v.tensor_scalar(inv, ct3[:, :, NP:CW], 1.0, None, ALU.max))
            step(v.reciprocal(inv, inv))
            v.sem_inc(s_inv, 1)
            v.sem_inc(s_rused, 2)
            with step.loop(NT // 2, 8) as i:
                for u in range(2):
                    j = 2 * i + u
                    row, c = crow[:, u, :], ct[:, bass.ds(j * CW, NP)]
                    v.wait_ge(s_row, j + 1)
                    dg = crow[:, u, bass.ds(j * P, P)]
                    step(v.tensor_tensor(dg, dg, ident[:, :], ALU.add))
                    v.sem_inc(s_crow, 1)
                    step.count(v.tensor_scalar(mask1[:, bass.ds(j * NP, NP)], row, 0.0, NONE, ALU.is_equal, ALU.mult))
                    step.count(v.tensor_scalar(ct[:, bass.ds(j * CW, NP)].bitcast(BF16), c, 0.0, NONE, ALU.is_equal, ALU.mult))
                    step(v.tensor_reduce(deg[:, bass.ds(j, 1)], row, AX, ALU.add))
                    v.sem_inc(s_rused, 1)
            v.sem_inc(s_deg, 1)
            v.wait_ge(s_root, 1)
            step(v.reciprocal(dinv[:, :], dinv[:, :]))

        def pe_phase3(pe):
            pe.sem_inc(s_cturn, 2)
            with pe.Fori(0, NT // 2) as i:
                for u in range(2):
                    j = 2 * i + u
                    pe.wait_ge(s_crow, j + 1)
                    pe.wait_ge(s_cout, j + 1)
                    for s in range(NT):
                        last = pe.transpose(psf[:, u * 2048 + s * P:u * 2048 + (s + 1) * P], crow[:, u, s * P:(s + 1) * P], ident[:, :])
                    last.then_inc(s_cturn, 1)

        def act_phase3(act):
            def row(j, u):
                act.wait_ge(s_cturn, j + 1)
                act.wait_ge(s_rused, j + 1)
                act.activation(crow[:, u, :], ct[:, bass.ds(j * CW, NP)], ACT.Copy).then_inc(s_row, 1)

            def turned(j, u):
                act.wait_ge(s_cturn, j + 3)
                act.activation(cnt3[:, :, bass.ds(j * P, P)], psf[:, u * 2048:u * 2048 + NP].rearrange("p (s n) -> p s n", n=P), ACT.Copy)\
                   .then_inc(s_cout, 1)

            act.sem_inc(s_cout, 2)
            row(0, 0)
            with act.Fori(0, NT // 2 - 1) as i:
                for u in range(2):
                    row(2 * i + u + 1, 1 - u)
                    turned(2 * i + u, u)
            row(NT - 1, 1)
            turned(NT - 2, 0)
            turned(NT - 1, 1)
            act.wait_ge(s_deg, 1)
            act.activation(dinv[:, :], deg, ACT.Sqrt).then_inc(s_root, 1)

        class Attention:
            def __init__(self, name, HN, mask, layers):
                self.HN, self.C, self.mask, self.layers = HN, D // HN, mask, layers
                self.banks = 5 if HN == 4 else 2
                self.narrow = 2 * (self.C + 1) < P + P // 2
                self.late = 3 if self.narrow else 1
                self.b0 = 6 if self.narrow else 3
                self.tpb = NT // self.banks
                cv = Carve(work, WORK)
                heads = [cv((HN + 1) * NT).rearrange("p (h j) -> p h j", h=HN + 1) for _ in range(5)]
                self.M, self.R1, self.R2, self.L2, self.y = heads
                self.mh = cv(NT)
                self.diag = [cv(NP) for _ in range(2)]
                self.R1b = [cv(N) for _ in range(2)]
                self.R2b = [cv(N) for _ in range(2)]
                self.t2 = [cv(N) for _ in range(2)]
                self.t = [cv(N) for _ in range(2)]
                self.p = [cv(NP) for _ in range(2)]
                self.o = cv(NT * self.C)
                self.den = cv(NT)
                if self.narrow:
                    self.feat = [cv(NT * (self.C + 1)) for _ in range(2)]
                    self.flat = cv(NP)[0:self.C + 1, :]
                    self.s_feat, self.s_turned = sem(name + "_features"), sem(name + "_turned")
                (self.s_in_, self.s_diagA, self.s_bcA, self.s_maxed, self.s_hr, self.s_diagC, self.s_bcC, self.s_rb, self.s_t2r,
                 self.s_tr, self.s_er, self.s_pr, self.s_agg, self.s_out, self.s_stored, self.s_aggfree) = (
                    sem(f"{name}_{s}") for s in ("features_in", "max_spread", "max_rows", "maxed", "heads_ready", "spread", "rows",
                                                 "rows_taken", "second_ready", "exponent_ready", "exp_ready", "weights_ready",
                                                 "summed", "head_ready", "head_stored", "sums_free"))

                self.used = cv.at

            def sp(self, sp, n, ahead=None):
                _, o_dram, load_from = self.layers[n]
                if load_from is not None:
                    sp.dma_start(hbuf[:, 0:NT * (D + self.HN)].rearrange("p (j n) -> p j n", j=NT),
                                 load_from.rearrange("(j p) n -> p j n", p=P)).then_inc(self.s_in_, 16)
                if ahead is not None:
                    sp.wait_ge(self.s_maxed, 2 + self.HN * (n + 1))
                    ahead(sp)
                od = o_dram.rearrange("(j p) n -> p j n", p=P)
                with sp.Fori(0, self.HN) as h:
                    sp.wait_ge(self.s_out, self.HN * n + h + 1)
                    sp.dma_start(od[:, :, bass.ds(h * self.C, self.C)], self.o.rearrange("p (j c) -> p j c", j=NT))\
                      .then_inc(self.s_stored, 16)
                sp.wait_ge(self.s_stored, 16 * self.HN * (n + 1))

            def pool(self, g, step, n):
                HN, H0 = self.HN, self.HN * n

                def spread(k, vec, signal):
                    g.tensor_tensor(self.diag[k].rearrange("p (j n) -> p j n", j=NT),
                                    ident[:, :].unsqueeze(1).to_broadcast([P, NT, P]),
                                    vec.rearrange("p h j -> p (h j)").unsqueeze(2).to_broadcast([P, NT, P]), ALU.mult).then_inc(signal, 1)

                with g.Fori(0, HN // 2) as i:
                    for u in range(2):
                        h = 2 * i + u
                        g.wait_ge(self.s_bcA, H0 + h + 1)
                        spread(u, self.layers[n][0][0][:, bass.ds(h, 1), :], self.s_diagA)
                g.wait_ge(self.s_bcA, H0 + HN + 2)
                g.wait_ge(self.s_hr, n + 1)
                if self.narrow:
                    g.tensor_copy(self.feat[0].rearrange("p (j c) -> p j c", j=NT),
                                  hbuf[:, 0:NT * (D + HN)].rearrange("p (j h c) -> p j h c", j=NT, h=HN)[:, :, 0, :]).then_inc(self.s_feat, 1)
                spread(0, self.R1[:, 0:1, :], self.s_diagC)
                spread(1, self.R2[:, 0:1, :], self.s_diagC)

                def next_head(h):
                    for k, r in ((0, self.R1), (1, self.R2)):
                        g.wait_ge(self.s_bcC, 2 * (H0 + n + h - 1) + k + 1)
                        spread(k, r[:, bass.ds(h, 1), :], self.s_diagC)

                def features(h, u):
                    g.wait_ge(self.s_agg, 2 + NT * (h - 1))
                    g.tensor_copy(self.feat[u].rearrange("p (j c) -> p j c", j=NT),
                                  hbuf[:, 0:NT * (D + HN)].rearrange("p (j h c) -> p j h c", j=NT, h=HN)[:, :, bass.ds(h, 1), :]
                                  .rearrange("p j h c -> p j (h c)")).then_inc(self.s_feat, 1)

                if self.narrow:
                    features(1, 1)
                    with g.Fori(0, HN // 2 - 1) as i:
                        for u in range(2):
                            next_head(2 * i + u + 1)
                            features(2 * i + u + 2, u)
                    next_head(HN - 1)
                    next_head(HN)
                else:
                    with g.Fori(0, HN) as i:
                        next_head(i + 1)

            def dve(self, v, step, n):
                HN, C = self.HN, self.C
                H0 = HN * n
                L, Rr = self.layers[n][0]
                if n == 0:
                    v.sem_inc(self.s_tr, 2)
                    v.sem_inc(self.s_pr, 2)
                    v.sem_inc(self.s_maxed, 2)
                with step.loop(HN // 2, 2 * (NT + 1)) as i:
                    for u in range(2):
                        h = 2 * i + u
                        v.wait_ge(self.s_bcA, H0 + h + 3)
                        step.carry()
                        for j in range(NT):
                            step(v.tensor_tensor_reduce(self.p[0][:, 0:N], self.mask[:, j, 0:N], psf[:, u * 1536:u * 1536 + N], 1.0, NONE,
                                                        ALU.add, ALU.max, self.mh[:, j:j + 1]))
                            step.carry()
                        v.sem_inc(self.s_maxed, 1)
                        step(v.tensor_copy(self.M[:, bass.ds(h, 1), :].rearrange("p h j -> p (h j)"), self.mh))
                for p in self.p:
                    step.count(v.memset(p[:, N:NP], 0.0))
                M, R1, R2, L2, y = (t[:, 0:HN, :] for t in (self.M, self.R1, self.R2, self.L2, self.y))
                step(v.tensor_scalar(y, M, 0.1 * NONE, -NONE, ALU.is_lt, ALU.mult))
                step(v.tensor_tensor(M, M, y, ALU.add))
                step(v.tensor_tensor(y, M, Rr, ALU.add))
                step(v.scalar_tensor_tensor(M, y, SLOPE, y, ALU.mult, ALU.max))
                step.count(v.tensor_tensor(R1, Rr, M, ALU.subtract))
                step.count(v.scalar_tensor_tensor(R2, Rr, SLOPE, M, ALU.mult, ALU.subtract))
                for t in (self.R1, self.R2):
                    step.count(v.memset(t[:, HN, :], 0.0))
                step(v.tensor_scalar(L2, L, SLOPE, None, ALU.mult))
                v.sem_inc(self.s_hr, 1)
                v.sem_inc(self.s_aggfree, 1)

                def T(i, g):
                    hh, s = divmod(g, NT)
                    h = 2 * i + hh
                    if s == 0:
                        v.wait_ge(self.s_rb, 2 * (H0 + n + h + 1))
                    v.wait_ge(self.s_pr, NT * H0 + 2 * NT * i + g + 1)
                    v.wait_ge(self.s_t2r, NT * H0 + 2 * NT * i + g + 1)
                    l = L[:, bass.ds(h, 1), s:s + 1].rearrange("p h s -> p (h s)")
                    v.scalar_tensor_tensor(self.t[g % 2], self.R1b[hh], l, self.t2[g % 2], ALU.add, ALU.max)\
                     .then_inc(self.s_tr, 1)

                def weigh(i, g):
                    v.wait_ge(self.s_er, NT * H0 + 2 * NT * i + g + 1)
                    v.wait_ge(self.s_agg, NT * H0 + 2 * NT * i + g + 1)
                    v.scalar_tensor_tensor(self.p[g % 2][:, 0:N], self.t[g % 2], 1.0, cnt3[:, g % NT, 0:N], ALU.min, ALU.mult)\
                     .then_inc(self.s_pr, 1)

                def evict(i, hh):
                    h = 2 * i + hh
                    if self.narrow:
                        v.wait_ge(self.s_turned, h + 1)
                    else:
                        v.wait_ge(self.s_agg, 2 + NT * (H0 + h + 1))
                    if not (isinstance(h, int) and H0 + h == 0):
                        v.wait_ge(self.s_stored, 16 * (H0 + h))
                    acc = ps[:, self.b0:self.b0 + self.banks, 0:self.tpb * (C + 1)].rearrange("p b (t c) -> p b t c", c=C + 1)
                    den = self.den.rearrange("p (b t) -> p b t", b=self.banks)
                    step(v.tensor_scalar(den, acc[:, :, :, C], TINY, None, ALU.add if HN == 4 else ALU.max))
                    step(v.reciprocal(self.den, self.den))
                    step(v.tensor_tensor(self.o.rearrange("p (b t c) -> p b t c", b=self.banks, c=C), acc[:, :, :, 0:C],
                                         den.unsqueeze(3).to_broadcast([P, self.banks, self.tpb, C]), ALU.mult))
                    v.sem_inc(self.s_out, 1)
                    if not self.narrow:
                        v.sem_inc(self.s_aggfree, 1)

                def pair(i, first=False, last=False):
                    for g in range(1, 2 * NT + 1):
                        if g < 2 * NT:
                            T(i, g)
                        elif not last:
                            T(i + 1, 0)
                        weigh(i, g - 1)
                        if g == self.late and not first:
                            evict(i - 1, 1)
                        if g == NT + self.late:
                            evict(i, 0)

                T(0, 0)
                pair(0, first=True)
                if HN > 4:
                    with step.loop(HN // 2 - 2, 6) as i:
                        pair(i + 1)
                pair(HN // 2 - 1, last=True)
                evict(HN // 2 - 1, 1)

            def pe(self, pe, n):
                HN, C = self.HN, self.C
                H0 = HN * n
                if n == 0:
                    pe.sem_inc(self.s_agg, 2)
                    pe.sem_inc(self.s_bcA, 2)

                def repeat_rows(k, at=0):
                    for n0 in range(0, N, 512):
                        n1 = min(N, n0 + 512)
                        last = pe.matmul(psf[:, at + n0:at + n1], ones[:, :], self.diag[k][:, n0:n1], start=True, stop=True)
                    return last

                with pe.Fori(0, HN // 2) as i:
                    for u in range(2):
                        h = 2 * i + u
                        pe.wait_ge(self.s_diagA, H0 + h + 1)
                        pe.wait_ge(self.s_maxed, H0 + h + 1)
                        repeat_rows(u, 1536 * u).then_inc(self.s_bcA, 1)
                pe.wait_ge(self.s_maxed, 2 + H0 + HN)
                for k in range(2):
                    pe.wait_ge(self.s_diagC, 2 * (H0 + n) + k + 1)
                    if k:
                        pe.wait_ge(self.s_rb, 2 * (H0 + n) + 1)
                    repeat_rows(k).then_inc(self.s_bcC, 1)
                if self.layers[n][2] is not None:
                    pe.wait_ge(self.s_in_, 16 * (n + 1))
                def turn_back(h):
                    pe.wait_ge(self.s_aggfree, h + 2)
                    if not isinstance(h, int) or h:
                        pe.wait_ge(self.s_out, h)
                    for dt in range(NT):
                        b, t = divmod(dt, self.tpb)
                        last = pe.transpose(ps[:, self.b0 + b, t * (C + 1):(t + 1) * (C + 1)], self.flat[:, dt * P:(dt + 1) * P],
                                            ident[0:C + 1, 0:C + 1])
                    last.then_inc(self.s_turned, 1)

                def pair(i, first=False):
                    for g in range(2 * NT):
                        hh, s = divmod(g, NT)
                        h = 2 * i + hh
                        if s == 0:
                            if self.narrow:
                                pe.wait_ge(self.s_feat, h + 1)
                            pe.wait_ge(self.s_aggfree, H0 + n + h + 1)
                        pe.wait_ge(self.s_pr, 2 + NT * H0 + 2 * NT * i + g + 1)
                        if self.narrow:
                            for n0 in range(0, NP, 512):
                                n1 = min(NP, n0 + 512)
                                last = pe.matmul(psf[0:C + 1, 1536 + n0:1536 + n1], self.feat[hh][:, s * (C + 1):(s + 1) * (C + 1)],
                                                 self.p[g % 2][:, n0:n1], start=(s == 0), stop=(s == NT - 1))
                        else:
                            hs = hbuf[:, bass.ds(h * (C + 1) + s * (D + HN), C + 1)]
                            for dt in range(NT):
                                b, t = divmod(dt, self.tpb)
                                last = pe.matmul(ps[:, self.b0 + b, t * (C + 1):(t + 1) * (C + 1)], self.p[g % 2][:, dt * P:(dt + 1) * P],
                                                 hs, start=(s == 0 and t == 0), stop=(s == NT - 1), skip_group_check=True)
                        last.then_inc(self.s_agg, 1)
                        if self.narrow and s == 0 and not (first and g == 0):
                            turn_back(h - 1)
                        if s in (1, 4):
                            k = (s - 1) // 3
                            pe.wait_ge(self.s_diagC, 2 * (H0 + n + h + 1) + k + 1)
                            pe.wait_ge(self.s_rb, 2 * (H0 + n + h + 1) + k)
                            repeat_rows(k).then_inc(self.s_bcC, 1)

                pair(0, first=True)
                with pe.Fori(0, HN // 2 - 1) as i:
                    pair(i + 1)
                if self.narrow:
                    turn_back(HN - 1)

            def act(self, act, step, n):
                H0 = self.HN * n

                def rows_out(hh, k, head):
                    act.wait_ge(self.s_bcC, 2 * (H0 + n + head) + k + 1)
                    act.activation((self.R1b, self.R2b)[k][hh], psf[:, 0:N], ACT.Copy).then_inc(self.s_rb, 1)

                def T2(i, g):
                    hh, s = divmod(g, NT)
                    h = 2 * i + hh
                    if s == 0:
                        act.wait_ge(self.s_rb, 2 * (H0 + n + h + 1))
                    act.wait_ge(self.s_tr, NT * H0 + 2 * NT * i + g + 1)
                    b = self.L2[:, bass.ds(h, 1), s:s + 1].rearrange("p h s -> p (h s)")
                    act.activation(self.t2[g % 2], self.R2b[hh], ACT.Identity, bias=b).then_inc(self.s_t2r, 1)

                def EX(i, g):
                    act.wait_ge(self.s_tr, 2 + NT * H0 + 2 * NT * i + g + 1)
                    act.activation(self.t[g % 2], self.t[g % 2], ACT.Exp).then_inc(self.s_er, 1)

                def sums_out(h):
                    act.wait_ge(self.s_agg, 2 + NT * (h + 1))
                    if not isinstance(h, int) or h:
                        act.wait_ge(self.s_turned, h)
                    act.activation(self.flat, psf[0:self.C + 1, 1536:1536 + NP], ACT.Copy).then_inc(self.s_aggfree, 1)

                def pair(i, first=False, last=False):
                    for g in range(1, 2 * NT + 1):
                        if g < 2 * NT:
                            T2(i, g)
                        elif not last:
                            T2(i + 1, 0)
                        EX(i, g - 1)
                        hh, s = divmod(g, NT)
                        if self.narrow and s == 1 and not (first and g == 1):
                            sums_out(2 * i + hh - 1)
                        if s in (5, 8):
                            rows_out(1 - hh, (s - 5) // 3, 2 * i + hh + 1)

                act.wait_ge(self.s_hr, n + 1)
                rows_out(0, 0, 0)
                rows_out(0, 1, 0)
                T2(0, 0)
                pair(0, first=True)
                if self.HN > 4:
                    with act.Fori(0, self.HN // 2 - 2) as i:
                        pair(i + 1)
                pair(self.HN // 2 - 1, last=True)
                if self.narrow:
                    sums_out(self.HN - 1)

        att0 = Attention("gat", 4, mask1v, [(lr0[l], gat_d[l], h_d[l]) for l in range(3)])

        assert att0.used <= WORK - KC * D

        def store_tiles(g, step, ready, slots, dst, stored, before=0):
            def store(j, u):
                g.wait_ge(ready, before + j + 1)
                step.carry()
                n = tile_rows(j) if dst is out else P
                g.dma_start(dst[bass.ds(j * P, n), :], slots[0:n, u, :]).then_inc(stored[u], 16)

            with g.Fori(0, NT // 2 - 1) as i:
                for u in range(2):
                    store(2 * i + u, u)
            for u in range(2):
                store(NT - 2 + u, u)
            for u in range(2):
                g.wait_ge(stored[u], 8 * before + 16 * (NT // 2))

        def two(name):
            return [sem(f"{name}{u}") for u in range(2)]

        c4 = Carve(work, WORK)
        h4 = Carve(hbuf, NT * (D + 12))
        colb = h4(3 * KC)
        z4 = h4(2 * D).rearrange("p (u n) -> p u n", u=2)
        x4s = c4(2 * D).rearrange("p (u n) -> p u n", u=2)
        s_x4s, s_z4st = two("wout_x_in"), two("x1_stored")
        s_z4, s_colb = sem("x1_ready"), sem("gat_bias_in")
        w4 = [v.rearrange("p (c n) -> p c n", c=KC) for v in (mask1[:, :].bitcast(F32)[:, 0:KC * D], c4(KC * D), work[:, WORK - KC * D:])]
        r4 = c4(6 * D).rearrange("p (u r n) -> p u r n", u=2, r=3)
        xt4 = h4(6 * D).rearrange("p (u c n) -> p u c n", u=2, c=3 * KC)
        W_OUT = Dense("wout", gat_d, [a["L0_gnn_W_out"][l * D:(l + 1) * D, :] for l in range(3)], w4, r4, xt4,
                      a["L0_gnn_b_out"], h4(D, parts=1), beside=(a["x"], x4s, s_x4s))
        norm1 = Norm()
        assert c4.at <= 3 * KC * D

        def sp_wout(sp):
            for l in range(3):
                sp.dma_start(colb[:, l * KC:(l + 1) * KC], a[f"L0_gnn_b{l}"].rearrange("(c p) -> p c", p=P),
                             allow_slow_non_contiguous=True).then_inc(s_colb, 16)
            W_OUT.load(sp, (1,))
            W_OUT.stream(sp)
            conv1.dense.load(sp)

        def act_wout(act):
            act.wait_ge(s_colb, 48)
            for u in range(2):
                W_OUT.take(act, 0, u, colb)
            with act.Fori(0, NT // 2 - 1) as i:
                for u in range(2):
                    W_OUT.take(act, i + 1, u, colb)
                    norm1.scalar(act, 2 * i + u)
            for u in range(2):
                norm1.scalar(act, NT - 2 + u)

        def dve_wout(v, step):
            v.sem_inc(W_OUT.emptied, 2)

            def pair(i, first=False):
                for u in range(2):
                    j = 2 * i + u
                    z = z4[:, u, :]
                    v.wait_ge(W_OUT.product, W_OUT.b["product"] + j + 3)
                    v.wait_ge(s_x4s[u], 16 * (i + 1))
                    if not first:
                        v.wait_ge(s_z4st[u], 16 * i)
                    step(v.scalar_tensor_tensor(halves(z), W_OUT.psum(u), 0.0, halves(x4s[:, u, :]), ALU.max, ALU.add))
                    v.sem_inc(W_OUT.emptied, 1)
                    norm1.vector(v, step, z, j)
                    v.sem_inc(s_z4, 1)

            pair(0, first=True)
            with step.loop(NT // 2 - 1, 2 * (1 + Norm.VSTEPS)) as i:
                pair(i + 1)

        conv_sems = {n: sem("conv_" + n) for n in ("b_in", "g", "cols", "agg", "emptied", "ready", "w_split", "x_low", "g_high", "cols_low")}
        conv_sems.update(x_in=two("conv_x_in"), stored=two("conv_stored"))

        class Convolution:
            def __init__(self, turn, rows, weight, bias, x_dram, out_dram):
                self.bias, self.out_dram, self.n = bias, out_dram, turn
                whi, wlo, glo = (wsplit[:, 0:KC * D], wsplit[:, KC * D:2 * KC * D], wsplit[:, 2 * KC * D:2 * KC * D + NT * D])
                xhi, xlo = (xsplit[:, k * 2 * D:(k + 1) * 2 * D].rearrange("p (u n) -> p u n", u=2) for k in range(2))
                xp, wp = Carve(xplain[:, :], NT * NP // 2 - 4 * D), Carve(wplain[:, :], KC * D)
                self.dense = Dense("conv", [rows], [weight], work[:, 3 * KC * D:4 * KC * D].rearrange("p (c n) -> p c n", c=KC),
                                   xp(2 * D).rearrange("p (u r n) -> p u r n", u=2, r=1),
                                   xp(2 * D).rearrange("p (u c n) -> p u c n", u=2, c=KC),
                                   split=(whi, wlo, xhi, xlo, (conv_sems["w_split"], conv_sems["x_low"]), turn))
                self.col, self.col_lo = ([wsplit[:, (2 * k + u) * NP:(2 * k + u + 1) * NP].rearrange("p (s n) -> p s n", s=NT)
                                          for u in range(2)] for k in range(2))
                self.g, self.g_lo = hsplit[:, 0:NT * D], glo
                self.brow = wp(D)
                self.xs = wp(2 * D).rearrange("p (u n) -> p u n", u=2)
                self.z = wp(2 * D).rearrange("p (u n) -> p u n", u=2)
                self.s_ghi, self.s_collo = conv_sems["g_high"], conv_sems["cols_low"]
                self.x_dram = x_dram
                self.x_in, self.stored = conv_sems["x_in"], conv_sems["stored"]
                self.s_b_in, self.s_g, self.s_cols, self.s_ready = (conv_sems[n] for n in ("b_in", "g", "cols", "ready"))
                self.s_agg, self.s_emptied = conv_sems["agg"], conv_sems["emptied"]
                self.at = turn * NT
                self.at2 = turn * (NT + 2)
                self.norm = Norm()

            def sp(self, sp):
                self.dense.stream(sp)
                sp.dma_start(self.brow, self.bias.partition_broadcast(P)).then_inc(self.s_b_in, 16)
                with sp.Fori(0, NT // 2) as i:
                    for u in range(2):
                        j = 2 * i + u
                        sp.wait_ge(self.s_emptied, self.at2 + j + 1)
                        sp.dma_start(self.xs[:, u, :], self.x_dram[bass.ds(j * P, P), :]).then_inc(self.x_in[u], 16)

            def act(self, act, step):
                d = self.dense

                def empty(j, u, i):
                    act.wait_ge(d.product, d.b["product"] + j + 3)
                    act.activation(halves(self.g[:, bass.ds(j * D, D)]), d.psum(u), ACT.Copy, scale=dinv[:, bass.ds(j, 1)])\
                       .then_inc(self.s_ghi, 1)

                d.take_and_empty(act, step.loop, 0, empty)

                def column(j, u):
                    act.wait_ge(self.s_agg, self.at2 + j + 1)
                    act.activation(self.col[u], cnt3[:, :, bass.ds(j * P, P)], ACT.Copy).then_inc(self.s_cols, 1)

                for u in range(2):
                    column(u, u)
                with act.Fori(0, NT // 2 - 1) as i:
                    for u in range(2):
                        column(2 * (i + 1) + u, u)
                        self.norm.scalar(act, 2 * i + u)
                for u in range(2):
                    self.norm.scalar(act, NT - 2 + u)

            def pe(self, pe):
                self.dense.multiply(pe)
                pe.sem_inc(self.s_agg, 2)
                pe.wait_ge(self.s_g, self.n + 1)
                with pe.Fori(0, NT // 2) as i:
                    for u in range(2):
                        j = 2 * i + u
                        pe.wait_ge(self.s_collo, self.at + j + 1)
                        pe.wait_ge(self.s_emptied, self.at2 + j + 1)
                        for h in range(2):
                            for q, (x, g) in enumerate(((self.col, self.g), (self.col, self.g_lo), (self.col_lo, self.g))):
                                for s in range(NT):
                                    last = pe.matmul(ps[:, 2 * u + h, 0:HALF], x[u][:, s, :],
                                                     g[:, s * D + h * HALF:s * D + (h + 1) * HALF],
                                                     start=(q == 0 and s == 0), stop=(q == 2 and s == NT - 1))
                        last.then_inc(self.s_agg, 1)

            def dve(self, v, step):
                v.sem_inc(self.dense.emptied, 2)
                v.sem_inc(self.s_emptied, 2)
                d = self.dense
                d.split_weights(v, step)

                def low_g(j, u):
                    v.wait_ge(self.s_ghi, self.at + j + 1)
                    step(v.scalar_tensor_tensor(halves(self.g_lo[:, bass.ds(j * D, D)]), d.psum(u), dinv[:, bass.ds(j, 1)],
                                                halves(self.g[:, bass.ds(j * D, D)].bitcast(F32)), ALU.mult, ALU.subtract))
                    v.sem_inc(d.emptied, 1)

                for u in range(2):
                    d.low_rows(v, 0, u)
                with step.loop(NT // 2 - 1, 2) as i:
                    for u in range(2):
                        low_g(2 * i + u, u)
                        d.low_rows(v, i + 1, u)
                for u in range(2):
                    low_g(NT - 2 + u, u)
                v.sem_inc(self.s_g, 1)

                def low_column(j, u):
                    v.wait_ge(self.s_cols, self.at + j + 1)
                    v.tensor_tensor(self.col_lo[u], cnt3[:, :, bass.ds(j * P, P)], self.col[u].bitcast(F32), ALU.subtract)\
                     .then_inc(self.s_collo, 1)

                for u in range(2):
                    low_column(u, u)
                v.wait_ge(self.s_b_in, 16 * (self.n + 1))

                def pair(i, first=False, last=False):
                    for u in range(2):
                        j = 2 * i + u
                        z = self.z[:, u, :]
                        v.wait_ge(self.s_agg, self.at2 + j + 3)
                        if not first:
                            v.wait_ge(self.stored[u], 8 * self.at + 16 * i)
                        step(v.scalar_tensor_tensor(halves(z), ps[:, 2 * u:2 * u + 2, 0:HALF], dinv[:, bass.ds(j, 1)],
                                                    halves(self.brow), ALU.mult, ALU.add))
                        v.wait_ge(self.x_in[u], 8 * self.at + 16 * (i + 1))
                        step(v.tensor_tensor(z, z, self.xs[:, u, :], ALU.add))
                        v.sem_inc(self.s_emptied, 1)
                        if not last:
                            low_column(j + 2, u)
                        self.norm.vector(v, step, z, j)
                        v.sem_inc(self.s_ready, 1)

                pair(0, first=True)
                with step.loop(NT // 2 - 2, 2 * (2 + Norm.VSTEPS)) as i:
                    pair(i + 1)
                pair(NT // 2 - 1, last=True)

            def pool(self, g, step):
                store_tiles(g, step, self.s_ready, self.z, self.out_dram, self.stored, self.at)

        conv1 = Convolution(0, x1_d, a["L1_gnn_W"], a["L1_gnn_b"], x1_d, x2_d)

        c5 = Carve(work, WORK)
        wbd = c5(2 * P)
        rows5 = c5(2 * D).rearrange("p (u n) -> p u n", u=2)
        xt5 = c5(2 * D).rearrange("p (u c n) -> p u c n", u=2, c=KC)
        res5 = c5(2 * D).rearrange("p (u n) -> p u n", u=2)
        avecs5 = [c5(D) for _ in range(2)]
        prod5 = c5(D)
        s_w5, s_w5z, s_ones5 = sem("wbd_in"), sem("wbd_zero"), sem("ones5")
        s_rows5, s_res5 = two("rows5_in"), two("res_stored")
        s_turn5, s_take5, s_prod5, s_free5 = sem("turned5"), sem("taken5"), sem("product5"), sem("free5")
        ft = hbuf[:, 0:NT * (D + 12)].rearrange("p (j n) -> p j n", j=NT)

        def pool_heads(g, step):
            step(g.memset(wbd, 0.0))
            g.sem_inc(s_w5z, 1)
            step(g.memset(hbuf[:, 0:NT * (D + 12)], 1.0))
            g.sem_inc(s_ones5, 1)

        def sp_heads(sp):
            for vec, name in zip(avecs5, ("L2_gnn_attn_l", "L2_gnn_attn_r")):
                sp.dma_start(vec, a[name].rearrange("o h c -> (o h c)").partition_broadcast(P)).then_inc(s_vecs, 16)
            sp.wait_ge(s_w5z, 1)
            for q in range(2):
                for k, w in ((0, a["L2_gnn_W"]), (1, a["L2_gnn_W_res"])):
                    sp.dma_start(wbd[64 * q:64 * q + 64, k * P + 64 * q:k * P + 64 * q + 64], w).then_inc(s_w5, 16)
            with sp.Fori(0, NT // 2) as i:
                for u in range(2):
                    j = 2 * i + u
                    sp.wait_ge(s_turn5, j + 1)
                    sp.dma_start(rows5[:, u, :], x2_d[bass.ds(j * P, P), :]).then_inc(s_rows5[u], 16)

        def dve_heads(v, step):
            v.wait_ge(s_vecs, 128)
            with step.loop(NT // 2, 8) as i:
                for u in range(2):
                    j = 2 * i + u
                    v.wait_ge(s_free5, 2 * j + 4)
                    project(v, step, hbuf[:, bass.ds(j * (D + 12), D + 12)].rearrange("p (h c) -> p h c", h=12)[:, :, 0:64],
                            avecs5, prod5, lr2, j, 12)

        def pe_heads(pe):
            pe.sem_inc(s_turn5, 2)
            pe.sem_inc(s_prod5, 2)
            pe.sem_inc(s_free5, 2)
            pe.wait_ge(s_w5, 64)
            with pe.Fori(0, NT // 2) as i:
                for u in range(2):
                    pe.wait_ge(s_rows5[u], 16 * (i + 1))
                    for c in range(KC):
                        last = pe.transpose(ps[:, 2 * u + c // 3, (c % 3) * P:(c % 3 + 1) * P], rows5[:, u, c * P:(c + 1) * P], ident[:, :])
                    last.then_inc(s_turn5, 1)
                for u in range(2):
                    pe.wait_ge(s_take5, 2 * i + u + 1)
                    for hf in range(2):
                        pe.wait_ge(s_free5, 2 * (2 * i + u) + hf + 1)
                        for c in range(3):
                            last = pe.matmul(ps[:, 4 + 2 * hf + c // 2, (c % 2) * 2 * P:(c % 2 + 1) * 2 * P],
                                             xt5[:, u, 3 * hf + c, :], wbd, start=True, stop=True)
                        last.then_inc(s_prod5, 1)

        def act_heads(act, step):
            act.wait_ge(s_ones5, 1)
            for u in range(2):
                act.sem_inc(s_res5[u], 16)
            with step.loop(NT // 2, 4) as i:
                for u in range(2):
                    j = 2 * i + u
                    act.wait_ge(s_turn5, j + 3)
                    act.wait_ge(s_prod5, 2 * j + 1)
                    act.activation(xt5[:, u].rearrange("p (a b) n -> p a (b n)", a=2), ps[:, 2 * u:2 * u + 2, 0:HALF], ACT.Copy)\
                       .then_inc(s_take5, 1)
                for u in range(2):
                    j = 2 * i + u
                    act.wait_ge(s_res5[u], 16 * (i + 1))
                    for hf in range(2):
                        act.wait_ge(s_prod5, 2 * j + hf + 3)
                        for b, n in ((0, 2), (1, 1)):
                            blocks = ps[:, 4 + 2 * hf + b, 0:n * 2 * P].rearrange("p (c k m) -> p c k m", k=2, m=P)
                            head = 6 * hf + 4 * b
                            act.activation(hbuf[:, bass.ds(j * (D + 12) + head * 65, 65 * 2 * n)].rearrange("p (c h m) -> p c h m", h=2, m=65)[:, :, :, 0:64],
                                           blocks[:, :, 0, :].rearrange("p c (h m) -> p c h m", h=2), ACT.Copy)
                            ins = act.activation(res5[:, u, head * 64:head * 64 + n * P].rearrange("p (c m) -> p c m", m=P),
                                                 blocks[:, :, 1, :], ACT.Copy)
                        step(ins)
                        act.sem_inc(s_free5, 1)
                    act.dma_start(res_d[bass.ds(j * P, P), :], res5[:, u, :]).then_inc(s_res5[u], 16)
            for u in range(2):
                act.wait_ge(s_res5[u], 16 * (NT // 2 + 1))

        att2 = Attention("attb", 12, mask2v, [(lr2, agg2_d, None)])

        def self_loops(v, step, op):
            for j in range(NT):
                blk = cnt3[:, j, j * P:(j + 1) * P]
                step.count(v.tensor_tensor(blk, blk, ident[:, :], op))
            step.wait()

        c6 = Carve(work, WORK)
        in6 = [c6(2 * D).rearrange("p (u n) -> p u n", u=2) for _ in range(3)]
        s_in6, s_st6 = two("x3_parts_in"), two("x3_stored")
        s_ready6 = sem("x3_ready")
        norm6 = Norm()

        def sp_join(sp):
            W_ROOT.load(sp)

            def parts(j, u, i):
                if not isinstance(i, int) or i:
                    sp.wait_ge(s_st6[u], 16 * i)
                for t, src in zip(in6, (agg2_d, res_d, x2_d)):
                    sp.dma_start(t[:, u, :], src[bass.ds(j * P, P), :]).then_inc(s_in6[u], 16)

            for u in range(2):
                parts(u, u, 0)
            with sp.Fori(0, NT // 2 - 1) as i:
                for u in range(2):
                    parts(2 * (i + 1) + u, u, i + 1)
                    W_ROOT.stream_tile(sp, 2 * i + u, u, P)
            for u in range(2):
                sp.wait_ge(s_st6[u], 16 * (NT // 2))
                W_ROOT.stream_tile(sp, NT - 2 + u, u, P)

        def dve_join(v, step):
            with step.loop(NT // 2, 2 * (2 + Norm.VSTEPS)) as i:
                for u in range(2):
                    z = in6[0][:, u, :]
                    v.wait_ge(s_in6[u], 48 * (i + 1))
                    step(v.tensor_tensor(z, z, in6[1][:, u, :], ALU.add))
                    step(v.scalar_tensor_tensor(z, z, 0.0, in6[2][:, u, :], ALU.max, ALU.add))
                    norm6.vector(v, step, z, 2 * i + u)
                    v.sem_inc(s_ready6, 1)

        whi7, wlo7 = wsplit[:, 0:2 * KC * D], wsplit[:, 2 * KC * D:4 * KC * D]
        GW = 4
        c7 = Carve(ct[:, :].bitcast(F32), NT * CW // 2)
        rows7 = c7(GW * D).rearrange("p (u r n) -> p u r n", u=GW, r=1)
        brow7 = c7(D, parts=1)
        idx7 = c7(2 * GW, I32).rearrange("p (u c) -> p u c", c=2)
        iv7 = c7(GW)
        invs7 = c7(RT)
        xt7 = xplain[:, 0:2 * D].rearrange("p (u c n) -> p u c n", u=2, c=KC)
        msg7 = xplain[:, 2 * D:4 * D].rearrange("p (u n) -> p u n", u=2)
        xhi7, xlo7 = (xsplit[:, k * 2 * D:(k + 1) * 2 * D].rearrange("p (u n) -> p u n", u=2) for k in range(2))
        W_ROOT = Dense("root", [x3_d], [a["L3_gnn_W_root"]], wplain[:, :].rearrange("p (c n) -> p c n", c=KC),
                       rows7, xt7, a["L3_gnn_b_rgcn"], brow7)
        conv3 = Convolution(1, h1_d, a["L3_gnn_W_gcn"], a["L3_gnn_b_gcn"], x3_d, out)
        s_wrel, s_msgst = sem("wrel_in"), two("messages_stored")
        s_gath = [sem(f"rows_gathered{u}") for u in range(GW)]
        s_turn7, s_take7, s_prod7, s_emp7, s_lo7 = (sem(n) for n in ("turned7", "taken7", "product7", "emptied7", "low_parts7"))
        s_split7 = sem("weights_split7")
        s_rootout = sem("root_out")

        def sp_rel(sp):
            sp.wait_ge(W_ROOT.product, W_ROOT.all_products)
            with sp.Fori(0, R) as r:
                sp.wait_ge(s_split7, r + 1)
                sp.dma_start(wplain[:, :].rearrange("p (c n) -> p c n", c=KC),
                             a["L3_gnn_W_rel"].rearrange("r (c p) n -> r p c n", p=P)[bass.ds(r, 1)].rearrange("r p c n -> (r p) c n"))\
                  .then_inc(s_wrel, 16)

        def dve_rel(v, step):
            v.sem_inc(s_split7, 1)
            with step.loop(R // 2, 4) as i:
                for u in range(2):
                    r = 2 * i + u
                    lo, hi = (w[:, u * KC * D:(u + 1) * KC * D] for w in (wlo7, whi7))
                    last = v.value_load(end_rel[0:1, bass.ds(r, 1)], min_val=0, max_val=RT)
                    v.wait_ge(s_wrel, 16 * (r + 1))
                    v.wait_ge(s_prod7, last + 2)
                    step(v.tensor_copy(hi, wplain[:, :]))
                    step(v.tensor_tensor(lo, wplain[:, :], hi.bitcast(F32), ALU.subtract))
                    v.sem_inc(s_split7, 1)

        def pool_rel(g, step):
            def gather(k, u, n):
                if n is not None:
                    g.wait_ge(s_turn7, k - GW + 3)
                    g.wait_ge(s_gath[u], n)
                step(g.tensor_copy(idx7[:, u, :], relrec[:, bass.ds(2 * k, 2)]))
                step.carry()
                g.indirect_dma_start(out=rows7[:, u, 0, :], out_offset=None, in_=x3_d,
                                     in_offset=bass.IndirectOffsetOnAxis(idx7[:, u, 0:1], 0)).then_inc(s_gath[u], 16)
                g.indirect_dma_start(out=iv7[:, u:u + 1], out_offset=None, in_=inv_d,
                                     in_offset=bass.IndirectOffsetOnAxis(idx7[:, u, 1:2], 0)).then_inc(s_gath[u], 16)

            def low(k, u, way, gathers):
                g.wait_ge(s_gath[way], 32 * gathers)
                step(g.tensor_copy(invs7[:, bass.ds(k, 1)], iv7[:, way:way + 1]))
                g.wait_ge(s_take7, k + 1)
                g.wait_ge(s_prod7, k + 1)
                step(g.tensor_tensor(xlo7[:, u, :], xt7[:, u].rearrange("p c n -> p (c n)"), xhi7[:, u, :].bitcast(F32), ALU.subtract))
                g.sem_inc(s_lo7, 1)

            g.sem_inc(s_lo7, 2)
            g.wait_ge(W_ROOT.turned, W_ROOT.all_turned)
            for u in range(GW):
                gather(u, u, None)
            low(0, 0, 0, 1)
            with step.loop(RT // GW, 3 * GW) as i:
                for u in range(GW):
                    k = GW * i + u
                    gather(k + GW, u, 32 * (i + 1))
                    low(k + 1, (u + 1) % 2, (u + 1) % GW, i + 1 + (u + 1) // GW)
            for k in range(RT // GW * GW, RT - 1):
                low(k + 1, (k + 1) % 2, (k + 1) % GW, (k + 1) // GW + 1)
            for u in range(GW):
                g.wait_ge(s_gath[u], 32 * (RT // GW + 1))

        def pe_rel(pe):
            W_ROOT.multiply(pe)
            pe.wait_ge(s_rootout, 1)
            pe.sem_inc(s_turn7, 2)
            pe.sem_inc(s_prod7, 2)

            def turn(u, gathers):
                pe.wait_ge(s_gath[u], 32 * gathers)
                for c in range(KC):
                    last = pe.transpose(ps[:, 2 * (u % 2) + c // 3, (c % 3) * P:(c % 3 + 1) * P], rows7[:, u, 0, c * P:(c + 1) * P], ident[:, :])
                last.then_inc(s_turn7, 1)

            def messages(k, u):
                r = pe.value_load(tile_rel[0:1, bass.ds(k, 1)], min_val=0, max_val=R - 1)
                pe.wait_ge(s_split7, r + 2)
                base = (r % 2) * (KC * D)
                pe.wait_ge(s_take7, k + 1)
                pe.wait_ge(s_lo7, k + 3)
                pe.wait_ge(s_emp7, k + 1)
                for h in range(2):
                    for q, (x, w) in enumerate(((xhi7, whi7), (xhi7, wlo7), (xlo7, whi7))):
                        for c in range(KC):
                            last = pe.matmul(ps[:, 4 + 2 * u + h, 0:HALF], x[:, u, c * P:(c + 1) * P],
                                             w[:, bass.ds(base + (c * D + h * HALF), HALF)],
                                             start=(q == 0 and c == 0), stop=(q == 2 and c == KC - 1))
                last.then_inc(s_prod7, 1)

            turn(0, 1)
            with pe.Fori(0, RT // GW) as i:
                for u in range(GW):
                    turn((u + 1) % GW, i + 1 + (u + 1) // GW)
                    messages(GW * i + u, u % 2)
            for k in range(RT // GW * GW, RT):
                if k + 1 < RT:
                    turn((k + 1) % GW, (k + 1) // GW + 1)
                messages(k, k % 2)

        def act_rel(act, step):
            def norms(i):
                for u in range(2):
                    norm6.scalar(act, 2 * i + u)

            def empty(j, u, i):
                act.wait_ge(W_ROOT.product, W_ROOT.b["product"] + j + 3)
                step(act.activation(halves(hbuf[:, bass.ds(j * D, D)]), W_ROOT.psum(u), ACT.Copy))
                act.sem_inc(W_ROOT.emptied, 1)

            norms(0)
            W_ROOT.take_and_empty(act, step.loop, 2, empty, before=norms)
            act.sem_inc(s_rootout, 1)

            def take(k, u):
                act.wait_ge(s_turn7, k + 3)
                act.wait_ge(s_lo7, k + 1)
                act.wait_ge(s_prod7, k + 1)
                step.count(act.activation(xt7[:, u].rearrange("p (a b) n -> p a (b n)", a=2), ps[:, 2 * u:2 * u + 2, 0:HALF], ACT.Copy))
                step(act.activation(halves(xhi7[:, u, :]), ps[:, 2 * u:2 * u + 2, 0:HALF], ACT.Copy))
                act.sem_inc(s_take7, 1)

            def store(k, u, i):
                act.wait_ge(s_prod7, k + 3)
                act.wait_ge(s_msgst[u], 16 * (i + 1))
                step(act.activation(halves(msg7[:, u, :]), ps[:, 4 + 2 * u:6 + 2 * u, 0:HALF], ACT.Copy,
                                    scale=invs7[:, bass.ds(k, 1)]))
                act.sem_inc(s_emp7, 1)
                act.dma_start(msg_d[bass.ds(k * P, P), :], msg7[:, u, :]).then_inc(s_msgst[u], 16)

            act.sem_inc(s_emp7, 2)
            for u in range(2):
                act.sem_inc(s_msgst[u], 16)
            take(0, 0)
            with step.loop(RT // 2 - 1, 6) as i:
                for u in range(2):
                    take(2 * i + u + 1, 1 - u)
                    store(2 * i + u, u, i)
            take(RT - 1, 1)
            store(RT - 2, 0, RT // 2 - 1)
            store(RT - 1, 1, RT // 2 - 1)
            for u in range(2):
                act.wait_ge(s_msgst[u], 16 * (RT // 2 + 1))

        c8 = Carve(work, WORK)
        mg8 = c8(2 * GT * D).rearrange("p (u n) -> p u n", u=2 * GT)
        sel8 = c8(2 * GT * P).rearrange("p (u n) -> p u n", u=2 * GT)
        idx8 = c8(2 * GT, I32)
        rows8 = c8(BT, I32)
        s_g8 = [sem(f"messages_in{u}") for u in range(2 * GT)]
        s_idx8, s_sel8, s_sum8, s_add8, s_h1 = (sem(n) for n in ("indices8", "selected8", "summed8", "added8", "h1_stored"))

        def pool_sum(g, step):
            def group(k, u, first=False):
                for w in range(GT):
                    way = GT * u + w
                    if not first:
                        g.wait_ge(s_sum8, k + 1)
                        g.wait_ge(s_g8[way], 16 * (k // 2))
                    step(g.tensor_copy(idx8[:, way:way + 1], rows8[:, bass.ds(GT * k + w, 1)]))
                    step.carry()
                    g.indirect_dma_start(out=mg8[:, way, :], out_offset=None, in_=msg_d,
                                         in_offset=bass.IndirectOffsetOnAxis(idx8[:, way:way + 1], 0)).then_inc(s_g8[way], 16)

            g.wait_ge(s_idx8, 1)
            for u in range(2):
                group(u, u, True)
            with step.loop(BG // 2 - 1, 2 * GT) as i:
                for u in range(2):
                    group(2 * (i + 1) + u, u)
            if BG % 2:
                group(BG - 1, 0)

        def pe_sum(pe):
            def group(k, u):
                pe.wait_ge(s_sel8, k + 1)
                pe.wait_ge(s_add8, k + 1)
                for w in range(GT):
                    way = GT * u + w
                    pe.wait_ge(s_g8[way], 16 * (k // 2 + 1))
                    for h in range(2):
                        last = pe.matmul(ps[:, 2 * u + h, 0:HALF], sel8[:, way, :], mg8[:, way, h * HALF:(h + 1) * HALF],
                                         start=(w == 0), stop=(w == GT - 1))
                last.then_inc(s_sum8, 1)

            pe.sem_inc(s_sum8, 2)
            group_loop(lambda n: pe.Fori(0, n), group)

        def dve_sum(v, step):
            step(v.tensor_copy(rows8, drec3[:, :, 3]))
            v.sem_inc(s_idx8, 1)
            v.sem_inc(s_add8, 2)

            def select(k, u):
                v.wait_ge(s_sum8, k + 1)
                for w in range(GT):
                    dr = drec3[:, bass.ds(GT * k + w, 1), 1:2].rearrange("p k c -> p (k c)")
                    step.count(v.tensor_scalar(sel8[:, GT * u + w, :], iota[:, 0:P], dr, None, ALU.is_equal))
                step.wait()
                v.sem_inc(s_sel8, 1)

            def add(k, u):
                b = v.value_load(group_dst[0:1, bass.ds(k, 1)], min_val=0, max_val=NT - 1)
                v.wait_ge(s_sum8, k + 3)
                t = halves(hbuf[:, bass.ds(b * D, D)])
                step(v.tensor_tensor(t, ps[:, 2 * u:2 * u + 2, 0:HALF], t, ALU.add))
                v.sem_inc(s_add8, 1)

            select(0, 0)
            with step.loop((BG - 1) // 2, 2 * (GT + 1)) as i:
                for u in range(2):
                    select(2 * i + u + 1, 1 - u)
                    add(2 * i + u, u)
            for k in range((BG - 1) // 2 * 2, BG):
                if k + 1 < BG:
                    select(k + 1, (k + 1) % 2)
                add(k, k % 2)

        def sp_h1(sp):
            sp.dma_start(h1_d.rearrange("(j p) n -> p j n", p=P), hbuf[:, 0:NT * D].rearrange("p (j n) -> p j n", j=NT)).then_inc(s_h1, 16)
            sp.wait_ge(s_h1, 16)


        block = ctx.enter_context(nc.Block())

        @block.sync
        def _(sp):
            sp_phase1(sp)
            meet(sp)
            meet(sp)
            sp.wait_ge(s_inv, 1)
            sp.dma_start(inv_d.rearrange("(j p r) c -> p j (r c)", p=P, r=R), inv).then_inc(s_invd, 16)
            sp.wait_ge(s_invd, 16)
            meet(sp)
            for l in range(3):
                att0.sp(sp, l, (lambda sp: W_OUT.load(sp, (0, 2))) if l == 2 else None)
                meet(sp)
            sp_wout(sp)
            meet(sp)
            conv1.sp(sp)
            meet(sp)
            sp_heads(sp)
            meet(sp)
            att2.sp(sp, 0)
            meet(sp)
            sp_join(sp)
            sp_rel(sp)
            meet(sp)
            conv3.dense.load(sp)
            meet(sp)
            sp_h1(sp)
            meet(sp)
            conv3.sp(sp)
            meet(sp)

        @block.tensor
        def _(pe):
            pe_phase1(pe)
            meet(pe)
            pe_phase2(pe)
            meet(pe)
            pe_phase3(pe)
            meet(pe)
            for l in range(3):
                att0.pe(pe, l)
                meet(pe)
            W_OUT.multiply(pe)
            meet(pe)
            conv1.pe(pe)
            meet(pe)
            pe_heads(pe)
            meet(pe)
            att2.pe(pe, 0)
            meet(pe)
            pe_rel(pe)
            meet(pe)
            pe_sum(pe)
            meet(pe)
            meet(pe)
            conv3.pe(pe)
            meet(pe)

        @block.scalar
        def _(act):
            step = Steps(act, act_step)
            act_phase1(act, step)
            meet(act)
            meet(act)
            act_phase3(act)
            meet(act)
            for l in range(3):
                att0.act(act, step, l)
                meet(act)
            act_wout(act)
            meet(act)
            conv1.act(act, step)
            meet(act)
            act_heads(act, step)
            meet(act)
            att2.act(act, step, 0)
            meet(act)
            act_rel(act, step)
            meet(act)
            meet(act)
            meet(act)
            conv3.act(act, step)
            meet(act)

        @block.vector
        def _(v):
            step = Steps(v, dve_step, dve_carrier)
            dve_phase1(v, step)
            meet(v)
            dve_phase2(v, step)
            meet(v)
            dve_phase3(v, step)
            meet(v)
            for l in range(3):
                att0.dve(v, step, l)
                meet(v)
            dve_wout(v, step)
            meet(v)
            conv1.dve(v, step)
            meet(v)
            self_loops(v, step, ALU.subtract)
            dve_heads(v, step)
            meet(v)
            att2.dve(v, step, 0)
            meet(v)
            self_loops(v, step, ALU.add)
            v.sem_inc(W_ROOT.emptied, 2)
            dve_join(v, step)
            dve_rel(v, step)
            meet(v)
            dve_sum(v, step)
            meet(v)
            meet(v)
            conv3.dve(v, step)
            meet(v)

        @block.gpsimd
        def _(g):
            step = Steps(g, pool_step, pool_carrier)
            pool_phase1(g, step)
            meet(g)
            pool_phase2(g, step)
            meet(g)
            meet(g)
            for l in range(3):
                att0.pool(g, step, l)
                meet(g)
            store_tiles(g, step, s_z4, z4, x1_d, s_z4st)
            meet(g)
            conv1.pool(g, step)
            meet(g)
            pool_heads(g, step)
            meet(g)
            att2.pool(g, step, 0)
            meet(g)
            store_tiles(g, step, s_ready6, in6[0], x3_d, s_st6)
            pool_rel(g, step)
            meet(g)
            pool_sum(g, step)
            meet(g)
            meet(g)
            conv3.pool(g, step)
            meet(g)


_OUTS = [((N, D), "float32")]


def kernel(**inputs):
    import numpy as _np
    import concourse.bacc as _bacc
    from concourse import mybir as _mybir
    from concourse.bass_utils import run_bass_kernel_spmd as _run

    nc = _bacc.Bacc("TRN2", target_bir_lowering=False, num_devices=1)
    arrays, args = {}, {}
    for name, value in inputs.items():
        if name == "edge_weight1":
            continue
        v = _np.ascontiguousarray(value)
        if name in ("L2_gnn_W", "L2_gnn_W_res"):
            v = _np.ascontiguousarray(v.T)
        arrays[f"in_{name}"] = v
        args[name] = nc.dram_tensor(f"in_{name}", v.shape, _mybir.dt.from_np(v.dtype), kind="ExternalInput").ap()
    o = nc.dram_tensor("out_0", (N, D), _mybir.dt.float32, kind="ExternalOutput").ap()
    build(nc, args, o)
    r = _run(nc, [arrays], core_ids=[0])
    return r.results[0]["out_0"]
```
